# Optimizing a Trainium2 kernel written in Bass

```python
import numpy as np
import jax
import jax.numpy as jnp

def _softmax(x, axis=-1):
    return jax.nn.softmax(x, axis=axis)

def _gelu(x):
    return jax.nn.gelu(x, approximate=True)

def _silu(x):
    return jax.nn.silu(x)

def _sigmoid(x):
    return jax.nn.sigmoid(x)

def _layernorm(x, axis=-1, eps=1e-05):
    m = jnp.mean(x, axis=axis, keepdims=True)
    v = jnp.var(x, axis=axis, keepdims=True)
    return (x - m) / jnp.sqrt(v + eps)

def _scatter_add(tgt, idx, src, axis=0):
    return tgt.at[idx].add(src)

def _segment_sum(src, seg, n):
    return jax.ops.segment_sum(src, seg, n)
kernel_name = 'mk_prb_d1_jaxref_r8_aaab6d'

def setup_inputs(seed: int=0):
    np.random.seed(seed)
    _w = jnp.asarray

    def _L0_attn_setup():
        import jax, jax.numpy as jnp
        import numpy as np
        B, T, D, H, NT = (2, 256, 128, 16, 7)
        HD = D // H
        TEMP = 0.5
        key = jax.random.key(seed)
        ks = jax.random.split(key, 6)
        x = jax.random.normal(ks[0], (B, T, D), jnp.float32)
        qkv_w = jax.random.normal(ks[1], (3 * D, D), jnp.float32) / np.sqrt(D)
        out_w = jax.random.normal(ks[2], (D, D), jnp.float32) / np.sqrt(D)
        hex_w = jax.random.normal(ks[3], (6, D), jnp.float32) * 0.02
        q6_w = jax.random.normal(ks[4], (6, D), jnp.float32) * 0.02
        tr = np.zeros((NT, 6, 6), dtype=np.float32)
        for i in range(6):
            tr[i] = np.eye(6)
            tr[i, i, i] = -1.0
        tr[6] = -np.eye(6)
        transforms = jnp.asarray(tr)
        transform_weights = jax.random.normal(ks[5], (H, NT), jnp.float32) * 0.01
        hamming_lambda_logit = jnp.asarray(np.log(0.1 / 0.9), jnp.float32)
        scale_logit = jnp.zeros((), jnp.float32)
        sips_alpha = jnp.ones((1,), jnp.float32)
        sips_beta = jnp.full((1,), np.sqrt(HD), jnp.float32)
        return {'x': x, 'qkv_w': qkv_w, 'out_w': out_w, 'hex_w': hex_w, 'hamming_lambda_logit': hamming_lambda_logit, 'q6_w': q6_w, 'transforms': transforms, 'transform_weights': transform_weights, 'scale_logit': scale_logit, 'sips_alpha': sips_alpha, 'sips_beta': sips_beta}
    _L0_attn_in = _L0_attn_setup()

    def _L0_ffn_setup():
        import jax, jax.numpy as jnp
        import numpy as np
        D_MODEL, D_FF, N_EXP = (128, 512, 8)
        key = jax.random.key(seed)
        ks = jax.random.split(key, 8)
        s = lambda fan_in: 1.0 / np.sqrt(fan_in)
        x = jax.random.normal(ks[0], (4, 256, D_MODEL), dtype=jnp.float32)
        Wr = jax.random.uniform(ks[1], (N_EXP, D_MODEL), jnp.float32, -s(D_MODEL), s(D_MODEL))
        br = jax.random.uniform(ks[2], (N_EXP,), jnp.float32, -s(D_MODEL), s(D_MODEL))
        W1 = jax.random.uniform(ks[3], (N_EXP, D_FF, D_MODEL), jnp.float32, -s(D_MODEL), s(D_MODEL))
        b1 = jax.random.uniform(ks[4], (N_EXP, D_FF), jnp.float32, -s(D_MODEL), s(D_MODEL))
        W2 = jax.random.uniform(ks[5], (N_EXP, D_MODEL, D_FF), jnp.float32, -s(D_FF), s(D_FF))
        b2 = jax.random.uniform(ks[6], (N_EXP, D_MODEL), jnp.float32, -s(D_FF), s(D_FF))
        return {'x': x, 'Wr': Wr, 'br': br, 'W1': W1, 'b1': b1, 'W2': W2, 'b2': b2}
    _L0_ffn_in = _L0_ffn_setup()
    _d = {'L0_attn_x': _L0_attn_in['x'], 'L0_attn_qkv_w': _L0_attn_in['qkv_w'], 'L0_attn_out_w': _L0_attn_in['out_w'], 'L0_attn_hex_w': _L0_attn_in['hex_w'], 'L0_attn_hamming_lambda_logit': _L0_attn_in['hamming_lambda_logit'], 'L0_attn_q6_w': _L0_attn_in['q6_w'], 'L0_attn_transforms': _L0_attn_in['transforms'], 'L0_attn_transform_weights': _L0_attn_in['transform_weights'], 'L0_attn_scale_logit': _L0_attn_in['scale_logit'], 'L0_attn_sips_alpha': _L0_attn_in['sips_alpha'], 'L0_attn_sips_beta': _L0_attn_in['sips_beta'], 'L0_ffn_Wr': _L0_ffn_in['Wr'], 'L0_ffn_br': _L0_ffn_in['br'], 'L0_ffn_W1': _L0_ffn_in['W1'], 'L0_ffn_b1': _L0_ffn_in['b1'], 'L0_ffn_W2': _L0_ffn_in['W2'], 'L0_ffn_b2': _L0_ffn_in['b2']}
    _x0 = _d['L0_attn_x']
    _d['L0_attn_x'] = jax.random.normal(jax.random.fold_in(jax.random.key(seed), 1), (16, 512, 128), dtype=_x0.dtype)
    del _x0
    return _d

def reference(L0_attn_x, L0_attn_qkv_w, L0_attn_out_w, L0_attn_hex_w, L0_attn_hamming_lambda_logit, L0_attn_q6_w, L0_attn_transforms, L0_attn_transform_weights, L0_attn_scale_logit, L0_attn_sips_alpha, L0_attn_sips_beta, L0_ffn_Wr, L0_ffn_br, L0_ffn_W1, L0_ffn_b1, L0_ffn_W2, L0_ffn_b2):

    def _L0_attn_ref(x, qkv_w, out_w, hex_w, hamming_lambda_logit, q6_w, transforms, transform_weights, scale_logit, sips_alpha, sips_beta):
        import jax, jax.numpy as jnp
        import numpy as np
        B, T, D, H, NT = (2, 256, 128, 16, 7)
        HD = D // H
        TEMP = 0.5
        b, t, _ = x.shape
        qkv = (x @ qkv_w.T).reshape(b, t, 3, H, HD)
        q = jnp.transpose(qkv[:, :, 0], (0, 2, 1, 3))
        k = jnp.transpose(qkv[:, :, 1], (0, 2, 1, 3))
        v = jnpp = jnp.transpose(qkv[:, :, 2], (0, 2, 1, 3))
        raw = jnp.einsum('bhid,bhjd->bhij', q, k)
        scores = sips_alpha[0] * jnp.tanh(raw / sips_beta[0])
        soft_bits = jnp.tanh(x @ hex_w.T)
        hamming = jnp.einsum('bid,bjd->bij', soft_bits, soft_bits) / 2.0
        lam = jax.nn.sigmoid(hamming_lambda_logit)
        scores = scores + lam * hamming[:, None, :, :]
        hexc = jnp.tanh(x @ q6_w.T)
        w = jax.nn.softmax(transform_weights / TEMP, axis=-1)
        Mh = jnp.einsum('ht,tde->hde', w, transforms)
        lat = jnp.einsum('bid,hde,bje->bhij', hexc, Mh, hexc) / 6.0
        lat = lat * (jax.nn.sigmoid(scale_logit) * 2.0)
        scores = scores + lat
        causal = jnp.tril(jnp.ones((t, t), bool))
        scores = jnp.where(causal[None, None], scores, -jnp.inf)
        attn = jax.nn.softmax(scores, axis=-1)
        out = jnp.einsum('bhij,bhjd->bhid', attn, v)
        out = jnp.transpose(out, (0, 2, 1, 3)).reshape(b, t, D)
        return out @ out_w.T

    def _L0_ffn_ref(x, Wr, br, W1, b1, W2, b2):
        import jax, jax.numpy as jnp
        import numpy as np
        D_MODEL, D_FF, N_EXP = (128, 512, 8)
        B, S, D = x.shape
        xf = x.reshape(-1, D)
        logits = xf @ Wr.T + br
        expert_idx = jnp.argmax(logits, axis=-1)
        h = jax.nn.relu(jnp.einsum('td,efd->etf', xf, W1) + b1[:, None, :])
        y = jnp.einsum('etf,edf->etd', h, W2) + b2[:, None, :]
        out = y[expert_idx, jnp.arange(xf.shape[0])]
        return out.reshape(B, S, D)
    x = L0_attn_x
    xn = _layernorm(x, axis=-1)
    x = x + _L0_attn_ref(xn, L0_attn_qkv_w, L0_attn_out_w, L0_attn_hex_w, L0_attn_hamming_lambda_logit, L0_attn_q6_w, L0_attn_transforms, L0_attn_transform_weights, L0_attn_scale_logit, L0_attn_sips_alpha, L0_attn_sips_beta) + _L0_ffn_ref(xn, L0_ffn_Wr, L0_ffn_br, L0_ffn_W1, L0_ffn_b1, L0_ffn_W2, L0_ffn_b2)
    return x

_drawn_inputs = setup_inputs


def setup_inputs(seed=0):
    import zlib

    import numpy as np

    out = dict(_drawn_inputs(seed))
    spreads = {}
    factors = {'L0_attn_hex_w': 43.552,
     'L0_attn_q6_w': 8.0,
     'L0_attn_transforms': 8.0,
     'L0_attn_transform_weights': 27.787,
     'L0_ffn_b1': 2.851}
    for name, (base, spread) in spreads.items():
        noise = np.random.default_rng([zlib.crc32(name.encode()), seed]).standard_normal(out[name].shape)
        drawn = base * np.exp(spread * noise) if base else spread * noise
        out[name] = jnp.asarray(drawn.astype(out[name].dtype))
    for name, factor in factors.items():
        out[name] = (out[name] * factor).astype(out[name].dtype)
    return out
```

```python
from contextlib import ExitStack

import concourse.bass as bass
from concourse import mybir

F32 = mybir.dt.float32
BF16 = mybir.dt.bfloat16
I32 = mybir.dt.int32
U32 = mybir.dt.uint32
ALU = mybir.AluOpType
ACT = mybir.ActivationFunctionType
AX = mybir.AxisListType.X

P = 128
B, T, D = 16, 512, 128
H, HD = 16, 8
NT, NE6 = 7, 6
E, F = 8, 512
TT = T // P
NTOK = B * TT
FC = F // P
NSLOT = 72
FG = 3
HP = 32
QH = 4
NQ = H // QH
CH = 2 * T
NC = 5
NTERM = 6
QPART = (0, 0, 0, 1, 1, 2)
RK_ROWS = NTERM * HD
LK_ROWS = 2 * NTERM * NE6
NSHIFT = 3
SHIFT0 = RK_ROWS + LK_ROWS
ROWS = SHIFT0 + NSHIFT
HEX0 = 32
HAM0 = H * NE6
NA = HAM0 + 3 * NE6
SAFE_RANGE = 40.0


def chunk_parts():
    parts = []
    for j in range(QH):
        parts.append((j, 0, j, 0, 0))
        parts.append((j, T, j, 3, 3 * P))
        parts.append((j, T + P, j, 1, P))
        parts.append((QH, j * 2 * P, j, 2, 2 * P))
    return parts


PARTS = chunk_parts()


def build(nc, a, out):
    x_d = a["L0_attn_x"]
    with ExitStack() as ctx:
        def sb(name, shape, dt=F32):
            return ctx.enter_context(nc.sbuf_tensor(name, shape, dt))

        def sem(name):
            return ctx.enter_context(nc.semaphore(name))

        w1_d = nc.dram_tensor("w1_transposed_b1", [E, P, F + FC], F32, kind="Internal").ap()
        w2_d = nc.dram_tensor("w2_transposed_b2", [E, P, F + D], F32, kind="Internal").ap()
        mx_d = nc.dram_tensor("shift_parts", [2, NSHIFT, H * T], BF16, kind="Internal").ap()
        xt_d = nc.dram_tensor("xn_transposed", [B, P, T], F32, kind="Internal").ap()
        xs_d = nc.dram_tensor("x_sorted", [NSLOT * P, D], F32, kind="Internal").ap()
        ys_d = nc.dram_tensor("y_sorted", [NSLOT * P, D], F32, kind="Internal").ap()
        m_d = nc.dram_tensor("mix", [H, NE6 * NE6], F32, kind="Internal").ap()
        qp_d = nc.dram_tensor("q_parts", [2, 3, P, T], BF16, kind="Internal").ap()
        kp_d = nc.dram_tensor("k_parts", [2, 3, P, T], BF16, kind="Internal").ap()
        ap_d = nc.dram_tensor("a_parts", [2, 3, P, T], BF16, kind="Internal").ap()
        hp_d = nc.dram_tensor("h_parts", [2, 2, 3, NE6, T], BF16, kind="Internal").ap()

        ident = sb("ident", [P, P])
        z = sb("z", [P, NTOK, D])
        wqkvT = sb("wqkvT", [P, 3 * D])
        woT = sb("woT", [P, D])
        hexT = sb("hexT", [P, 64])
        mixS = sb("mixS", [64, P])
        par = sb("par", [P, 8])
        posu = sb("posu", [P, NTOK], U32)
        etile = sb("etile", [P, NSLOT], I32)
        flag = sb("flag", [1, 1], I32)
        mean = sb("mean", [P, NTOK])
        rstd = sb("rstd", [P, NTOK])
        S = sb("S", [P, 2, NC, CH])
        QS = [sb(f"QS{i}", [ROWS, H, T], BF16) for i in range(2)]
        LK = [sb(f"LK{i}", [ROWS, T], BF16) for i in range(2)]
        V1 = [sb(f"V1_{i}", [P, TT, H, HP]) for i in range(2)]

        ps = [ctx.enter_context(nc.psum_tensor(f"bank{i}", [P, T], F32)) for i in range(1)]
        raw = [ctx.enter_context(nc.psum_tensor(f"raw{i}", [P, CH], F32)) for i in range(2)]
        lin = [ctx.enter_context(nc.psum_tensor(f"lin{i}", [P, T], F32)) for i in range(2)]
        pv = ctx.enter_context(nc.psum_tensor("pv", [P, T], F32))
        misc = ps[0]

        setup(nc, a, out, locals())
        layer(nc, a, out, locals())


class Link:

    def __init__(self, eng, sem, base=0):
        self.eng, self.sem, self.n = eng, sem, base

    def __call__(self, ins):
        self.n = self.n + 1
        ins.then_inc(self.sem, 1)
        self.eng.wait_ge(self.sem, self.n)


def setup(nc, a, out, g):
    ident, z, wqkvT, woT, hexT, mixS, par = (g[k] for k in ("ident", "z", "wqkvT", "woT", "hexT", "mixS", "par"))
    posu, etile, flag, mean, rstd, S, V1 = (g[k] for k in ("posu", "etile", "flag", "mean", "rstd", "S", "V1"))
    QS, LK, raw, lin, pv, misc = (g[k] for k in ("QS", "LK", "raw", "lin", "pv", "misc"))
    w1_d, w2_d, xt_d, xs_d, m_d, x_d = (g[k] for k in ("w1_d", "w2_d", "xt_d", "xs_d", "m_d", "x_d"))
    SX = 9 * P * 2
    NCLEAR = NSLOT * D // SX
    with ExitStack() as ctx:
        def sb(name, shape, dt=F32):
            return ctx.enter_context(nc.sbuf_tensor(name, shape, dt))

        def sem(name):
            return ctx.enter_context(nc.semaphore(name))

        small_in, x_in, w_in, b1_in = sem("small_in"), [sem(f"x_in{i}") for i in range(4)], sem("w_in"), sem("b1_in")
        const_ok, cleared, zeros_ok = sem("const_ok"), sem("cleared"), sem("zeros_ok")
        pe_small, small_out, act_chain, dve_chain, pool_chain = sem("pe_small"), sem("small_out"), sem("act_chain"), sem("dve_chain"), sem("pool_chain")
        b1_ok, b1_out, b2_out = sem("b1_ok"), sem("b1_out"), sem("b2_out")
        var_ok, root_ok, xn_ok, xnT_full, xnT_ok, lg_full, lg_out, xt_out = (sem(n) for n in (
            "var_ok", "root_ok", "xn_ok", "xnT_full", "xnT_ok", "lg_full", "lg_out", "xt_out"))
        oh_ok, rank_full, stats_ok = sem("oh_ok"), sem("rank_full"), sem("stats_ok")
        mix_exp_in, mix_exp, sig_in, sig_exp, mix_sb, mix_out, mix_in, ones_in = (sem(n) for n in (
            "mix_exp_in", "mix_exp", "sig_in", "sig_exp", "mix_sb", "mix_out", "mix_in", "ones_in"))

        wqkv = sb("wqkv", [P, 3, D])
        wo = sb("wo", [P, D])
        hx = sb("hx", [64, D])
        wr = sb("wr", [E, D])
        wrT = sb("wrT", [P, E])
        brr = sb("brr", [P, E])
        b1 = sb("b1", [E * FC, P])
        b1T = sb("b1T", [P, E * FC])
        b2r = sb("b2r", [P, E, D])
        tw = sb("tw", [H, NT])
        twT = sb("twT", [NT, H])
        tr = sb("tr", [NT, NE6 * NE6])
        st16 = sb("st16", [H, 8])
        mix = sb("mix_sb_t", [H, NE6 * NE6])
        plog = sb("plog", [P, 8])
        stats = sb("stats", [P, NTOK, 6])
        tA, tB, tC, tD = (sb(n, [P, NTOK]) for n in ("tA", "tB", "tC", "tD"))
        xn = [sb(f"xn{i}", [P, TT, D]) for i in range(2)]
        xT = [sb(f"xT{i}", [P, T]) for i in range(2)]
        lg = sb("lg", [P, NTOK, E])
        eq = sb("eq", [P, NTOK, E])
        ohf = sb("ohf", [P, NTOK, E])
        ohb = sb("ohb", [P, NTOK, E], BF16)
        scan = [sb(f"scan{i}", [P, NTOK, E]) for i in range(2)]
        cmp = sb("cmp", [P, NSLOT, E])
        sm = sb("sm", [P, 8, E])
        desc = sb("desc", [P, E])
        j128 = sb("j128", [P, NTOK])
        slotid = sb("slotid", [P, NSLOT])
        tri = sb("tri", [P, P], BF16)
        onesb = sb("onesb", [P, P], BF16)
        onesrow = sb("onesrow", [NSHIFT, T], BF16)
        zeros = S[:, 0].rearrange("p c n -> p (c n)")[:, 0:SX]
        NSMALL = 12

        block = ctx.enter_context(nc.Block())

        @block.sync
        def _(sp):
            sp.sem_inc(xt_out, 1)
            sp.dma_start(wqkv[:], a["L0_attn_qkv_w"].rearrange("(c p) d -> p c d", p=P)).then_inc(w_in, 16)
            sp.dma_start(wo[:], a["L0_attn_out_w"]).then_inc(w_in, 16)
            sp.wait_ge(zeros_ok, 1)
            sp.dma_start(hx[0:NE6], a["L0_attn_hex_w"]).then_inc(w_in, 16)
            sp.dma_start(hx[HEX0:HEX0 + NE6], a["L0_attn_q6_w"]).then_inc(w_in, 16)
            sp.dma_start(wr[:], a["L0_ffn_Wr"]).then_inc(w_in, 16)
            sp.dma_start(b1[:], a["L0_ffn_b1"].rearrange("e (c p) -> (e c) p", p=P)).then_inc(w_in, 16)
            for i in range(4):
                q = NTOK // 4
                sp.dma_start(z[:, i * q:(i + 1) * q, :],
                             x_d[4 * i:4 * i + 4].rearrange("b (t p) d -> p (b t) d", p=P)).then_inc(x_in[i], 16)
            sp.wait_ge(b1_ok, 1)
            sp.dma_start(w1_d[:, :, F:F + FC].rearrange("e p c -> p e c"), b1T[:].rearrange("p (e c) -> p e c", c=FC)).then_inc(b1_out, 16)
            with sp.Fori(0, B // 2) as bp:
                for i in range(2):
                    sp.wait_ge(xnT_ok, bp * 2 + i + 2)
                    sp.dma_start(xt_d[bass.ds(bp * 2 + i, 1)].rearrange("b p n -> p (b n)"), xT[i][:]).then_inc(xt_out, 16)
            sp.wait_ge(mix_in, 16)
            sp.wait_ge(xt_out, 16 * B + 1)
            sp.wait_ge(b1_out, 16)
            sp.wait_ge(b2_out, 16)

        @block.scalar
        def _(act):
            act.sem_inc(xnT_ok, 1)
            for k, (dst, src) in enumerate((
                (par[:, 0:1], a["L0_attn_sips_alpha"].rearrange("(a n) -> a n", a=1).to_broadcast([P, 1])),
                (plog[:, 0:1], a["L0_attn_sips_beta"].rearrange("(a n) -> a n", a=1).to_broadcast([P, 1])),
                (plog[:, 1:2], bass.AP(a["L0_attn_hamming_lambda_logit"].tensor, 0, [[0, P], [1, 1]])),
                (plog[:, 2:3], bass.AP(a["L0_attn_scale_logit"].tensor, 0, [[0, P], [1, 1]])),
                (brr[:], a["L0_ffn_br"].rearrange("(a n) -> a n", a=1).to_broadcast([P, E])),
                (b2r[:], bass.AP(a["L0_ffn_b2"].tensor, 0, [[0, P], [D, E], [1, D]])),
                (tw[:], a["L0_attn_transform_weights"]),
                (tr[:], a["L0_attn_transforms"].rearrange("t d e -> t (d e)")),
            )):
                act.dma_start(dst, src).then_inc(small_in, 16)
            act.wait_ge(zeros_ok, 1)
            for i in range(NCLEAR):
                act.dma_start(xs_d.rearrange("(p r) d -> p (r d)", p=P)[:, i * SX:(i + 1) * SX], zeros).then_inc(cleared, 16)
            for i in range(2):
                act.dma_start(LK[i][SHIFT0:ROWS, :], onesrow[:]).then_inc(ones_in, 16)
            act.wait_ge(mix_exp_in, 1)
            nc.scalar.activation(st16[:, 0:NT], tw[:], ACT.Exp, bias=st16[:, 7:8], scale=2.0).then_inc(mix_exp, 1)
            nc.scalar.activation(plog[:, 4:6], plog[:, 1:3], ACT.Exp, scale=-1.0).then_inc(sig_exp, 1)
            act.wait_ge(mix_sb, 1)
            act.dma_start(g["m_d"], mix[:]).then_inc(mix_out, 16)
            act.wait_ge(mix_out, 16)
            act.dma_start(mixS[HEX0:HEX0 + NE6, 0:H * NE6].rearrange("d (e h) -> d e h", h=H),
                          g["m_d"].rearrange("h (d e) -> d e h", e=NE6), allow_slow_non_contiguous=True).then_inc(mix_in, 16)
            act.wait_ge(small_in, 16 * 8)
            act.dma_start(w2_d[:, :, F:F + D].rearrange("e p d -> p e d"), b2r[:]).then_inc(b2_out, 16)
            act.wait_ge(var_ok, 1)
            nc.scalar.activation(rstd[:], tB[:], ACT.Sqrt).then_inc(root_ok, 1)
            with act.Fori(0, B // 2) as bp:
                for i in range(2):
                    act.wait_ge(xnT_full, bp * 2 + i + 2)
                    act.wait_ge(xt_out, bp * 32 + 1)
                    act.wait_ge(lg_full, bp * 2 + 1)
                    nc.scalar.copy(xT[i][:], lin[i][:]).then_inc(xnT_ok, 1)
            act.wait_ge(ones_in, 32)
            act.wait_ge(cleared, 16 * NCLEAR)

        @block.gpsimd
        def _(pool):
            link = Link(pool, pool_chain)
            link(nc.gpsimd.memset(hx[:], 0.0))
            link(nc.gpsimd.memset(zeros, 0.0))
            for i in range(2):
                link(nc.gpsimd.memset(LK[i][:], 0.0))
            nc.gpsimd.memset(onesrow[:], 1.0).then_inc(zeros_ok, 1)
            link(nc.gpsimd.memset(ident[:], 0.0))
            link(nc.gpsimd.affine_select(out=ident[:], in_=ident[:], compare_op=ALU.not_equal, fill=1.0, base=0,
                                         pattern=[[-1, P]], channel_multiplier=1))
            link(nc.gpsimd.memset(onesb[:], 1.0))
            link(nc.gpsimd.affine_select(out=tri[:], in_=onesb[:], compare_op=ALU.is_gt, fill=0.0, base=0,
                                         pattern=[[1, P]], channel_multiplier=-1))
            link(nc.gpsimd.iota(j128[:], pattern=[[P, NTOK]], base=0, channel_multiplier=0, allow_small_or_imprecise_dtypes=True))
            link(nc.gpsimd.iota(slotid[:], pattern=[[1, NSLOT]], base=0, channel_multiplier=0, allow_small_or_imprecise_dtypes=True))
            nc.gpsimd.iota(desc[:], pattern=[[-1, E]], base=E, channel_multiplier=0,
                           allow_small_or_imprecise_dtypes=True).then_inc(const_ok, 1)
            for i in range(2):
                link(nc.gpsimd.memset(V1[i][:], 0.0))
                link(nc.gpsimd.memset(V1[i][:, :, :, HD:HD + 1], 1.0))
                link(nc.gpsimd.memset(QS[i][96:ROWS].rearrange("p h n -> p (h n)"), 0.0))

        @block.tensor
        def _(pe):
            pe.sem_inc(xnT_full, 1)
            pe.sem_inc(lg_full, 1)
            pe.wait_ge(const_ok, 1)
            pe.wait_ge(w_in, 96)
            for c in range(3):
                m = nc.tensor.transpose(misc[:, c * D:(c + 1) * D], wqkv[:, c, :], ident[:])
            m.then_inc(pe_small, 1)
            m = nc.tensor.transpose(pv[:, 0:D], wo[:], ident[:])
            m = nc.tensor.transpose(pv[:, D:D + 64], hx[:], ident[0:64, 0:64])
            m = nc.tensor.transpose(pv[:, 192:192 + E], wr[:], ident[0:E, 0:E])
            nc.tensor.transpose(pv[:, 256:256 + E * FC], b1[:], ident[0:E * FC, 0:E * FC]).then_inc(pe_small, 1)
            pe.wait_ge(mix_exp, 2)
            pe.wait_ge(small_out, 3)
            nc.tensor.transpose(misc[0:NT, 0:H], st16[:, 0:NT], ident[0:H, 0:H]).then_inc(pe_small, 1)
            pe.wait_ge(small_out, 4)
            nc.tensor.matmul(misc[0:H, 64:64 + NE6 * NE6], twT[:], tr[:], start=True, stop=True).then_inc(pe_small, 1)
            pe.wait_ge(small_out, 5)
            nc.tensor.matmul(misc[0:1, 128:128 + H], st16[:, 0:1], ident[0:H, 0:H], start=True, stop=True).then_inc(pe_small, 1)
            with pe.Fori(0, B // 2) as bp:
                for i in range(2):
                    pe.wait_ge(xn_ok, bp * 2 + i + 1)
                    pe.wait_ge(xnT_ok, bp * 2 + 1)
                    for t in range(TT):
                        m = nc.tensor.transpose(lin[i][:, t * P:(t + 1) * P], xn[i][:, t, :], ident[:])
                    m.then_inc(xnT_full, 1)
                    pe.wait_ge(xnT_ok, bp * 2 + i + 2)
                    pe.wait_ge(lg_out, bp * 2 + i + 1)
                    for t in range(TT):
                        m = nc.tensor.matmul(pv[:, t * E:(t + 1) * E], xT[i][:, t * P:(t + 1) * P], wrT[:],
                                             start=True, stop=True)
                    m.then_inc(lg_full, 1)
            pe.wait_ge(oh_ok, 1)
            oh = ohb[:].rearrange("p t e -> p (t e)")
            nc.tensor.matmul(misc[:, 0:T], tri[:], oh, start=True, stop=True).then_inc(rank_full, 1)
            nc.tensor.matmul(lin[0][:, 0:T], onesb[:], oh, start=True, stop=True).then_inc(rank_full, 1)

        @block.vector
        def _(dve):
            link = Link(dve, dve_chain)
            v = nc.vector
            dve.sem_inc(lg_out, 1)
            link(v.memset(mixS[:], 0.0))
            dve.wait_ge(pe_small, 1)
            v.tensor_copy(wqkvT[:, 0:2 * D].rearrange("p (c d h) -> p c d h", c=2, h=H)[:, 0],
                          misc[:, 0:D].rearrange("p (h d) -> p d h", h=H))
            v.tensor_copy(wqkvT[:, 0:2 * D].rearrange("p (c d h) -> p c d h", c=2, h=H)[:, 1],
                          misc[:, D:2 * D].rearrange("p (h d) -> p d h", h=H))
            v.tensor_copy(wqkvT[:, 2 * D:3 * D], misc[:, 2 * D:3 * D]).then_inc(small_out, 1)
            dve.wait_ge(pe_small, 2)
            dve.wait_ge(w_in, 96)
            v.tensor_copy(woT[:], pv[:, 0:D]).then_inc(small_out, 1)
            v.tensor_copy(hexT[:], pv[:, D:D + 64])
            v.tensor_copy(wrT[:], pv[:, 192:192 + E]).then_inc(small_out, 1)
            v.tensor_copy(b1T[:], pv[:, 256:256 + E * FC]).then_inc(b1_ok, 1)
            dve.wait_ge(small_in, 16 * 8)
            link(v.reduce_max(st16[:, 7:8], tw[:], AX))
            v.tensor_scalar(st16[:, 7:8], st16[:, 7:8], -2.0, None, ALU.mult).then_inc(mix_exp_in, 1)
            dve.wait_ge(mix_exp, 1)
            link(v.reduce_sum(st16[:, 7:8], st16[:, 0:NT], AX))
            link(v.reciprocal(st16[:, 7:8], st16[:, 7:8]))
            v.tensor_scalar(st16[:, 0:NT], st16[:, 0:NT], st16[:, 7:8], None, ALU.mult).then_inc(mix_exp, 1)
            dve.wait_ge(sig_exp, 1)
            link(v.tensor_scalar(plog[:, 4:6], plog[:, 4:6], 1.0, None, ALU.add))
            link(v.reciprocal(par[:, 2:4], plog[:, 4:6]))
            link(v.reciprocal(par[:, 1:2], plog[:, 0:1]))
            link(v.tensor_scalar(par[:, 4:5], par[:, 2:3], 0.5, None, ALU.mult))
            link(v.tensor_scalar(par[:, 5:6], par[:, 3:4], 2.0 / 6.0, None, ALU.mult))
            link(v.tensor_scalar(mixS[0:NE6, HAM0:HAM0 + NE6], ident[0:NE6, 0:NE6], par[0:NE6, 4:5], None, ALU.mult))
            link(v.tensor_copy(mixS[HEX0:HEX0 + NE6, HAM0 + NE6:HAM0 + 2 * NE6], ident[HEX0:HEX0 + NE6, HEX0:HEX0 + NE6]))
            link(v.tensor_copy(mixS[0:NE6, HAM0 + 2 * NE6:NA], ident[0:NE6, 0:NE6]))
            dve.wait_ge(pe_small, 3)
            v.tensor_copy(twT[:], misc[0:NT, 0:H]).then_inc(small_out, 1)
            dve.wait_ge(pe_small, 4)
            v.tensor_scalar(mix[:], misc[0:H, 64:64 + NE6 * NE6], par[0:H, 5:6], None, ALU.mult).then_inc(mix_sb, 1)
            dve.wait_ge(mix_sb, 1)
            v.tensor_reduce(st16[:, 0:1], mix[:], AX, ALU.add, apply_absolute_value=True).then_inc(small_out, 1)
            dve.wait_ge(pe_small, 5)
            link(v.reduce_max(plog[0:1, 6:7], misc[0:1, 128:128 + H], AX))
            link(v.scalar_tensor_tensor(out=plog[0:1, 6:7], in0=par[0:1, 2:3], scalar=3.0, in1=plog[0:1, 6:7],
                                        op0=ALU.mult, op1=ALU.add))
            link(v.tensor_scalar(plog[0:1, 7:8], par[0:1, 0:1], -1.0, None, ALU.mult))
            link(v.tensor_tensor(plog[0:1, 7:8], plog[0:1, 7:8], par[0:1, 0:1], ALU.max))
            link(v.tensor_tensor(plog[0:1, 6:7], plog[0:1, 6:7], plog[0:1, 7:8], ALU.add))
            link(v.tensor_scalar(flag[:], plog[0:1, 6:7], SAFE_RANGE, None, ALU.is_le))

            for i in range(4):
                dve.wait_ge(x_in[i], 16)
                with dve.Fori(0, 4) as b:
                    for t in range(TT):
                        tile = (b + 4 * i) * TT + t
                        m = v.bn_stats(stats[:, bass.ds(tile, 1), :], z[:, bass.ds(tile, 1), :])
                    m.then_inc(stats_ok, 1)
            dve.wait_ge(stats_ok, B)
            me, mo, qe, qo = (stats[:, :, k] for k in (1, 4, 2, 5))
            link(v.tensor_tensor(tA[:], me, mo, ALU.add))
            link(v.tensor_scalar(mean[:], tA[:], 0.5, None, ALU.mult))
            link(v.tensor_tensor(tA[:], me, mo, ALU.subtract))
            link(v.tensor_tensor(tA[:], tA[:], tA[:], ALU.mult))
            link(v.tensor_scalar(tA[:], tA[:], 0.25, None, ALU.mult))
            link(v.tensor_tensor(tB[:], qe, qo, ALU.add))
            link(v.scalar_tensor_tensor(out=tB[:], in0=tB[:], scalar=1.0 / D, in1=tA[:], op0=ALU.mult, op1=ALU.add))
            v.tensor_scalar(tB[:], tB[:], 1e-5, None, ALU.add).then_inc(var_ok, 1)
            dve.wait_ge(root_ok, 1)
            link(v.reciprocal(tC[:], rstd[:]))
            link(v.tensor_tensor(tD[:], tC[:], tC[:], ALU.mult))
            link(v.tensor_tensor(tD[:], tD[:], tB[:], ALU.mult))
            link(v.tensor_scalar(tD[:], tD[:], -0.5, 1.5, ALU.mult, ALU.add))
            link(v.tensor_tensor(rstd[:], tC[:], tD[:], ALU.mult))

            def logits_out(b, i):
                dve.wait_ge(lg_full, b * 2 + i + 2)
                v.tensor_tensor(lg[:, bass.ds((b * 2 + i) * TT, TT), :],
                                pv[:, 0:TT * E].rearrange("p (t e) -> p t e", e=E),
                                brr[:].rearrange("p (a e) -> p a e", a=1).to_broadcast([P, TT, E]), ALU.add).then_inc(lg_out, 1)

            with dve.Fori(0, B // 2) as bp:
                for i in range(2):
                    dve.wait_ge(xnT_full, bp * 2 + 1)
                    for t in range(TT):
                        tile = (bp * 2 + i) * TT + t
                        m = v.tensor_scalar(xn[i][:, t, :], z[:, bass.ds(tile, 1), :], mean[:, bass.ds(tile, 1)],
                                            rstd[:, bass.ds(tile, 1)], ALU.subtract, ALU.mult)
                    m.then_inc(xn_ok, 1)
                for i in range(2):
                    logits_out(bp, i)

            def over_t(ap):
                return ap.rearrange("p (t a) -> p t a", a=1).to_broadcast([P, NTOK, E])

            def over_e(ap):
                return ap.rearrange("p (a e) -> p a e", a=1).to_broadcast([P, NTOK, E])

            dve.wait_ge(lg_out, B + 1)
            link(v.tensor_reduce(tA[:], lg[:], AX, ALU.max))
            link(v.tensor_tensor(eq[:], lg[:], over_t(tA[:]), ALU.is_ge))
            link(v.tensor_tensor(eq[:], eq[:], over_e(desc[:]), ALU.mult))
            link(v.tensor_reduce(tA[:], eq[:], AX, ALU.max))
            link(v.tensor_tensor(ohf[:], eq[:], over_t(tA[:]), ALU.is_equal))
            v.tensor_copy(ohb[:], ohf[:]).then_inc(oh_ok, 1)
            dve.wait_ge(rank_full, 2)
            tot = lin[0][:, 0:T].rearrange("p (t e) -> p t e", e=E)
            link(v.tensor_copy(scan[0][:], tot))
            cur, k = 0, 1
            while k < NTOK:
                link(v.tensor_copy(scan[1 - cur][:, 0:k, :], scan[cur][:, 0:k, :]))
                link(v.tensor_tensor(scan[1 - cur][:, k:, :], scan[cur][:, k:, :], scan[cur][:, 0:NTOK - k, :], ALU.add))
                cur, k = 1 - cur, 2 * k
            incl, other = scan[cur], scan[1 - cur]
            link(v.tensor_copy(sm[:, 0, :], incl[:, NTOK - 1, :]))
            link(v.tensor_tensor(eq[:], over_e(sm[:, 0, :]), over_t(j128[:]), ALU.is_gt))
            link(v.tensor_reduce(sm[:, 1, :], eq[:].rearrange("p t e -> p e t"), AX, ALU.add))
            src, k = 1, 1
            while k < E:
                link(v.tensor_copy(sm[:, src + 1, 0:k], sm[:, src, 0:k]))
                link(v.tensor_tensor(sm[:, src + 1, k:], sm[:, src, k:], sm[:, src, 0:E - k], ALU.add))
                src, k = src + 1, 2 * k
            link(v.tensor_tensor(sm[:, 5, :], sm[:, src, :], sm[:, 1, :], ALU.subtract))
            link(v.tensor_scalar(sm[:, 6, :], sm[:, 5, :], float(P), None, ALU.mult))
            link(v.tensor_tensor(incl[:], incl[:], tot, ALU.subtract))
            link(v.tensor_tensor(other[:], misc[:, 0:T].rearrange("p (t e) -> p t e", e=E), incl[:], ALU.add))
            link(v.tensor_tensor(other[:], other[:], over_e(sm[:, 6, :]), ALU.add))
            link(v.tensor_tensor(other[:], other[:], ohf[:], ALU.mult))
            link(v.tensor_reduce(tA[:], other[:], AX, ALU.add))
            link(v.tensor_copy(posu[:], tA[:]))
            link(v.tensor_tensor(cmp[:], slotid[:].rearrange("p (t a) -> p t a", a=1).to_broadcast([P, NSLOT, E]),
                                 sm[:, src, :].rearrange("p (a e) -> p a e", a=1).to_broadcast([P, NSLOT, E]), ALU.is_ge))
            link(v.tensor_reduce(slotid[:], cmp[:], AX, ALU.add))
            link(v.tensor_scalar(etile[:], slotid[:], float(E - 1), None, ALU.min))


PROLOGUE = ["q", "k", "codes", "mixed", "v"]
ATTN_JOBS = [(0, 0, "merge"), (0, 1, "proj"), (0, 2, "q"), (0, 3, "k"), (0, 4, "o0"), (1, 0, "codes"), (1, 1, "v"),
             (1, 2, "mixed"), (1, 4, "o1"), (2, 4, "o2"), (3, 4, "o3")]
W_JOBS = [(1, 3, "w0"), (2, 0, "w1"), (2, 1, "w2"), (2, 2, "w3"), (2, 3, "w4"), (3, 0, "w5"), (3, 1, "w6"), (3, 2, "w7")]
F_JOBS = [(1, 3, "fxA"), (2, 0, "h0A"), (2, 1, "h1A"), (2, 2, "h2A"), (2, 3, "fyA"), (2, 3, "fxB"),
          (3, 0, "h0B"), (3, 1, "h1B"), (3, 2, "h2B"), (3, 3, "fyB")]
KINDS = {
    "first": sorted([j for j in ATTN_JOBS if j[2] not in ("merge", "proj")] + W_JOBS, key=lambda j: j[:2]),
    "second": sorted(ATTN_JOBS + W_JOBS, key=lambda j: j[:2]),
    "ffn": sorted(ATTN_JOBS + F_JOBS, key=lambda j: j[:2]),
    "plain": ATTN_JOBS,
    "last": [j for j in ATTN_JOBS if j[2] not in PROLOGUE],
}
F_FROM, F_TO = 2, 14
assert (F_TO - F_FROM) * 2 * FG == NSLOT
N_RAW_IN, N_LIN_IN = 9, 18
NYG = 4


def turn(b, kind, job):
    names = [j[2] for j in KINDS[kind]]
    n = len(PROLOGUE) + names.index(job)
    if kind == "first":
        return n
    n += len(KINDS["first"])
    if kind == "second":
        return n
    n += len(KINDS["second"])
    if kind == "ffn":
        return (b - F_FROM) * len(KINDS["ffn"]) + n
    n += len(KINDS["ffn"]) * (F_TO - F_FROM)
    if kind == "plain":
        return n
    return n + len(KINDS["plain"])


TAIL_TURN = turn(B - 1, "last", KINDS["last"][-1][2]) + 1
KIND_BEFORE = {"second": "first", "plain": "ffn", "last": "plain"}


def each_batch(eng, body):
    body(0, 0, "first")
    body(1, 1, "second")
    with eng.Fori(0, (F_TO - F_FROM) // 2) as bp:
        body(bp * 2 + F_FROM, 0, "ffn")
        body(bp * 2 + F_FROM + 1, 1, "ffn")
    body(B - 2, 0, "plain")
    body(B - 1, 1, "last")


def following(b, pb, q):
    return (b, pb, q + 1) if q + 1 < NQ else (b + 1, 1 - pb, 0)


def layer(nc, a, out, g):
    z, wqkvT, woT, hexT, mixS, par, ident, S = (g[k] for k in ("z", "wqkvT", "woT", "hexT", "mixS", "par", "ident", "S"))
    QS, LK, V1, raw, lin, pv, misc = (g[k] for k in ("QS", "LK", "V1", "raw", "lin", "pv", "misc"))
    xt_d, qp_d, kp_d, ap_d, hp_d = (g[k] for k in ("xt_d", "qp_d", "kp_d", "ap_d", "hp_d"))
    w1_d, w2_d, xs_d, ys_d = (g[k] for k in ("w1_d", "w2_d", "xs_d", "ys_d"))
    etile, posu, mean, rstd = (g[k] for k in ("etile", "posu", "mean", "rstd"))

    with ExitStack() as ctx:
        def sb(name, shape, dt=F32):
            return ctx.enter_context(nc.sbuf_tensor(name, shape, dt))

        def sem(name):
            return ctx.enter_context(nc.semaphore(name))

        RK = [sb(f"RK{i}", [ROWS, H, T], BF16) for i in range(2)]
        xTr = [sb(f"xTr{i}", [P, T]) for i in range(2)]
        sQ, sK, rest, oT = (sb(n, [P, T]) for n in ("sQ", "sK", "rest", "oT"))
        sA, aT = sQ, oT
        ht = sb("ht", [64, T])
        parts = sb("parts", [P, 3, T], BF16)
        at = sb("at", [P, TT, D])
        rec = sb("rec", [P, TT, QH])
        w1 = [sb(f"w1_{i}", [P, F + FC]) for i in range(FG)]
        w2 = [sb(f"w2_{i}", [P, F + D]) for i in range(FG)]
        one = sb("one", [P, 1])
        xin = sb("xin", [P, FG, D])
        xsT = sb("xsT", [P, FG, P])
        hid = [sb(f"hid{i}", [P, FC, P]) for i in range(FG)]
        ysb = sb("ysb", [P, FG, D])
        yg = sb("yg", [P, NYG, D])
        xs = [x[:, i, :] for x in (xin, xsT, ysb, hid[2]) for i in range(FG)]
        NXS = len(xs)

        raw_full, t_done, lin_full, s_done, e_done, m_done = (sem(n) for n in (
            "raw_full", "t_done", "lin_full", "s_done", "e_done", "m_done"))
        pv_done, oT_ok, rec_ok = sem("pv_done"), sem("oT_ok"), sem("rec_ok")
        misc_full, misc_used = sem("misc_full"), sem("misc_used")
        waited, waited_sp, waited_pe, rk_clear = sem("waited"), sem("waited_sp"), sem("waited_pe"), sem("rk_clear")
        split_ok, split_chain = {n: sem(f"split_{n}") for n in "qka"}, sem("split_chain")
        stored, h_stored = {n: sem(f"stored_{n}") for n in "qka"}, sem("h_stored")
        xt_in = [sem(f"xt_in{i}") for i in range(2)]
        raw_in = [sem(f"raw_in{i}") for i in range(2)]
        lin_in = [sem(f"lin_in{i}") for i in range(2)]
        ew_in, ew_out = [sem(f"ew_in{i}") for i in range(2)], sem("ew_out")
        mx_d = g["mx_d"]
        xs_ok, xs_sent, xs_done = sem("xs_ok"), [sem(f"xs_sent{i}") for i in range(NXS)], sem("xs_done")
        relu_ok, hidden_ok = sem("relu_ok"), sem("hidden_ok")
        fx_in, w1_in, w2_in, y_out = sem("fx_in"), [sem(f"w1_in{i}") for i in range(FG)], sem("w2_in"), sem("y_out")
        y_all, yg_in, sum_ok, final_out = sem("y_all"), [sem(f"yg_in{i}") for i in range(NYG)], sem("sum_ok"), sem("final_out")

        def first_after(kind):
            return next(j[2] for j in KINDS[kind] if j[:2] >= (NQ - 2, 3))

        def jobs_at(kind, s, c):
            return [j[2] for j in KINDS[kind] if j[:2] == (s, c)]

        tmax = sb("tmax", [P, T])
        mx = sb("mx", [P, H * TT])
        mrest = sb("mrest", [H * TT, P])
        mparts = sb("mparts", [H * TT, NSHIFT, P], BF16)
        hidden = sb("hidden", [P, P])
        px_full, px_used, px_sum, px_max, px_split, px_out, px_in = (sem(n) for n in (
            "px_full", "px_used", "px_sum", "px_max", "px_split", "px_out", "px_in"))
        NPX = 2 * H * TT + 1
        HT = H * TT

        def general(eng):
            return eng.If(eng.value_load(g["flag"][0:1, 0:1], min_val=0, max_val=1) == 0)

        block = ctx.enter_context(nc.Block())

        @block.tensor
        def _(pe):
            mm = nc.tensor.matmul
            pe.sem_inc(raw_full, 1)
            pe.sem_inc(lin_full, 1)
            pe.sem_inc(pv_done, 1)

            def fill_raw(bf, pf, q, c):
                n = (bf * NQ + q) * NC + c
                if not (isinstance(n, int) and n < 2):
                    pe.wait_ge(t_done, n - 1)
                if q == 0 and c == 0:
                    pe.wait_ge(lin_in[pf], (bf - pf) * (8 * N_LIN_IN) + 16 * N_LIN_IN)
                    pe.wait_ge(raw_in[pf], (bf - pf) * (8 * N_RAW_IN) + 16 * N_RAW_IN)
                for cc, col, j, kt, qs in PARTS:
                    if cc == c:
                        h = q * QH + j
                        m = mm(raw[(q + c) % 2][:, col:col + T - qs], RK[pf][:, h, kt * P:(kt + 1) * P],
                               QS[pf][:, h, qs:T], start=True, stop=True)
                m.then_inc(raw_full, 1)

            def fill_lin(bf, pf, q, c):
                n = (bf * NQ + q) * NC + c
                for half in range(2):
                    if not (isinstance(n, int) and n == 0):
                        pe.wait_ge(s_done, n * 2 - 1 + half)
                    for cc, col, j, kt, qs in PARTS:
                        if cc == c and col // T == half:
                            h = q * QH + j
                            m = mm(lin[half][:, col - half * T:col - half * T + T - qs], LK[pf][:, kt * P:(kt + 1) * P],
                                   QS[pf][:, h, qs:T], start=True, stop=True)
                    m.then_inc(lin_full, 1)

            def weigh(pb, q, kts):
                for kt in kts:
                    for cc, col, j, k, qs in PARTS:
                        if k == kt:
                            m = mm(pv[j * HP:(j + 1) * HP, qs:T], V1[pb][:, kt, q * QH + j, :],
                                   S[:, q % 2, cc, col:col + T - qs], start=(kt == 0), stop=(kt == 2))
                return m

            def turn_tiles(src, n=TT):
                for t in range(n):
                    m = nc.tensor.transpose(misc[:, t * P:(t + 1) * P], src(t), ident[:])
                return m

            def job(name, n, b, pb):
                if not (isinstance(n, int) and n == 0):
                    pe.wait_ge(misc_used, n)
                bn, pn = b + 1, 1 - pb
                k = (b - F_FROM) * 2 + (1 if name[-1] == "B" else 0)
                if name == "q":
                    pe.wait_ge(xt_in[pn], (bn - pn) * 8 + 16)
                    m = mm(misc[:], wqkvT[:, 0:D], xTr[pn][:], start=True, stop=True)
                elif name == "k":
                    m = mm(misc[:], wqkvT[:, D:2 * D], xTr[pn][:], start=True, stop=True)
                elif name == "codes":
                    m = mm(misc[0:64], hexT[:], xTr[pn][:], start=True, stop=True)
                elif name == "mixed":
                    m = mm(misc[:], mixS[:], ht[:], start=True, stop=True)
                elif name == "v":
                    for t in range(TT):
                        m = mm(misc[:, t * P:(t + 1) * P], xTr[pn][:, t * P:(t + 1) * P], wqkvT[:, 2 * D:3 * D],
                               start=True, stop=True)
                elif name[0] == "o":
                    pe.wait_ge(oT_ok, b * NQ + int(name[1]) + 2)
                    m = turn_tiles(lambda t: oT[:, t * P:(t + 1) * P])
                elif name == "merge":
                    m = turn_tiles(lambda t: at[:, t, :])
                elif name == "proj":
                    for t in range(TT):
                        m = mm(misc[:, t * P:(t + 1) * P], aT[:, t * P:(t + 1) * P], woT[:], start=True, stop=True)
                elif name[0] == "w":
                    i, e = int(name[1]), b * (E // 2) + int(name[1]) // 2
                    if i % 2 == 0:
                        pe.wait_ge(ew_in[e % 2], (e // 2 + 1) * 32)
                    m = turn_tiles(lambda t: (w1, w2)[i % 2][e % 2][:, t * P:(t + 1) * P])
                elif name[:2] == "fx":
                    pe.wait_ge(fx_in, k * 16 + 16)
                    m = turn_tiles(lambda t: xin[:, t, :], FG)
                elif name[0] == "h":
                    i = int(name[1])
                    pe.wait_ge(w1_in[i], k * 16 + 16)
                    for c in range(FC):
                        m = mm(misc[:, c * P:(c + 1) * P], w1[i][:, c * P:(c + 1) * P], xsT[:, i, :], start=True, stop=True)
                elif name[:2] == "fy":
                    pe.wait_ge(w2_in, k * 48 + 48)
                    pe.wait_ge(relu_ok, k * FG + FG)
                    for i in range(FG):
                        for c in range(FC):
                            m = mm(misc[:, i * P:(i + 1) * P], hid[i][:, c, :], w2[i][:, c * P:(c + 1) * P],
                                   start=(c == 0), stop=(c == FC - 1))
                m.then_inc(misc_full, 1)

            def maxima(bn, pn, n):
                pe.wait_ge(lin_in[pn], (bn - pn) * (8 * N_LIN_IN) + 16 * N_LIN_IN)
                pe.wait_ge(raw_in[pn], (bn - pn) * (8 * N_RAW_IN) + 16 * N_RAW_IN)
                pe.wait_ge(misc_used, n)
                pe.sem_inc(waited_pe, 1)
                with pe.Fori(0, H) as h:
                    for qt in range(TT):
                        w, t = (qt + 1) * P, bn * NPX + (h * TT + qt) * 2
                        query = QS[pn][0:SHIFT0, bass.ds(h, 1), qt * P:w].rearrange("r h n -> r (h n)")
                        pe.wait_ge(px_used, t + 1)
                        mm(misc[:, 0:w], query, RK[pn][0:SHIFT0, bass.ds(h, 1), 0:w].rearrange("r h n -> r (h n)"),
                           start=True, stop=True).then_inc(px_full, 1)
                        pe.wait_ge(px_used, t + 2)
                        mm(misc[:, 0:w], query, LK[pn][0:SHIFT0, 0:w], start=True, stop=True).then_inc(px_full, 1)
                pe.wait_ge(px_used, bn * NPX + NPX)
                pe.wait_ge(px_max, (bn + 1) * HT + 1)
                pe.sem_inc(waited_pe, 1)
                nc.tensor.transpose(misc[0:HT, 0:P], mx[:], ident[:]).then_inc(px_full, 1)
                pe.wait_ge(px_used, (bn + 1) * NPX + 1)
                pe.wait_ge(px_in, bn * 16 + 16)

            for n, name in enumerate(PROLOGUE):
                job(name, n, -1, 1)
            with general(pe):
                maxima(0, 0, len(PROLOGUE))
            fill_raw(0, 0, 0, 0)
            fill_raw(0, 0, 0, 1)
            for c in range(NC):
                fill_lin(0, 0, 0, c)
                fill_raw(0, 0, (c + 2) // NC, (c + 2) % NC)

            def body(b, pb, kind):
                for s in range(NQ):
                    bf, pf, qf = following(b, pb, s)
                    front = not (kind == "last" and s == NQ - 1)
                    for c in range(NC):
                        if front:
                            fill_lin(bf, pf, qf, c)
                            if c + 2 < NC:
                                fill_raw(bf, pf, qf, c + 2)
                            elif not (kind == "last" and s == NQ - 2):
                                if s == NQ - 2 and c == 3:
                                    with general(pe):
                                        maxima(b + 1, 1 - pb, turn(b, kind, first_after(kind)))
                                fill_raw(*following(bf, pf, qf), c + 2 - NC)
                        if c == 1:
                            pe.wait_ge(m_done, (b * NQ + s) * 2 + 1)
                            pe.wait_ge(oT_ok, b * NQ + s + 1)
                            weigh(pb, s, [0])
                        if c == 2:
                            weigh(pb, s, [1, 3])
                        if c == 3:
                            pe.wait_ge(m_done, (b * NQ + s) * 2 + 2)
                            weigh(pb, s, [2]).then_inc(pv_done, 1)
                        for name in jobs_at(kind, s, c):
                            job(name, turn(b, kind, name), b, pb)

            each_batch(pe, body)
            job("merge", TAIL_TURN, B - 1, 1)
            job("proj", TAIL_TURN + 1, B - 1, 1)

        @block.scalar
        def _(act):
            def tanh(bf, q, c):
                n = (bf * NQ + q) * NC + c
                act.wait_ge(raw_full, n + 2)
                if c == 0 and not (isinstance(n, int) and n == 0):
                    act.wait_ge(pv_done, bf * NQ + q)
                nc.scalar.activation(S[:, q % 2, c, :], raw[(q + c) % 2][:], ACT.Tanh).then_inc(t_done, 1)

            def exp(bf, q, c0, c1):
                act.wait_ge(s_done, (bf * NQ + q) * (2 * NC) + 2 * c1)
                x = S[:, q % 2, c0:c1, :]
                nc.scalar.activation(x, x, ACT.Exp).then_inc(e_done, 1)

            def codes(n):
                act.wait_ge(misc_full, n + 1)
                nc.scalar.activation(ht[:], misc[0:64], ACT.Tanh).then_inc(misc_used, 1)

            def maxima(bn):
                with act.Fori(0, H) as h:
                    for qt in range(TT):
                        w, i = (qt + 1) * P, h * TT + qt
                        act.wait_ge(px_full, bn * NPX + i * 2 + 1)
                        act.wait_ge(px_max, bn * HT + i + 1)
                        nc.scalar.activation(tmax[:, 0:w], misc[:, 0:w], ACT.Tanh).then_inc(px_used, 1)

            codes(PROLOGUE.index("codes"))
            with general(act):
                maxima(0)
            for c in range(4):
                tanh(0, 0, c)
            exp(0, 0, 0, 2)
            tanh(0, 0, 4)
            exp(0, 0, 2, 4)

            def body(b, pb, kind):
                for s in range(NQ):
                    bf, _, qf = following(b, pb, s)
                    if kind == "last" and s == NQ - 1:
                        exp(b, s, 4, 5)
                        continue
                    tanh(bf, qf, 0)
                    exp(b, s, 4, 5)
                    tanh(bf, qf, 1)
                    tanh(bf, qf, 2)
                    if s == 1 and kind != "last":
                        codes(turn(b, kind, "codes"))
                    tanh(bf, qf, 3)
                    exp(bf, qf, 0, 2)
                    tanh(bf, qf, 4)
                    if s == NQ - 2 and kind != "last":
                        with general(act):
                            maxima(b + 1)
                    exp(bf, qf, 2, 4)

            each_batch(act, body)

        @block.vector
        def _(dve):
            v = nc.vector
            dve.sem_inc(oT_ok, 1)
            for i in range(2):
                v.memset(RK[i][:].bitcast(U32), 0).then_inc(rk_clear, 1)
            v.memset(hidden[:], 0.0).then_inc(hidden_ok, 1)
            v.memset(one[:], 1.0).then_inc(rk_clear, 1)

            def add(bf, q, c, half):
                n = (bf * NQ + q) * NC + c
                if half == 0:
                    dve.wait_ge(t_done, n + 1)
                dve.wait_ge(lin_full, n * 2 + half + 2)
                x = S[:, q % 2, c, half * T:(half + 1) * T]
                v.scalar_tensor_tensor(out=x, in0=x, scalar=par[:, 0:1], in1=lin[half][:], op0=ALU.mult,
                                       op1=ALU.add).then_inc(s_done, 1)

            def take(name, n, b, pb):
                bn, pn = b + 1, 1 - pb
                first = isinstance(b, int) and b < 0
                dve.wait_ge(misc_full, n + 1)
                if name == "q":
                    if not first:
                        dve.wait_ge(split_ok["a"], b + 1)
                    v.tensor_scalar(sQ[:], misc[:], par[:, 1:2], None, ALU.mult).then_inc(misc_used, 1)
                elif name == "k":
                    if not first:
                        dve.wait_ge(split_ok["k"], b + 1)
                    v.tensor_copy(sK[:], misc[:]).then_inc(misc_used, 1)
                elif name == "mixed":
                    dve.wait_ge(split_ok["q"], b + 2)
                    v.tensor_copy(sA[:], misc[:]).then_inc(misc_used, 1)
                elif name == "v":
                    if not first:
                        dve.wait_ge(pv_done, b * NQ + 1)
                    v.tensor_copy(V1[pn][:, :, :, 0:HD], misc[:].rearrange("p (t h d) -> p t h d", t=TT, h=H)).then_inc(misc_used, 1)
                elif name[0] == "o":
                    s = int(name[1])
                    o = misc[:].rearrange("p (t j r) -> p t j r", t=TT, j=QH)
                    v.reciprocal(rec[:], o[:, :, :, HD]).then_inc(rec_ok, 1)
                    dve.wait_ge(rec_ok, b * NQ + s + 1)
                    v.tensor_tensor(at[:, :, s * QH * HD:(s + 1) * QH * HD].rearrange("p t (j d) -> p t j d", j=QH),
                                    o[:, :, :, 0:HD],
                                    rec[:].rearrange("p t (j a) -> p t j a", a=1).to_broadcast([P, TT, QH, HD]),
                                    ALU.mult).then_inc(misc_used, 1)
                elif name == "merge":
                    v.tensor_copy(aT[:], misc[:]).then_inc(misc_used, 1)
                elif name == "proj":
                    bp = b - 1
                    zb = z[:, bass.ds(bp * TT, TT), :]
                    v.tensor_tensor(zb, misc[:].rearrange("p (t d) -> p t d", t=TT), zb, ALU.add).then_inc(misc_used, 1)
                elif name[0] == "w":
                    i = int(name[1])
                    dst = (hid[0], hid[1])[i % 2]
                    j = b * (E // 2) * 2 + i
                    if j >= 2:
                        dve.wait_ge(ew_out, (j - 1) * 16)
                    v.tensor_copy(dst[:].rearrange("p c n -> p (c n)"), misc[:]).then_inc(misc_used, 1)
                elif name[:2] == "fx":
                    v.tensor_copy(xsT[:], misc[:, 0:FG * P].rearrange("p (i n) -> p i n", i=FG)).then_inc(misc_used, 1)
                elif name[0] == "h":
                    i = int(name[1])
                    v.tensor_tensor(hid[i][:], misc[:].rearrange("p (c n) -> p c n", c=FC),
                                    w1[i][:, F:F + FC].rearrange("p (c a) -> p c a", a=1).to_broadcast([P, FC, P]),
                                    ALU.add).then_inc(misc_used, 1)
                elif name[:2] == "fy":
                    k = (b - F_FROM) * 2 + (1 if name[-1] == "B" else 0)
                    dve.wait_ge(y_out, k * 16 + 1)
                    for i in range(FG):
                        m = v.tensor_tensor(ysb[:, i, :], misc[:, i * P:(i + 1) * P], w2[i][:, F:F + D], ALU.add)
                    m.then_inc(misc_used, 1)

            def normalise(tile):
                i = tile % NXS
                if tile >= NXS:
                    dve.wait_ge(xs_sent[i], tile // NXS * 16)
                v.tensor_scalar(xs[i], z[:, tile, :], mean[:, tile:tile + 1], rstd[:, tile:tile + 1],
                                ALU.subtract, ALU.mult).then_inc(xs_ok, 1)

            def add_back(tile):
                i = tile % NYG
                dve.wait_ge(yg_in[i], tile // NYG * 16 + 16)
                v.tensor_tensor(z[:, tile, :], z[:, tile, :], yg[:, i, :], ALU.add).then_inc(sum_ok, 1)

            def maxima(bn):
                with dve.Fori(0, H) as h:
                    for qt in range(TT):
                        w, i = (qt + 1) * P, h * TT + qt
                        dve.wait_ge(px_full, bn * NPX + i * 2 + 2)
                        v.scalar_tensor_tensor(out=tmax[:, 0:w], in0=tmax[:, 0:w], scalar=par[:, 0:1], in1=misc[:, 0:w],
                                               op0=ALU.mult, op1=ALU.add).then_inc(px_sum, 1)
                        dve.wait_ge(px_sum, (bn * HT + i) * 2 + 1)
                        v.tensor_tensor(tmax[:, w - P:w], tmax[:, w - P:w], hidden[:], ALU.add).then_inc(px_sum, 1)
                        dve.wait_ge(px_sum, (bn * HT + i) * 2 + 2)
                        v.tensor_reduce(mx[:, bass.ds(i, 1)], tmax[:, 0:w], AX, ALU.max, negate=True).then_inc(px_max, 1)
                        dve.sem_inc(px_used, 1)
                dve.wait_ge(px_full, (bn + 1) * NPX)
                m, link = misc[0:HT, 0:P], Link(dve, px_split, bn * 4)
                link(v.tensor_copy(mparts[:, 0, :], m))
                link(v.tensor_tensor(mrest[:], m, mparts[:, 0, :], ALU.subtract))
                link(v.tensor_copy(mparts[:, 1, :], mrest[:]))
                link(v.tensor_tensor(mparts[:, 2, :], mrest[:], mparts[:, 1, :], ALU.subtract))
                dve.sem_inc(px_used, 1)

            dve.sem_inc(px_used, 1)
            dve.sem_inc(px_max, 1)
            for n, name in enumerate(PROLOGUE):
                if name != "codes":
                    take(name, n, -1, 1)
            dve.wait_ge(hidden_ok, 2)
            with general(dve):
                maxima(0)
            for c in range(NC):
                for half in range(2):
                    add(0, 0, c, half)

            def body(b, pb, kind):
                pending = []
                if kind != "first":
                    before = KIND_BEFORE.get(kind, "ffn")
                    pending = [("o3", turn(b, kind, KINDS[kind][0][2]) - 1, b - 1, 1 - pb)]
                for s in range(NQ):
                    bf, _, qf = following(b, pb, s)
                    front = not (kind == "last" and s == NQ - 1)
                    for c in range(NC):
                        if c == 4:
                            dve.wait_ge(pv_done, b * NQ + s + 2)
                            v.tensor_copy(oT[:], pv[:]).then_inc(oT_ok, 1)
                        if front:
                            add(bf, qf, c, 0)
                        for p in pending:
                            take(*p)
                        pending = []
                        if kind in ("first", "second") and c < 4:
                            for i in range(2):
                                normalise((b * NQ + s) * 8 + c * 2 + i)
                        if kind in ("plain", "last") and c > 0:
                            tile = ((b - B + 2) * NQ + s - 1) * NYG + c - 1
                            if tile >= 0:
                                add_back(tile)
                        if front:
                            add(bf, qf, c, 1)
                        if s == NQ - 2 and c == 3 and kind != "last":
                            with general(dve):
                                maxima(b + 1)
                        for name in jobs_at(kind, s, c):
                            if name == "codes":
                                continue
                            p = (name, turn(b, kind, name), b, pb)
                            if name == "fyA":
                                take(*p)
                            else:
                                pending.append(p)

            each_batch(dve, body)
            take("o3", TAIL_TURN - 1, B - 1, 1)
            take("merge", TAIL_TURN, B - 1, 1)
            take("proj", TAIL_TURN + 1, B, 0)
            for tile in range(NTOK // 2 - NYG, NTOK):
                add_back(tile)

        @block.gpsimd
        def _(pool):
            gp = nc.gpsimd
            ones_t = one[:].to_broadcast([P, T])
            pool.wait_ge(rk_clear, 3)
            pool.wait_ge(hidden_ok, 1)
            gp.affine_select(out=hidden[:], in_=hidden[:], compare_op=ALU.is_ge, fill=-3e38, base=0, pattern=[[-1, P]],
                             channel_multiplier=1).then_inc(hidden_ok, 1)

            def mask(b, s, first):
                Sq = S[:, s % 2]
                pool.wait_ge(e_done, (b * NQ + s) * 3 + (2 if first else 3))
                pool.sem_inc(waited, 1)
                if first:
                    x = Sq[:, 0:QH, 0:P]
                    gp.affine_select(out=x, in_=x, compare_op=ALU.is_ge, fill=0.0, base=0, pattern=[[0, QH], [1, P]],
                                     channel_multiplier=-1)
                    x = Sq[:, 0:QH, T:T + 2 * P].rearrange("p c (k n) -> p c k n", k=2)
                    gp.affine_select(out=x, in_=x, compare_op=ALU.is_ge, fill=0.0, base=0, pattern=[[0, QH], [0, 2], [1, P]],
                                     channel_multiplier=-1).then_inc(m_done, 1)
                else:
                    x = Sq[:, QH].rearrange("p (j n) -> p j n", j=QH)[:, :, 0:P]
                    gp.affine_select(out=x, in_=x, compare_op=ALU.is_ge, fill=0.0, base=0, pattern=[[0, QH], [1, P]],
                                     channel_multiplier=-1).then_inc(m_done, 1)

            def split(n, bn, k):
                src, r, pt = {"q": sQ, "k": sK, "a": sA}[n][:], rest[:], parts
                link = Link(pool, split_chain, (bn * 3 + "qka".index(n)) * 3)
                pool.wait_ge(misc_used, k + 1)
                if n == "k":
                    pool.wait_ge(stored["q"], bn * 16 + 16)
                elif n == "a":
                    pool.wait_ge(stored["k"], bn * 16 + 16)
                elif not (isinstance(bn, int) and bn == 0):
                    pool.wait_ge(stored["a"], bn * 16)
                    pool.wait_ge(h_stored, bn * 32)
                link(gp.tensor_tensor(pt[:, 0, :], src, ones_t, ALU.mult))
                link(gp.tensor_tensor(r, src, pt[:, 0, :], ALU.subtract))
                link(gp.tensor_tensor(pt[:, 1, :], r, ones_t, ALU.mult))
                gp.tensor_tensor(pt[:, 2, :], r, pt[:, 1, :], ALU.subtract).then_inc(split_ok[n], 1)
                pool.wait_ge(split_ok[n], bn + 1)

            def scatter(tile):
                pool.wait_ge(xs_ok, tile + 1)
                gp.indirect_dma_start(out=xs_d, out_offset=bass.IndirectOffsetOnAxis(ap=posu[:, tile:tile + 1], axis=0),
                                      in_=xs[tile % NXS], in_offset=None).then_inc(xs_sent[tile % NXS], 16)

            def gather(tile):
                if tile >= NYG:
                    pool.wait_ge(sum_ok, tile - NYG + 1)
                gp.indirect_dma_start(out=yg[:, tile % NYG, :], out_offset=None, in_=ys_d,
                                      in_offset=bass.IndirectOffsetOnAxis(ap=posu[:, tile:tile + 1], axis=0)).then_inc(yg_in[tile % NYG], 16)

            def relu(k, i, n):
                pool.wait_ge(misc_used, n + 1)
                pool.sem_inc(waited, 1)
                gp.tensor_scalar(hid[i][:], hid[i][:], 0.0, None, ALU.max).then_inc(relu_ok, 1)

            for n, name in (("q", "q"), ("k", "k"), ("a", "mixed")):
                split(n, 0, PROLOGUE.index(name))

            def body(b, pb, kind):
                for s in range(NQ):
                    mask(b, s, True)
                    mask(b, s, False)
                    if kind in ("first", "second"):
                        for i in range(8):
                            scatter((b * NQ + s) * 8 + i)
                    for at_s, n, name in ((0, "q", "q"), (1, "k", "k"), (2, "a", "mixed")):
                        if s == at_s and kind != "last":
                            split(n, b + 1, turn(b, kind, name))
                    if kind == "ffn" and s >= 2:
                        for i in range(FG):
                            relu((b - F_FROM) * 2 + s - 2, i, turn(b, kind, f"h{i}" + "AB"[s - 2]))
                    if kind in ("plain", "last"):
                        if kind == "plain" and s == 0:
                            pool.wait_ge(y_all, 1)
                        for i in range(NYG):
                            gather(((b - B + 2) * NQ + s) * NYG + i)
                if kind == "second":
                    for i in range(NXS):
                        pool.wait_ge(xs_sent[i], (NTOK - i + NXS - 1) // NXS * 16)
                    pool.sem_inc(xs_done, 1)

            each_batch(pool, body)
            for tile in range(NTOK // 2, NTOK):
                gather(tile)

        @block.sync
        def _(sp):
            sp.sem_inc(y_out, 1)

            def load_x(b, pb):
                src = xt_d[b] if isinstance(b, int) else xt_d[bass.ds(b, 1)].rearrange("b p n -> p (b n)")
                sp.dma_start(xTr[pb][:], src).then_inc(xt_in[pb], 16)

            def stack_q(bn, pn):
                sp.wait_ge(split_ok["q"], bn + 1)
                sp.dma_start(qp_d[pn].rearrange("t r n -> r t n"), parts[:]).then_inc(stored["q"], 16)
                sp.wait_ge(stored["q"], bn * 16 + 16)
                if not (isinstance(bn, int) and bn == 0):
                    sp.wait_ge(raw_full, (bn - 1) * (NQ * NC) + 1)
                    sp.wait_ge(lin_full, (bn - 1) * (NQ * NC * 2) + 1)
                for t in range(NTERM):
                    sp.dma_start(QS[pn][t * HD:(t + 1) * HD].rearrange("d h n -> d (h n)"),
                                 qp_d[pn, QPART[t]].rearrange("(d h) n -> d (h n)", h=H)).then_inc(raw_in[pn], 16)

            def stack_k(bn, pn):
                sp.wait_ge(split_ok["k"], bn + 1)
                sp.dma_start(kp_d[pn].rearrange("t r n -> r t n"), parts[:]).then_inc(stored["k"], 16)
                sp.wait_ge(stored["k"], bn * 16 + 16)
                for r0, k in ((0, 3), (3, 2), (5, 1)):
                    sp.dma_start(RK[pn][r0 * HD:(r0 + k) * HD].rearrange("d h n -> d (h n)"),
                                 kp_d[pn, 0:k].rearrange("t (d h) n -> (t d) (h n)", h=H)).then_inc(raw_in[pn], 16)

            def stack_a(bn, pn):
                sp.wait_ge(split_ok["a"], bn + 1)
                for kind in range(2):
                    r0 = HAM0 + (1 + kind) * NE6
                    sp.dma_start(hp_d[pn, kind].rearrange("t e n -> e t n"), parts[r0:r0 + NE6]).then_inc(h_stored, 16)
                sp.dma_start(ap_d[pn, :, 0:HAM0 + NE6].rearrange("t r n -> r t n"), parts[0:HAM0 + NE6]).then_inc(stored["a"], 16)
                sp.wait_ge(h_stored, bn * 32 + 32)
                for kind in range(2):
                    for r0, k in ((0, 3), (3, 2), (5, 1)):
                        row = RK_ROWS + (kind * NTERM + r0) * NE6
                        sp.dma_start(LK[pn][row:row + k * NE6, :],
                                     hp_d[pn, kind, 0:k].rearrange("t e n -> (t e) n")).then_inc(lin_in[pn], 16)
                sp.wait_ge(stored["a"], bn * 16 + 16)
                for t in range(NTERM):
                    row = RK_ROWS + t * NE6
                    sp.dma_start(QS[pn][row:row + NE6].rearrange("e h n -> e (h n)"),
                                 ap_d[pn, QPART[t], 0:HAM0].rearrange("(e h) n -> e (h n)", h=H)).then_inc(lin_in[pn], 16)
                    row = RK_ROWS + (NTERM + t) * NE6
                    sp.dma_start(QS[pn][row:row + NE6],
                                 ap_d[pn, QPART[t], HAM0:HAM0 + NE6].rearrange("e (a n) -> e a n", a=1).to_broadcast([NE6, H, T])).then_inc(lin_in[pn], 16)

            def load_experts(e):
                if e >= 2:
                    n = e - 2
                    kind, b = ("first", 0) if n < E // 2 else ("second", 1)
                    sp.wait_ge(misc_full, turn(b, kind, f"w{n % (E // 2) * 2 + 1}") + 1)
                sp.dma_start(w1[e % 2][:, 0:F].rearrange("p (c d) -> p c d", c=FC),
                             a["L0_ffn_W1"][e].rearrange("(c p) d -> p c d", p=P)).then_inc(ew_in[e % 2], 16)
                sp.dma_start(w2[e % 2][:, 0:F], a["L0_ffn_W2"][e]).then_inc(ew_in[e % 2], 16)

            def store_expert(b, kind, i):
                e = b * (E // 2) + i // 2
                sp.wait_ge(misc_used, turn(b, kind, f"w{i}") + 1)
                if i % 2 == 0:
                    sp.dma_start(w1_d[e, :, 0:F], hid[0][:].rearrange("p c n -> p (c n)")).then_inc(ew_out, 16)
                else:
                    sp.dma_start(w2_d[e, :, 0:F], hid[1][:].rearrange("p c n -> p (c n)")).then_inc(ew_out, 16)
                sp.wait_ge(ew_out, (b * E + i + 1) * 16)

            def expert(s):
                sp.sem_inc(waited_sp, 1)
                return sp.value_load(etile[0:1, bass.ds(s, 1)], min_val=0, max_val=E - 1)

            def load_rows(k, before):
                sp.wait_ge(misc_full, before("fx") + 1)
                sp.dma_start(xin[:], xs_d[bass.ds(k * (FG * P), FG * P), :].rearrange("(i p) d -> p i d", p=P)).then_inc(fx_in, 16)

            def load_w1(k, i, before):
                sp.wait_ge(misc_used, before(f"h{i}") + 1)
                e = expert(k * FG + i)
                sp.dma_start(w1[i][:], w1_d[bass.ds(e, 1)].rearrange("e p f -> p (e f)")).then_inc(w1_in[i], 16)

            def load_w2(k, before):
                sp.wait_ge(misc_used, before("fy") + 1)
                for i in range(FG):
                    e = expert(k * FG + i)
                    sp.dma_start(w2[i][:], w2_d[bass.ds(e, 1)].rearrange("e p f -> p (e f)")).then_inc(w2_in, 16)

            def store_rows(k, n):
                sp.wait_ge(misc_used, n + 1)
                sp.dma_start(ys_d[bass.ds(k * (FG * P), FG * P), :].rearrange("(i p) d -> p i d", p=P), ysb[:]).then_inc(y_out, 16)

            def shift(bn, pn):
                sp.wait_ge(px_split, bn * 4 + 4)
                sp.dma_start(mx_d[pn].rearrange("t (r n) -> r t n", n=P), mparts[:]).then_inc(px_out, 16)
                sp.wait_ge(px_out, bn * 16 + 16)
                sp.dma_start(QS[pn][SHIFT0:ROWS].rearrange("r h n -> r (h n)"), mx_d[pn]).then_inc(px_in, 16)

            load_x(0, 0)
            load_x(1, 1)
            load_experts(0)
            load_experts(1)
            sp.wait_ge(rk_clear, 3)
            stack_q(0, 0)
            stack_k(0, 0)
            stack_a(0, 0)
            with general(sp):
                shift(0, 0)

            def body(b, pb, kind):
                bn, pn = b + 1, 1 - pb
                k = (b - F_FROM) * 2 if kind == "ffn" else None
                if kind in ("first", "second"):
                    stack_q(bn, pn)
                    stack_k(bn, pn)
                    for i in range(E):
                        store_expert(b, kind, i)
                        if i % 2 == 1:
                            e = b * (E // 2) + i // 2 + 2
                            if e < E:
                                load_experts(e)
                        if i == 3:
                            stack_a(bn, pn)
                            with general(sp):
                                shift(bn, pn)
                    if kind == "second":
                        sp.wait_ge(xs_done, 1)
                if kind == "ffn":
                    prior = lambda j: turn(b - 1, kind, j + "B")
                    load_rows(k, prior)
                    for i in range(FG):
                        load_w1(k, i, prior)
                    load_w2(k, prior)
                    stack_q(bn, pn)
                    stack_k(bn, pn)
                    own = lambda j: turn(b, kind, j + "A")
                    load_rows(k + 1, own)
                    load_w1(k + 1, 0, own)
                    load_w1(k + 1, 1, own)
                    stack_a(bn, pn)
                    with general(sp):
                        shift(bn, pn)
                    load_w1(k + 1, 2, own)
                    store_rows(k, turn(b, kind, "fyA"))
                    load_w2(k + 1, own)
                    store_rows(k + 1, turn(b, kind, "fyB"))
                if kind == "plain":
                    sp.wait_ge(y_out, NSLOT // FG * 16 + 1)
                    sp.sem_inc(y_all, 1)
                    stack_q(bn, pn)
                    stack_k(bn, pn)
                    stack_a(bn, pn)
                    with general(sp):
                        shift(bn, pn)
                if kind in ("first", "second", "ffn"):
                    sp.wait_ge(misc_full, turn(b, kind, "o3"))
                    if kind == "ffn" and not isinstance(b, int):
                        load_x_ahead(b, pb)
                    else:
                        load_x(b + 2, pb)

            def load_x_ahead(b, pb):
                load_x(b + 2, pb)

            each_batch(sp, body)

            def store_out(b):
                sp.wait_ge(sum_ok, (b + 1) * TT)
                if b == B - 1:
                    sp.wait_ge(misc_used, TAIL_TURN + 2)
                sp.dma_start(out[b].rearrange("(t p) d -> p t d", p=P), z[:, b * TT:(b + 1) * TT, :]).then_inc(final_out, 16)

            for b in range(B):
                store_out(b)
            sp.wait_ge(final_out, 16 * B)


_OUTS = [((16, 512, 128), 'float32')]
def kernel(**inputs):
    import numpy as _np
    import concourse.bacc as _bacc
    from concourse import mybir as _mybir
    from concourse.bass_utils import run_bass_kernel_spmd as _run
    nc = _bacc.Bacc("TRN2", target_bir_lowering=False, num_devices=1)
    arrays, args = {}, {}
    for name in inputs:
        a = _np.ascontiguousarray(inputs[name])
        arrays[f"in_{name}_dram"] = a
        args[name] = nc.dram_tensor(f"in_{name}_dram", a.shape, _mybir.dt.from_np(a.dtype), kind="ExternalInput").ap()
    out = nc.dram_tensor("out_0_dram", (16, 512, 128), _mybir.dt.float32, kind="ExternalOutput").ap()
    build(nc, args, out)
    r = _run(nc, [arrays], core_ids=[0])
    return r.results[0]["out_0_dram"]
```

```python
from contextlib import ExitStack

import concourse.bass as bass
from concourse import mybir

F32 = mybir.dt.float32
BF16 = mybir.dt.bfloat16
I32 = mybir.dt.int32
U32 = mybir.dt.uint32
ALU = mybir.AluOpType
ACT = mybir.ActivationFunctionType
AX = mybir.AxisListType.X

P = 128
B, T, D = 16, 512, 128
H, HD = 16, 8
NT, NE6 = 7, 6
E, F = 8, 512
TT = T // P
NTOK = B * TT
FC = F // P
NSLOT = 72
FG = 3
HP = 32
QH = 4
NQ = H // QH
CH = 2 * T
NC = 5
NTERM = 6
QPART = (0, 0, 0, 1, 1, 2)
RK_ROWS = NTERM * HD
LK_ROWS = 2 * NTERM * NE6
NSHIFT = 3
SHIFT0 = RK_ROWS + LK_ROWS
ROWS = SHIFT0 + NSHIFT
HEX0 = 32
HAM0 = H * NE6
NA = HAM0 + 3 * NE6
SAFE_RANGE = 40.0


def chunk_parts():
    parts = []
    for j in range(QH):
        parts.append((j, 0, j, 0, 0))
        parts.append((j, T, j, 3, 3 * P))
        parts.append((j, T + P, j, 1, P))
        parts.append((QH, j * 2 * P, j, 2, 2 * P))
    return parts


PARTS = chunk_parts()


def build(nc, a, out):
    x_d = a["L0_attn_x"]
    with ExitStack() as ctx:
        def sb(name, shape, dt=F32):
            return ctx.enter_context(nc.sbuf_tensor(name, shape, dt))

        def sem(name):
            return ctx.enter_context(nc.semaphore(name))

        w1_d = nc.dram_tensor("w1_transposed_b1", [E, P, F + FC], F32, kind="Internal").ap()
        w2_d = nc.dram_tensor("w2_transposed_b2", [E, P, F + D], F32, kind="Internal").ap()
        mx_d = nc.dram_tensor("shift_parts", [2, NSHIFT, H * T], BF16, kind="Internal").ap()
        xt_d = nc.dram_tensor("xn_transposed", [B, P, T], F32, kind="Internal").ap()
        xs_d = nc.dram_tensor("x_sorted", [NSLOT * P, D], F32, kind="Internal").ap()
        ys_d = nc.dram_tensor("y_sorted", [NSLOT * P, D], F32, kind="Internal").ap()
        m_d = nc.dram_tensor("mix", [H, NE6 * NE6], F32, kind="Internal").ap()
        qp_d = nc.dram_tensor("q_parts", [2, 3, P, T], BF16, kind="Internal").ap()
        kp_d = nc.dram_tensor("k_parts", [2, 3, P, T], BF16, kind="Internal").ap()
        ap_d = nc.dram_tensor("a_parts", [2, 3, P, T], BF16, kind="Internal").ap()
        hp_d = nc.dram_tensor("h_parts", [2, 2, 3, NE6, T], BF16, kind="Internal").ap()

        ident = sb("ident", [P, P])
        z = sb("z", [P, NTOK, D])
        wqkvT = sb("wqkvT", [P, 3 * D])
        woT = sb("woT", [P, D])
        hexT = sb("hexT", [P, 64])
        mixS = sb("mixS", [64, P])
        par = sb("par", [P, 8])
        posu = sb("posu", [P, NTOK], U32)
        etile = sb("etile", [P, NSLOT], I32)
        flag = sb("flag", [1, 1], I32)
        mean = sb("mean", [P, NTOK])
        rstd = sb("rstd", [P, NTOK])
        S = sb("S", [P, 2, NC, CH])
        QS = [sb(f"QS{i}", [ROWS, H, T], BF16) for i in range(2)]
        LK = [sb(f"LK{i}", [ROWS, T], BF16) for i in range(2)]
        V1 = [sb(f"V1_{i}", [P, TT, H, HP]) for i in range(2)]

        ps = [ctx.enter_context(nc.psum_tensor(f"bank{i}", [P, T], F32)) for i in range(1)]
        raw = [ctx.enter_context(nc.psum_tensor(f"raw{i}", [P, CH], F32)) for i in range(2)]
        lin = [ctx.enter_context(nc.psum_tensor(f"lin{i}", [P, T], F32)) for i in range(2)]
        pv = ctx.enter_context(nc.psum_tensor("pv", [P, T], F32))
        misc = ps[0]

        setup(nc, a, out, locals())
        layer(nc, a, out, locals())


class Link:

    def __init__(self, eng, sem, base=0):
        self.eng, self.sem, self.n = eng, sem, base

    def __call__(self, ins):
        self.n = self.n + 1
        ins.then_inc(self.sem, 1)
        self.eng.wait_ge(self.sem, self.n)


def setup(nc, a, out, g):
    ident, z, wqkvT, woT, hexT, mixS, par = (g[k] for k in ("ident", "z", "wqkvT", "woT", "hexT", "mixS", "par"))
    posu, etile, flag, mean, rstd, S, V1 = (g[k] for k in ("posu", "etile", "flag", "mean", "rstd", "S", "V1"))
    QS, LK, raw, lin, pv, misc = (g[k] for k in ("QS", "LK", "raw", "lin", "pv", "misc"))
    w1_d, w2_d, xt_d, xs_d, m_d, x_d = (g[k] for k in ("w1_d", "w2_d", "xt_d", "xs_d", "m_d", "x_d"))
    SX = 9 * P * 2
    NCLEAR = NSLOT * D // SX
    with ExitStack() as ctx:
        def sb(name, shape, dt=F32):
            return ctx.enter_context(nc.sbuf_tensor(name, shape, dt))

        def sem(name):
            return ctx.enter_context(nc.semaphore(name))

        small_in, x_in, w_in, b1_in = sem("small_in"), [sem(f"x_in{i}") for i in range(4)], sem("w_in"), sem("b1_in")
        const_ok, cleared, zeros_ok = sem("const_ok"), sem("cleared"), sem("zeros_ok")
        pe_small, small_out, act_chain, dve_chain, pool_chain = sem("pe_small"), sem("small_out"), sem("act_chain"), sem("dve_chain"), sem("pool_chain")
        b1_ok, b1_out, b2_out = sem("b1_ok"), sem("b1_out"), sem("b2_out")
        var_ok, root_ok, xn_ok, xnT_full, xnT_ok, lg_full, lg_out, xt_out = (sem(n) for n in (
            "var_ok", "root_ok", "xn_ok", "xnT_full", "xnT_ok", "lg_full", "lg_out", "xt_out"))
        oh_ok, rank_full, stats_ok = sem("oh_ok"), sem("rank_full"), sem("stats_ok")
        mix_exp_in, mix_exp, sig_in, sig_exp, mix_sb, mix_out, mix_in, ones_in = (sem(n) for n in (
            "mix_exp_in", "mix_exp", "sig_in", "sig_exp", "mix_sb", "mix_out", "mix_in", "ones_in"))

        wqkv = sb("wqkv", [P, 3, D])
        wo = sb("wo", [P, D])
        hx = sb("hx", [64, D])
        wr = sb("wr", [E, D])
        wrT = sb("wrT", [P, E])
        brr = sb("brr", [P, E])
        b1 = sb("b1", [E * FC, P])
        b1T = sb("b1T", [P, E * FC])
        b2r = sb("b2r", [P, E, D])
        tw = sb("tw", [H, NT])
        twT = sb("twT", [NT, H])
        tr = sb("tr", [NT, NE6 * NE6])
        st16 = sb("st16", [H, 8])
        mix = sb("mix_sb_t", [H, NE6 * NE6])
        plog = sb("plog", [P, 8])
        stats = sb("stats", [P, NTOK, 6])
        tA, tB, tC, tD = (sb(n, [P, NTOK]) for n in ("tA", "tB", "tC", "tD"))
        xn = [sb(f"xn{i}", [P, TT, D]) for i in range(2)]
        xT = [sb(f"xT{i}", [P, T]) for i in range(2)]
        lg = sb("lg", [P, NTOK, E])
        eq = sb("eq", [P, NTOK, E])
        ohf = sb("ohf", [P, NTOK, E])
        ohb = sb("ohb", [P, NTOK, E], BF16)
        scan = [sb(f"scan{i}", [P, NTOK, E]) for i in range(2)]
        cmp = sb("cmp", [P, NSLOT, E])
        sm = sb("sm", [P, 8, E])
        desc = sb("desc", [P, E])
        j128 = sb("j128", [P, NTOK])
        slotid = sb("slotid", [P, NSLOT])
        tri = sb("tri", [P, P], BF16)
        onesb = sb("onesb", [P, P], BF16)
        onesrow = sb("onesrow", [NSHIFT, T], BF16)
        zeros = S[:, 0].rearrange("p c n -> p (c n)")[:, 0:SX]
        NSMALL = 12

        block = ctx.enter_context(nc.Block())

        @block.sync
        def _(sp):
            sp.sem_inc(xt_out, 1)
            sp.dma_start(wqkv[:], a["L0_attn_qkv_w"].rearrange("(c p) d -> p c d", p=P)).then_inc(w_in, 16)
            sp.dma_start(wo[:], a["L0_attn_out_w"]).then_inc(w_in, 16)
            sp.wait_ge(zeros_ok, 1)
            sp.dma_start(hx[0:NE6], a["L0_attn_hex_w"]).then_inc(w_in, 16)
            sp.dma_start(hx[HEX0:HEX0 + NE6], a["L0_attn_q6_w"]).then_inc(w_in, 16)
            sp.dma_start(wr[:], a["L0_ffn_Wr"]).then_inc(w_in, 16)
            sp.dma_start(b1[:], a["L0_ffn_b1"].rearrange("e (c p) -> (e c) p", p=P)).then_inc(w_in, 16)
            for i in range(4):
                q = NTOK // 4
                sp.dma_start(z[:, i * q:(i + 1) * q, :],
                             x_d[4 * i:4 * i + 4].rearrange("b (t p) d -> p (b t) d", p=P)).then_inc(x_in[i], 16)
            sp.wait_ge(b1_ok, 1)
            sp.dma_start(w1_d[:, :, F:F + FC].rearrange("e p c -> p e c"), b1T[:].rearrange("p (e c) -> p e c", c=FC)).then_inc(b1_out, 16)
            with sp.Fori(0, B // 2) as bp:
                for i in range(2):
                    sp.wait_ge(xnT_ok, bp * 2 + i + 2)
                    sp.dma_start(xt_d[bass.ds(bp * 2 + i, 1)].rearrange("b p n -> p (b n)"), xT[i][:]).then_inc(xt_out, 16)
            sp.wait_ge(mix_in, 16)
            sp.wait_ge(xt_out, 16 * B + 1)
            sp.wait_ge(b1_out, 16)
            sp.wait_ge(b2_out, 16)

        @block.scalar
        def _(act):
            act.sem_inc(xnT_ok, 1)
            for k, (dst, src) in enumerate((
                (par[:, 0:1], a["L0_attn_sips_alpha"].rearrange("(a n) -> a n", a=1).to_broadcast([P, 1])),
                (plog[:, 0:1], a["L0_attn_sips_beta"].rearrange("(a n) -> a n", a=1).to_broadcast([P, 1])),
                (plog[:, 1:2], bass.AP(a["L0_attn_hamming_lambda_logit"].tensor, 0, [[0, P], [1, 1]])),
                (plog[:, 2:3], bass.AP(a["L0_attn_scale_logit"].tensor, 0, [[0, P], [1, 1]])),
                (brr[:], a["L0_ffn_br"].rearrange("(a n) -> a n", a=1).to_broadcast([P, E])),
                (b2r[:], bass.AP(a["L0_ffn_b2"].tensor, 0, [[0, P], [D, E], [1, D]])),
                (tw[:], a["L0_attn_transform_weights"]),
                (tr[:], a["L0_attn_transforms"].rearrange("t d e -> t (d e)")),
            )):
                act.dma_start(dst, src).then_inc(small_in, 16)
            act.wait_ge(zeros_ok, 1)
            for i in range(NCLEAR):
                act.dma_start(xs_d.rearrange("(p r) d -> p (r d)", p=P)[:, i * SX:(i + 1) * SX], zeros).then_inc(cleared, 16)
            for i in range(2):
                act.dma_start(LK[i][SHIFT0:ROWS, :], onesrow[:]).then_inc(ones_in, 16)
            act.wait_ge(mix_exp_in, 1)
            nc.scalar.activation(st16[:, 0:NT], tw[:], ACT.Exp, bias=st16[:, 7:8], scale=2.0).then_inc(mix_exp, 1)
            nc.scalar.activation(plog[:, 4:6], plog[:, 1:3], ACT.Exp, scale=-1.0).then_inc(sig_exp, 1)
            act.wait_ge(mix_sb, 1)
            act.dma_start(g["m_d"], mix[:]).then_inc(mix_out, 16)
            act.wait_ge(mix_out, 16)
            act.dma_start(mixS[HEX0:HEX0 + NE6, 0:H * NE6].rearrange("d (e h) -> d e h", h=H),
                          g["m_d"].rearrange("h (d e) -> d e h", e=NE6), allow_slow_non_contiguous=True).then_inc(mix_in, 16)
            act.wait_ge(small_in, 16 * 8)
            act.dma_start(w2_d[:, :, F:F + D].rearrange("e p d -> p e d"), b2r[:]).then_inc(b2_out, 16)
            act.wait_ge(var_ok, 1)
            nc.scalar.activation(rstd[:], tB[:], ACT.Sqrt).then_inc(root_ok, 1)
            with act.Fori(0, B // 2) as bp:
                for i in range(2):
                    act.wait_ge(xnT_full, bp * 2 + i + 2)
                    act.wait_ge(xt_out, bp * 32 + 1)
                    act.wait_ge(lg_full, bp * 2 + 1)
                    nc.scalar.copy(xT[i][:], lin[i][:]).then_inc(xnT_ok, 1)
            act.wait_ge(ones_in, 32)
            act.wait_ge(cleared, 16 * NCLEAR)

        @block.gpsimd
        def _(pool):
            link = Link(pool, pool_chain)
            link(nc.gpsimd.memset(hx[:], 0.0))
            link(nc.gpsimd.memset(zeros, 0.0))
            for i in range(2):
                link(nc.gpsimd.memset(LK[i][:], 0.0))
            nc.gpsimd.memset(onesrow[:], 1.0).then_inc(zeros_ok, 1)
            link(nc.gpsimd.memset(ident[:], 0.0))
            link(nc.gpsimd.affine_select(out=ident[:], in_=ident[:], compare_op=ALU.not_equal, fill=1.0, base=0,
                                         pattern=[[-1, P]], channel_multiplier=1))
            link(nc.gpsimd.memset(onesb[:], 1.0))
            link(nc.gpsimd.affine_select(out=tri[:], in_=onesb[:], compare_op=ALU.is_gt, fill=0.0, base=0,
                                         pattern=[[1, P]], channel_multiplier=-1))
            link(nc.gpsimd.iota(j128[:], pattern=[[P, NTOK]], base=0, channel_multiplier=0, allow_small_or_imprecise_dtypes=True))
            link(nc.gpsimd.iota(slotid[:], pattern=[[1, NSLOT]], base=0, channel_multiplier=0, allow_small_or_imprecise_dtypes=True))
            nc.gpsimd.iota(desc[:], pattern=[[-1, E]], base=E, channel_multiplier=0,
                           allow_small_or_imprecise_dtypes=True).then_inc(const_ok, 1)
            for i in range(2):
                link(nc.gpsimd.memset(V1[i][:], 0.0))
                link(nc.gpsimd.memset(V1[i][:, :, :, HD:HD + 1], 1.0))
                link(nc.gpsimd.memset(QS[i][96:ROWS].rearrange("p h n -> p (h n)"), 0.0))

        @block.tensor
        def _(pe):
            pe.sem_inc(xnT_full, 1)
            pe.sem_inc(lg_full, 1)
            pe.wait_ge(const_ok, 1)
            pe.wait_ge(w_in, 96)
            for c in range(3):
                m = nc.tensor.transpose(misc[:, c * D:(c + 1) * D], wqkv[:, c, :], ident[:])
            m.then_inc(pe_small, 1)
            m = nc.tensor.transpose(pv[:, 0:D], wo[:], ident[:])
            m = nc.tensor.transpose(pv[:, D:D + 64], hx[:], ident[0:64, 0:64])
            m = nc.tensor.transpose(pv[:, 192:192 + E], wr[:], ident[0:E, 0:E])
            nc.tensor.transpose(pv[:, 256:256 + E * FC], b1[:], ident[0:E * FC, 0:E * FC]).then_inc(pe_small, 1)
            pe.wait_ge(mix_exp, 2)
            pe.wait_ge(small_out, 3)
            nc.tensor.transpose(misc[0:NT, 0:H], st16[:, 0:NT], ident[0:H, 0:H]).then_inc(pe_small, 1)
            pe.wait_ge(small_out, 4)
            nc.tensor.matmul(misc[0:H, 64:64 + NE6 * NE6], twT[:], tr[:], start=True, stop=True).then_inc(pe_small, 1)
            pe.wait_ge(small_out, 5)
            nc.tensor.matmul(misc[0:1, 128:128 + H], st16[:, 0:1], ident[0:H, 0:H], start=True, stop=True).then_inc(pe_small, 1)
            with pe.Fori(0, B // 2) as bp:
                for i in range(2):
                    pe.wait_ge(xn_ok, bp * 2 + i + 1)
                    pe.wait_ge(xnT_ok, bp * 2 + 1)
                    for t in range(TT):
                        m = nc.tensor.transpose(lin[i][:, t * P:(t + 1) * P], xn[i][:, t, :], ident[:])
                    m.then_inc(xnT_full, 1)
                    pe.wait_ge(xnT_ok, bp * 2 + i + 2)
                    pe.wait_ge(lg_out, bp * 2 + i + 1)
                    for t in range(TT):
                        m = nc.tensor.matmul(pv[:, t * E:(t + 1) * E], xT[i][:, t * P:(t + 1) * P], wrT[:],
                                             start=True, stop=True)
                    m.then_inc(lg_full, 1)
            pe.wait_ge(oh_ok, 1)
            oh = ohb[:].rearrange("p t e -> p (t e)")
            nc.tensor.matmul(misc[:, 0:T], tri[:], oh, start=True, stop=True).then_inc(rank_full, 1)
            nc.tensor.matmul(lin[0][:, 0:T], onesb[:], oh, start=True, stop=True).then_inc(rank_full, 1)

        @block.vector
        def _(dve):
            link = Link(dve, dve_chain)
            v = nc.vector
            dve.sem_inc(lg_out, 1)
            link(v.memset(mixS[:], 0.0))
            dve.wait_ge(pe_small, 1)
            v.tensor_copy(wqkvT[:, 0:2 * D].rearrange("p (c d h) -> p c d h", c=2, h=H)[:, 0],
                          misc[:, 0:D].rearrange("p (h d) -> p d h", h=H))
            v.tensor_copy(wqkvT[:, 0:2 * D].rearrange("p (c d h) -> p c d h", c=2, h=H)[:, 1],
                          misc[:, D:2 * D].rearrange("p (h d) -> p d h", h=H))
            v.tensor_copy(wqkvT[:, 2 * D:3 * D], misc[:, 2 * D:3 * D]).then_inc(small_out, 1)
            dve.wait_ge(pe_small, 2)
            dve.wait_ge(w_in, 96)
            v.tensor_copy(woT[:], pv[:, 0:D]).then_inc(small_out, 1)
            v.tensor_copy(hexT[:], pv[:, D:D + 64])
            v.tensor_copy(wrT[:], pv[:, 192:192 + E]).then_inc(small_out, 1)
            v.tensor_copy(b1T[:], pv[:, 256:256 + E * FC]).then_inc(b1_ok, 1)
            dve.wait_ge(small_in, 16 * 8)
            link(v.reduce_max(st16[:, 7:8], tw[:], AX))
            v.tensor_scalar(st16[:, 7:8], st16[:, 7:8], -2.0, None, ALU.mult).then_inc(mix_exp_in, 1)
            dve.wait_ge(mix_exp, 1)
            link(v.reduce_sum(st16[:, 7:8], st16[:, 0:NT], AX))
            link(v.reciprocal(st16[:, 7:8], st16[:, 7:8]))
            v.tensor_scalar(st16[:, 0:NT], st16[:, 0:NT], st16[:, 7:8], None, ALU.mult).then_inc(mix_exp, 1)
            dve.wait_ge(sig_exp, 1)
            link(v.tensor_scalar(plog[:, 4:6], plog[:, 4:6], 1.0, None, ALU.add))
            link(v.reciprocal(par[:, 2:4], plog[:, 4:6]))
            link(v.reciprocal(par[:, 1:2], plog[:, 0:1]))
            link(v.tensor_scalar(par[:, 4:5], par[:, 2:3], 0.5, None, ALU.mult))
            link(v.tensor_scalar(par[:, 5:6], par[:, 3:4], 2.0 / 6.0, None, ALU.mult))
            link(v.tensor_scalar(mixS[0:NE6, HAM0:HAM0 + NE6], ident[0:NE6, 0:NE6], par[0:NE6, 4:5], None, ALU.mult))
            link(v.tensor_copy(mixS[HEX0:HEX0 + NE6, HAM0 + NE6:HAM0 + 2 * NE6], ident[HEX0:HEX0 + NE6, HEX0:HEX0 + NE6]))
            link(v.tensor_copy(mixS[0:NE6, HAM0 + 2 * NE6:NA], ident[0:NE6, 0:NE6]))
            dve.wait_ge(pe_small, 3)
            v.tensor_copy(twT[:], misc[0:NT, 0:H]).then_inc(small_out, 1)
            dve.wait_ge(pe_small, 4)
            v.tensor_scalar(mix[:], misc[0:H, 64:64 + NE6 * NE6], par[0:H, 5:6], None, ALU.mult).then_inc(mix_sb, 1)
            dve.wait_ge(mix_sb, 1)
            v.tensor_reduce(st16[:, 0:1], mix[:], AX, ALU.add, apply_absolute_value=True).then_inc(small_out, 1)
            dve.wait_ge(pe_small, 5)
            link(v.reduce_max(plog[0:1, 6:7], misc[0:1, 128:128 + H], AX))
            link(v.scalar_tensor_tensor(out=plog[0:1, 6:7], in0=par[0:1, 2:3], scalar=3.0, in1=plog[0:1, 6:7],
                                        op0=ALU.mult, op1=ALU.add))
            link(v.tensor_scalar(plog[0:1, 7:8], par[0:1, 0:1], -1.0, None, ALU.mult))
            link(v.tensor_tensor(plog[0:1, 7:8], plog[0:1, 7:8], par[0:1, 0:1], ALU.max))
            link(v.tensor_tensor(plog[0:1, 6:7], plog[0:1, 6:7], plog[0:1, 7:8], ALU.add))
            link(v.tensor_scalar(flag[:], plog[0:1, 6:7], SAFE_RANGE, None, ALU.is_le))

            for i in range(4):
                dve.wait_ge(x_in[i], 16)
                with dve.Fori(0, 4) as b:
                    for t in range(TT):
                        tile = (b + 4 * i) * TT + t
                        m = v.bn_stats(stats[:, bass.ds(tile, 1), :], z[:, bass.ds(tile, 1), :])
                    m.then_inc(stats_ok, 1)
            dve.wait_ge(stats_ok, B)
            me, mo, qe, qo = (stats[:, :, k] for k in (1, 4, 2, 5))
            link(v.tensor_tensor(tA[:], me, mo, ALU.add))
            link(v.tensor_scalar(mean[:], tA[:], 0.5, None, ALU.mult))
            link(v.tensor_tensor(tA[:], me, mo, ALU.subtract))
            link(v.tensor_tensor(tA[:], tA[:], tA[:], ALU.mult))
            link(v.tensor_scalar(tA[:], tA[:], 0.25, None, ALU.mult))
            link(v.tensor_tensor(tB[:], qe, qo, ALU.add))
            link(v.scalar_tensor_tensor(out=tB[:], in0=tB[:], scalar=1.0 / D, in1=tA[:], op0=ALU.mult, op1=ALU.add))
            v.tensor_scalar(tB[:], tB[:], 1e-5, None, ALU.add).then_inc(var_ok, 1)
            dve.wait_ge(root_ok, 1)
            link(v.reciprocal(tC[:], rstd[:]))
            link(v.tensor_tensor(tD[:], tC[:], tC[:], ALU.mult))
            link(v.tensor_tensor(tD[:], tD[:], tB[:], ALU.mult))
            link(v.tensor_scalar(tD[:], tD[:], -0.5, 1.5, ALU.mult, ALU.add))
            link(v.tensor_tensor(rstd[:], tC[:], tD[:], ALU.mult))

            def logits_out(b, i):
                dve.wait_ge(lg_full, b * 2 + i + 2)
                v.tensor_tensor(lg[:, bass.ds((b * 2 + i) * TT, TT), :],
                                pv[:, 0:TT * E].rearrange("p (t e) -> p t e", e=E),
                                brr[:].rearrange("p (a e) -> p a e", a=1).to_broadcast([P, TT, E]), ALU.add).then_inc(lg_out, 1)

            with dve.Fori(0, B // 2) as bp:
                for i in range(2):
                    dve.wait_ge(xnT_full, bp * 2 + 1)
                    for t in range(TT):
                        tile = (bp * 2 + i) * TT + t
                        m = v.tensor_scalar(xn[i][:, t, :], z[:, bass.ds(tile, 1), :], mean[:, bass.ds(tile, 1)],
                                            rstd[:, bass.ds(tile, 1)], ALU.subtract, ALU.mult)
                    m.then_inc(xn_ok, 1)
                for i in range(2):
                    logits_out(bp, i)

            def over_t(ap):
                return ap.rearrange("p (t a) -> p t a", a=1).to_broadcast([P, NTOK, E])

            def over_e(ap):
                return ap.rearrange("p (a e) -> p a e", a=1).to_broadcast([P, NTOK, E])

            dve.wait_ge(lg_out, B + 1)
            link(v.tensor_reduce(tA[:], lg[:], AX, ALU.max))
            link(v.tensor_tensor(eq[:], lg[:], over_t(tA[:]), ALU.is_ge))
            link(v.tensor_tensor(eq[:], eq[:], over_e(desc[:]), ALU.mult))
            link(v.tensor_reduce(tA[:], eq[:], AX, ALU.max))
            link(v.tensor_tensor(ohf[:], eq[:], over_t(tA[:]), ALU.is_equal))
            v.tensor_copy(ohb[:], ohf[:]).then_inc(oh_ok, 1)
            dve.wait_ge(rank_full, 2)
            tot = lin[0][:, 0:T].rearrange("p (t e) -> p t e", e=E)
            link(v.tensor_copy(scan[0][:], tot))
            cur, k = 0, 1
            while k < NTOK:
                link(v.tensor_copy(scan[1 - cur][:, 0:k, :], scan[cur][:, 0:k, :]))
                link(v.tensor_tensor(scan[1 - cur][:, k:, :], scan[cur][:, k:, :], scan[cur][:, 0:NTOK - k, :], ALU.add))
                cur, k = 1 - cur, 2 * k
            incl, other = scan[cur], scan[1 - cur]
            link(v.tensor_copy(sm[:, 0, :], incl[:, NTOK - 1, :]))
            link(v.tensor_tensor(eq[:], over_e(sm[:, 0, :]), over_t(j128[:]), ALU.is_gt))
            link(v.tensor_reduce(sm[:, 1, :], eq[:].rearrange("p t e -> p e t"), AX, ALU.add))
            src, k = 1, 1
            while k < E:
                link(v.tensor_copy(sm[:, src + 1, 0:k], sm[:, src, 0:k]))
                link(v.tensor_tensor(sm[:, src + 1, k:], sm[:, src, k:], sm[:, src, 0:E - k], ALU.add))
                src, k = src + 1, 2 * k
            link(v.tensor_tensor(sm[:, 5, :], sm[:, src, :], sm[:, 1, :], ALU.subtract))
            link(v.tensor_scalar(sm[:, 6, :], sm[:, 5, :], float(P), None, ALU.mult))
            link(v.tensor_tensor(incl[:], incl[:], tot, ALU.subtract))
            link(v.tensor_tensor(other[:], misc[:, 0:T].rearrange("p (t e) -> p t e", e=E), incl[:], ALU.add))
            link(v.tensor_tensor(other[:], other[:], over_e(sm[:, 6, :]), ALU.add))
            link(v.tensor_tensor(other[:], other[:], ohf[:], ALU.mult))
            link(v.tensor_reduce(tA[:], other[:], AX, ALU.add))
            link(v.tensor_copy(posu[:], tA[:]))
            link(v.tensor_tensor(cmp[:], slotid[:].rearrange("p (t a) -> p t a", a=1).to_broadcast([P, NSLOT, E]),
                                 sm[:, src, :].rearrange("p (a e) -> p a e", a=1).to_broadcast([P, NSLOT, E]), ALU.is_ge))
            link(v.tensor_reduce(slotid[:], cmp[:], AX, ALU.add))
            link(v.tensor_scalar(etile[:], slotid[:], float(E - 1), None, ALU.min))


PROLOGUE = ["q", "k", "codes", "mixed", "v"]
MERGE_JOBS = [(0, 2, "merge"), (0, 4, "proj")]
ATTN_JOBS = [(0, 0, "q"), (0, 1, "k"), (0, 3, "codes"), (0, 5, "v"), (0, 7, "mixed"), (0, 9, "o0"), (1, 9, "o1"),
             (2, 9, "o2"), (3, 9, "o3")]
W_JOBS = [(1, 1, "w0"), (1, 4, "w1"), (1, 7, "w2"), (2, 1, "w3"), (2, 4, "w4"), (2, 7, "w5"), (3, 2, "w6"), (3, 6, "w7")]
F_JOBS = [(0, 8, "fxA"), (1, 1, "h0A"), (1, 3, "h1A"), (1, 5, "h2A"), (1, 7, "fxB"), (2, 0, "y0A"), (2, 2, "y1A"),
          (2, 4, "y2A"), (2, 5, "h0B"), (2, 7, "h1B"), (3, 0, "h2B"), (3, 3, "y0B"), (3, 5, "y1B"), (3, 7, "y2B")]
KINDS = {
    "first": sorted(ATTN_JOBS + W_JOBS),
    "second": sorted(ATTN_JOBS + MERGE_JOBS + W_JOBS),
    "ffn": sorted(ATTN_JOBS + MERGE_JOBS + F_JOBS),
    "plain": sorted(ATTN_JOBS + MERGE_JOBS),
    "last": sorted([j for j in ATTN_JOBS if j[2] not in PROLOGUE] + MERGE_JOBS),
}
NU = 2 * NC
PV_AT = {2: [0], 4: [1, 3], 6: [2]}
SCATTERS = [4, 8, 10, 10]
RELUS = [(1, 0, "A"), (1, 1, "A"), (1, 2, "A"), (2, 0, "B"), (2, 1, "B"), (3, 2, "B")]
GATHERS = [[0, 3, 7, 7], [7, 7, 7, 7]]
F_FROM, F_TO = 2, 14
assert (F_TO - F_FROM) * 2 * FG == NSLOT
N_RAW_IN, N_LIN_IN = 9, 18


def turn(b, kind, job):
    names = [j[2] for j in KINDS[kind]]
    n = len(PROLOGUE) + names.index(job)
    if kind == "first":
        return n
    n += len(KINDS["first"])
    if kind == "second":
        return n
    n += len(KINDS["second"])
    if kind == "ffn":
        return (b - F_FROM) * len(KINDS["ffn"]) + n
    n += len(KINDS["ffn"]) * (F_TO - F_FROM)
    if kind == "plain":
        return n
    return n + len(KINDS["plain"])


TAIL_TURN = turn(B - 1, "last", KINDS["last"][-1][2]) + 1


def each_batch(eng, body):
    body(0, 0, "first")
    body(1, 1, "second")
    with eng.Fori(0, (F_TO - F_FROM) // 2) as bp:
        body(bp * 2 + F_FROM, 0, "ffn")
        body(bp * 2 + F_FROM + 1, 1, "ffn")
    body(B - 2, 0, "plain")
    body(B - 1, 1, "last")


def following(b, pb, q):
    return (b, pb, q + 1) if q + 1 < NQ else (b + 1, 1 - pb, 0)


def layer(nc, a, out, g):
    z, wqkvT, woT, hexT, mixS, par, ident, S = (g[k] for k in ("z", "wqkvT", "woT", "hexT", "mixS", "par", "ident", "S"))
    QS, LK, V1, raw, lin, pv, misc = (g[k] for k in ("QS", "LK", "V1", "raw", "lin", "pv", "misc"))
    xt_d, qp_d, kp_d, ap_d, hp_d = (g[k] for k in ("xt_d", "qp_d", "kp_d", "ap_d", "hp_d"))
    w1_d, w2_d, xs_d, ys_d = (g[k] for k in ("w1_d", "w2_d", "xs_d", "ys_d"))
    etile, posu, mean, rstd = (g[k] for k in ("etile", "posu", "mean", "rstd"))

    with ExitStack() as ctx:
        def sb(name, shape, dt=F32):
            return ctx.enter_context(nc.sbuf_tensor(name, shape, dt))

        def sem(name):
            return ctx.enter_context(nc.semaphore(name))

        RK = [sb(f"RK{i}", [ROWS, H, T], BF16) for i in range(2)]
        xTr = [sb(f"xTr{i}", [P, T]) for i in range(2)]
        sQ, sK, rest, oT = (sb(n, [P, T]) for n in ("sQ", "sK", "rest", "oT"))
        sA, aT = sQ, oT
        ht = sb("ht", [64, T])
        partsQ, partsK = sb("partsQ", [P, 3, T], BF16), sb("partsK", [P, 3, T], BF16)
        partsA = partsQ
        at = sb("at", [P, TT, D])
        rec = sb("rec", [P, TT, QH])
        w1 = [sb(f"w1_{i}", [P, F + FC]) for i in range(FG)]
        w2 = [sb(f"w2_{i}", [P, F + D]) for i in range(FG)]
        one = sb("one", [P, 1])
        xin = sb("xin", [P, FG, D])
        xsT = sb("xsT", [P, FG, P])
        hid = [sb(f"hid{i}", [P, FC, P]) for i in range(FG)]
        ysb = sb("ysb", [P, FG, D])
        xs = [x[:, i, :] for x in (xin, xsT, ysb, hid[2]) for i in range(FG)]
        NXS = len(xs)

        raw_full, t_done, lin_full, s_done, e_done, m_done = (sem(n) for n in (
            "raw_full", "t_done", "lin_full", "s_done", "e_done", "m_done"))
        pv_done, oT_ok, rec_ok = sem("pv_done"), sem("oT_ok"), sem("rec_ok")
        misc_full, misc_used = sem("misc_full"), sem("misc_used")
        waited, waited_sp, waited_pe, rk_clear = sem("waited"), sem("waited_sp"), sem("waited_pe"), sem("rk_clear")
        split_ok, split_chain = {n: sem(f"split_{n}") for n in "qka"}, sem("split_chain")
        stored, h_stored = {n: sem(f"stored_{n}") for n in "qka"}, sem("h_stored")
        xt_in = [sem(f"xt_in{i}") for i in range(2)]
        raw_in = [sem(f"raw_in{i}") for i in range(2)]
        lin_in = [sem(f"lin_in{i}") for i in range(2)]
        ew_in, ew_out = ([sem(f"{n}{i}") for i in range(2)] for n in ("ew_in", "ew_out"))
        mx_d = g["mx_d"]
        xs_ok, xs_sent, xs_done = sem("xs_ok"), [sem(f"xs_sent{i}") for i in range(NXS)], sem("xs_done")
        relu_ok, hidden_ok = sem("relu_ok"), sem("hidden_ok")
        fx_in, w1_in, w2_in, y_out = sem("fx_in"), [sem(f"w1_in{i}") for i in range(FG)], sem("w2_in"), sem("y_out")
        y_all, yg_in, sum_ok, final_out = sem("y_all"), [sem(f"yg_in{i}") for i in range(NXS)], sem("sum_ok"), sem("final_out")

        def first_after(kind):
            return next(j[2] for j in KINDS[kind] if j[:2] >= (NQ - 2, 6))

        def jobs_at(kind, s, u):
            return [j[2] for j in KINDS[kind] if j[:2] == (s, u)]

        def first_tile(counts, s):
            return sum(counts[:s])

        tmax = sb("tmax", [P, T])
        mx = sb("mx", [P, H * TT])
        mrest = tmax[0:H * TT, 0:P]
        mparts = sb("mparts", [H * TT, NSHIFT, P], BF16)
        hidden = sb("hidden", [P, P], BF16)
        px_full, px_used, px_sum, px_max, px_split, px_out, px_in = (sem(n) for n in (
            "px_full", "px_used", "px_sum", "px_max", "px_split", "px_out", "px_in"))
        NPX = 2 * H * TT + 1
        HT = H * TT

        def general(eng):
            return eng.If(eng.value_load(g["flag"][0:1, 0:1], min_val=0, max_val=1) == 0)

        block = ctx.enter_context(nc.Block())

        @block.tensor
        def _(pe):
            mm = nc.tensor.matmul
            pe.sem_inc(raw_full, 1)
            pe.sem_inc(lin_full, 1)
            pe.sem_inc(pv_done, 1)

            def fill_raw(bf, pf, q, c):
                n = (bf * NQ + q) * NC + c
                if not (isinstance(n, int) and n < 2):
                    pe.wait_ge(t_done, n - 1)
                if q == 0 and c == 0:
                    pe.wait_ge(lin_in[pf], (bf - pf) * (8 * N_LIN_IN) + 16 * N_LIN_IN)
                    pe.wait_ge(raw_in[pf], (bf - pf) * (8 * N_RAW_IN) + 16 * N_RAW_IN)
                for cc, col, j, kt, qs in PARTS:
                    if cc == c:
                        h = q * QH + j
                        m = mm(raw[(q + c) % 2][:, col:col + T - qs], RK[pf][:, h, kt * P:(kt + 1) * P],
                               QS[pf][:, h, qs:T], start=True, stop=True)
                m.then_inc(raw_full, 1)

            def fill_lin(bf, pf, q, u):
                c, half = u // 2, u % 2
                n = (bf * NQ + q) * NU + u
                if not (isinstance(n, int) and n < 2):
                    pe.wait_ge(s_done, n - 1)
                for cc, col, j, kt, qs in PARTS:
                    if cc == c and col // T == half:
                        h = q * QH + j
                        m = mm(lin[half][:, col - half * T:col - half * T + T - qs], LK[pf][:, kt * P:(kt + 1) * P],
                               QS[pf][:, h, qs:T], start=True, stop=True)
                m.then_inc(lin_full, 1)

            def weigh(pb, q, kts):
                for kt in kts:
                    for cc, col, j, k, qs in PARTS:
                        if k == kt:
                            m = mm(pv[j * HP:(j + 1) * HP, qs:T], V1[pb][:, kt, q * QH + j, :],
                                   S[:, q % 2, cc, col:col + T - qs], start=(kt == 0), stop=(kt == 2))
                return m

            def turn_tiles(src, n=TT):
                for t in range(n):
                    m = nc.tensor.transpose(misc[:, t * P:(t + 1) * P], src(t), ident[:])
                return m

            def job(name, n, b, pb):
                if not (isinstance(n, int) and n == 0):
                    pe.wait_ge(misc_used, n)
                bn, pn = b + 1, 1 - pb
                k = (b - F_FROM) * 2 + (1 if name[-1] == "B" else 0)
                if name == "q":
                    pe.wait_ge(xt_in[pn], (bn - pn) * 8 + 16)
                    m = mm(misc[:], wqkvT[:, 0:D], xTr[pn][:], start=True, stop=True)
                elif name == "k":
                    m = mm(misc[:], wqkvT[:, D:2 * D], xTr[pn][:], start=True, stop=True)
                elif name == "codes":
                    m = mm(misc[0:64], hexT[:], xTr[pn][:], start=True, stop=True)
                elif name == "mixed":
                    m = mm(misc[:], mixS[:], ht[:], start=True, stop=True)
                elif name == "v":
                    for t in range(TT):
                        m = mm(misc[:, t * P:(t + 1) * P], xTr[pn][:, t * P:(t + 1) * P], wqkvT[:, 2 * D:3 * D],
                               start=True, stop=True)
                elif name[0] == "o":
                    pe.wait_ge(oT_ok, b * NQ + int(name[1]) + 2)
                    m = turn_tiles(lambda t: oT[:, t * P:(t + 1) * P])
                elif name == "merge":
                    m = turn_tiles(lambda t: at[:, t, :])
                elif name == "proj":
                    for t in range(TT):
                        m = mm(misc[:, t * P:(t + 1) * P], aT[:, t * P:(t + 1) * P], woT[:], start=True, stop=True)
                elif name[0] == "w":
                    i, e = int(name[1]), b * (E // 2) + int(name[1]) // 2
                    if i % 2 == 0:
                        pe.wait_ge(ew_in[e % 2], (e // 2 + 1) * 32)
                    m = turn_tiles(lambda t: (w1, w2)[i % 2][e % 2][:, t * P:(t + 1) * P])
                elif name[:2] == "fx":
                    pe.wait_ge(fx_in, k * 16 + 16)
                    m = turn_tiles(lambda t: xin[:, t, :], FG)
                elif name[0] == "h":
                    i = int(name[1])
                    pe.wait_ge(w1_in[i], k * 16 + 16)
                    for c in range(FC):
                        m = mm(misc[:, c * P:(c + 1) * P], w1[i][:, c * P:(c + 1) * P], xsT[:, i, :], start=True, stop=True)
                elif name[0] == "y":
                    i = int(name[1])
                    pe.wait_ge(w2_in, k * 48 + 48)
                    pe.wait_ge(relu_ok, k * FG + i + 1)
                    for c in range(FC):
                        m = mm(misc[:, 0:P], hid[i][:, c, :], w2[i][:, c * P:(c + 1) * P], start=(c == 0), stop=(c == FC - 1))
                m.then_inc(misc_full, 1)

            def maxima(bn, pn, n):
                pe.wait_ge(lin_in[pn], (bn - pn) * (8 * N_LIN_IN) + 16 * N_LIN_IN)
                pe.wait_ge(raw_in[pn], (bn - pn) * (8 * N_RAW_IN) + 16 * N_RAW_IN)
                pe.wait_ge(misc_used, n)
                pe.sem_inc(waited_pe, 1)
                with pe.Fori(0, H) as h:
                    for qt in range(TT):
                        w, t = (qt + 1) * P, bn * NPX + (h * TT + qt) * 2
                        query = QS[pn][0:SHIFT0, bass.ds(h, 1), qt * P:w].rearrange("r h n -> r (h n)")
                        pe.wait_ge(px_used, t + 1)
                        mm(misc[:, 0:w], query, RK[pn][0:SHIFT0, bass.ds(h, 1), 0:w].rearrange("r h n -> r (h n)"),
                           start=True, stop=True).then_inc(px_full, 1)
                        pe.wait_ge(px_used, t + 2)
                        mm(misc[:, 0:w], query, LK[pn][0:SHIFT0, 0:w], start=True, stop=True).then_inc(px_full, 1)
                pe.wait_ge(px_used, bn * NPX + NPX)
                pe.wait_ge(px_max, (bn + 1) * HT + 1)
                pe.sem_inc(waited_pe, 1)
                nc.tensor.transpose(misc[0:HT, 0:P], mx[:], ident[:]).then_inc(px_full, 1)
                pe.wait_ge(px_used, (bn + 1) * NPX + 1)
                pe.wait_ge(px_in, bn * 16 + 16)

            for n, name in enumerate(PROLOGUE):
                job(name, n, -1, 1)
            with general(pe):
                maxima(0, 0, len(PROLOGUE))
            fill_raw(0, 0, 0, 0)
            fill_raw(0, 0, 0, 1)
            for u in range(NU):
                fill_lin(0, 0, 0, u)
                if u % 2 == 0:
                    fill_raw(0, 0, (u // 2 + 2) // NC, (u // 2 + 2) % NC)
            fill_lin(0, 0, 1, 0)

            def body(b, pb, kind):
                for s in range(NQ):
                    bf, pf, qf = following(b, pb, s)
                    last_front = kind == "last" and s == NQ - 2
                    front = not (kind == "last" and s == NQ - 1)
                    for u in range(NU):
                        c = u // 2
                        if front:
                            if u + 1 < NU:
                                fill_lin(bf, pf, qf, u + 1)
                            elif not last_front:
                                fill_lin(*following(bf, pf, qf), 0)
                            if u % 2 == 0:
                                if c + 2 < NC:
                                    fill_raw(bf, pf, qf, c + 2)
                                elif not last_front:
                                    if s == NQ - 2 and u == 6:
                                        with general(pe):
                                            maxima(b + 1, 1 - pb, turn(b, kind, first_after(kind)))
                                    fill_raw(*following(bf, pf, qf), c + 2 - NC)
                        if u in PV_AT:
                            if u == 2:
                                pe.wait_ge(m_done, (b * NQ + s) * 2 + 1)
                                pe.wait_ge(oT_ok, b * NQ + s + 1)
                            if u == 6:
                                pe.wait_ge(m_done, (b * NQ + s) * 2 + 2)
                            m = weigh(pb, s, PV_AT[u])
                            if u == 6:
                                m.then_inc(pv_done, 1)
                        for name in jobs_at(kind, s, u):
                            job(name, turn(b, kind, name), b, pb)

            each_batch(pe, body)
            job("merge", TAIL_TURN, B - 1, 1)
            job("proj", TAIL_TURN + 1, B - 1, 1)

        @block.scalar
        def _(act):
            def tanh(bf, q, c):
                n = (bf * NQ + q) * NC + c
                act.wait_ge(raw_full, n + 2)
                if c == 0 and not (isinstance(n, int) and n == 0):
                    act.wait_ge(pv_done, bf * NQ + q)
                nc.scalar.activation(S[:, q % 2, c, :], raw[(q + c) % 2][:], ACT.Tanh).then_inc(t_done, 1)

            def exp(bf, q, c0, c1):
                act.wait_ge(s_done, (bf * NQ + q) * (2 * NC) + 2 * c1)
                x = S[:, q % 2, c0:c1, :]
                nc.scalar.activation(x, x, ACT.Exp).then_inc(e_done, 1)

            def codes(n):
                act.wait_ge(misc_full, n + 1)
                nc.scalar.activation(ht[:], misc[0:64], ACT.Tanh).then_inc(misc_used, 1)

            def maxima(bn):
                with act.Fori(0, H) as h:
                    for qt in range(TT):
                        w, i = (qt + 1) * P, h * TT + qt
                        act.wait_ge(px_full, bn * NPX + i * 2 + 1)
                        act.wait_ge(px_max, bn * HT + i + 1)
                        nc.scalar.activation(tmax[:, 0:w], misc[:, 0:w], ACT.Tanh).then_inc(px_used, 1)

            codes(PROLOGUE.index("codes"))
            with general(act):
                maxima(0)
            for c in range(4):
                tanh(0, 0, c)
            exp(0, 0, 0, 2)
            tanh(0, 0, 4)
            exp(0, 0, 2, 4)

            def body(b, pb, kind):
                for s in range(NQ):
                    bf, _, qf = following(b, pb, s)
                    if kind == "last" and s == NQ - 1:
                        exp(b, s, 4, 5)
                        continue
                    tanh(bf, qf, 0)
                    tanh(bf, qf, 1)
                    exp(b, s, 4, 5)
                    tanh(bf, qf, 2)
                    tanh(bf, qf, 3)
                    if s == 0 and kind != "last":
                        codes(turn(b, kind, "codes"))
                    exp(bf, qf, 0, 2)
                    tanh(bf, qf, 4)
                    if s == NQ - 2 and kind != "last":
                        with general(act):
                            maxima(b + 1)
                    exp(bf, qf, 2, 4)

            each_batch(act, body)

        @block.vector
        def _(dve):
            v = nc.vector
            dve.sem_inc(oT_ok, 1)
            for i in range(2):
                v.memset(RK[i][:].bitcast(U32), 0).then_inc(rk_clear, 1)
            v.memset(hidden[:], 0.0).then_inc(hidden_ok, 1)
            v.memset(one[:], 1.0).then_inc(rk_clear, 1)

            def add(bf, q, c, half):
                n = (bf * NQ + q) * NC + c
                if half == 0:
                    dve.wait_ge(t_done, n + 1)
                dve.wait_ge(lin_full, n * 2 + half + 2)
                x = S[:, q % 2, c, half * T:(half + 1) * T]
                v.scalar_tensor_tensor(out=x, in0=x, scalar=par[:, 0:1], in1=lin[half][:], op0=ALU.mult,
                                       op1=ALU.add).then_inc(s_done, 1)

            def take(name, n, b, pb):
                bn, pn = b + 1, 1 - pb
                first = isinstance(b, int) and b < 0
                dve.wait_ge(misc_full, n + 1)
                if name == "q":
                    if not first:
                        dve.wait_ge(split_ok["a"], b + 1)
                    v.tensor_scalar(sQ[:], misc[:], par[:, 1:2], None, ALU.mult).then_inc(misc_used, 1)
                elif name == "k":
                    if not first:
                        dve.wait_ge(split_ok["k"], b + 1)
                    v.tensor_copy(sK[:], misc[:]).then_inc(misc_used, 1)
                elif name == "mixed":
                    dve.wait_ge(split_ok["q"], b + 2)
                    v.tensor_copy(sA[:], misc[:]).then_inc(misc_used, 1)
                elif name == "v":
                    if not first:
                        dve.wait_ge(pv_done, b * NQ + 1)
                    v.tensor_copy(V1[pn][:, :, :, 0:HD], misc[:].rearrange("p (t h d) -> p t h d", t=TT, h=H)).then_inc(misc_used, 1)
                elif name[0] == "o":
                    s = int(name[1])
                    o = misc[:].rearrange("p (t j r) -> p t j r", t=TT, j=QH)
                    v.reciprocal(rec[:], o[:, :, :, HD]).then_inc(rec_ok, 1)
                    dve.wait_ge(rec_ok, b * NQ + s + 1)
                    v.tensor_tensor(at[:, :, s * QH * HD:(s + 1) * QH * HD].rearrange("p t (j d) -> p t j d", j=QH),
                                    o[:, :, :, 0:HD],
                                    rec[:].rearrange("p t (j a) -> p t j a", a=1).to_broadcast([P, TT, QH, HD]),
                                    ALU.mult).then_inc(misc_used, 1)
                elif name == "merge":
                    v.tensor_copy(aT[:], misc[:]).then_inc(misc_used, 1)
                elif name == "proj":
                    bp = b - 1
                    zb = z[:, bass.ds(bp * TT, TT), :]
                    v.tensor_tensor(zb, misc[:].rearrange("p (t d) -> p t d", t=TT), zb, ALU.add).then_inc(misc_used, 1)
                elif name[0] == "w":
                    i = int(name[1])
                    dst = (hid[0], hid[1])[i % 2]
                    j = b * (E // 2) * 2 + i
                    if j >= 2:
                        dve.wait_ge(ew_out[i % 2], j // 2 * 16)
                    v.tensor_copy(dst[:].rearrange("p c n -> p (c n)"), misc[:]).then_inc(misc_used, 1)
                elif name[:2] == "fx":
                    v.tensor_copy(xsT[:], misc[:, 0:FG * P].rearrange("p (i n) -> p i n", i=FG)).then_inc(misc_used, 1)
                elif name[0] == "h":
                    i = int(name[1])
                    v.tensor_tensor(hid[i][:], misc[:].rearrange("p (c n) -> p c n", c=FC),
                                    w1[i][:, F:F + FC].rearrange("p (c a) -> p c a", a=1).to_broadcast([P, FC, P]),
                                    ALU.add).then_inc(misc_used, 1)
                elif name[0] == "y":
                    i, k = int(name[1]), (b - F_FROM) * 2 + (1 if name[-1] == "B" else 0)
                    if i == 0:
                        dve.wait_ge(y_out, k * 16 + 1)
                    v.tensor_tensor(ysb[:, i, :], misc[:, 0:P], w2[i][:, F:F + D], ALU.add).then_inc(misc_used, 1)

            def normalise(tile):
                i = tile % NXS
                if tile >= NXS:
                    dve.wait_ge(xs_sent[i], tile // NXS * 16)
                v.tensor_scalar(xs[i], z[:, tile, :], mean[:, tile:tile + 1], rstd[:, tile:tile + 1],
                                ALU.subtract, ALU.mult).then_inc(xs_ok, 1)

            def add_back(tile):
                i = tile % NXS
                dve.wait_ge(yg_in[i], tile // NXS * 16 + 16)
                v.tensor_tensor(z[:, tile, :], z[:, tile, :], xs[i], ALU.add).then_inc(sum_ok, 1)

            def maxima(bn):
                with dve.Fori(0, H) as h:
                    for qt in range(TT):
                        w, i = (qt + 1) * P, h * TT + qt
                        dve.wait_ge(px_full, bn * NPX + i * 2 + 2)
                        v.scalar_tensor_tensor(out=tmax[:, 0:w], in0=tmax[:, 0:w], scalar=par[:, 0:1], in1=misc[:, 0:w],
                                               op0=ALU.mult, op1=ALU.add).then_inc(px_sum, 1)
                        dve.wait_ge(px_sum, (bn * HT + i) * 2 + 1)
                        v.tensor_tensor(tmax[:, w - P:w], tmax[:, w - P:w], hidden[:], ALU.add).then_inc(px_sum, 1)
                        dve.wait_ge(px_sum, (bn * HT + i) * 2 + 2)
                        v.tensor_reduce(mx[:, bass.ds(i, 1)], tmax[:, 0:w], AX, ALU.max, negate=True).then_inc(px_max, 1)
                        dve.sem_inc(px_used, 1)
                dve.wait_ge(px_full, (bn + 1) * NPX)
                m, link = misc[0:HT, 0:P], Link(dve, px_split, bn * 4)
                link(v.tensor_copy(mparts[:, 0, :], m))
                link(v.tensor_tensor(mrest, m, mparts[:, 0, :], ALU.subtract))
                link(v.tensor_copy(mparts[:, 1, :], mrest))
                link(v.tensor_tensor(mparts[:, 2, :], mrest, mparts[:, 1, :], ALU.subtract))
                dve.sem_inc(px_used, 1)

            dve.sem_inc(px_used, 1)
            dve.sem_inc(px_max, 1)
            for n, name in enumerate(PROLOGUE):
                if name != "codes":
                    take(name, n, -1, 1)
            dve.wait_ge(hidden_ok, 2)
            with general(dve):
                maxima(0)
            for u in range(NU):
                add(0, 0, u // 2, u % 2)

            def body(b, pb, kind):
                pending = []
                if kind != "first":
                    pending = [("o3", turn(b, kind, KINDS[kind][0][2]) - 1, b - 1, 1 - pb)]
                for s in range(NQ):
                    bf, _, qf = following(b, pb, s)
                    front = not (kind == "last" and s == NQ - 1)
                    tiles = []
                    if kind in ("first", "second"):
                        t0 = b * (NTOK // 2) + first_tile(SCATTERS, s)
                        tiles = range(t0, t0 + SCATTERS[s])
                    if kind in ("plain", "last"):
                        counts, n = GATHERS[0] + GATHERS[1], (b - B + 2) * NQ + s
                        tiles = range(first_tile(counts, max(n - 1, 0)), first_tile(counts, n))
                    for u in range(NU):
                        if u == 8:
                            dve.wait_ge(pv_done, b * NQ + s + 2)
                            v.tensor_copy(oT[:], pv[:]).then_inc(oT_ok, 1)
                        if front:
                            add(bf, qf, u // 2, u % 2)
                        if s == NQ - 2 and u == 7 and kind != "last":
                            with general(dve):
                                maxima(b + 1)
                        for p in pending:
                            take(*p)
                        pending = [(name, turn(b, kind, name), b, pb) for name in jobs_at(kind, s, u) if name != "codes"]
                        if u < len(tiles):
                            (normalise if kind in ("first", "second") else add_back)(tiles[u])

            each_batch(dve, body)
            take("o3", TAIL_TURN - 1, B - 1, 1)
            take("merge", TAIL_TURN, B - 1, 1)
            take("proj", TAIL_TURN + 1, B, 0)
            for tile in range(sum(GATHERS[0] + GATHERS[1][:-1]), NTOK):
                add_back(tile)

        @block.gpsimd
        def _(pool):
            gp = nc.gpsimd
            ones_t = one[:].to_broadcast([P, T])
            pool.wait_ge(rk_clear, 3)
            pool.wait_ge(hidden_ok, 1)
            gp.affine_select(out=hidden[:], in_=hidden[:], compare_op=ALU.is_ge, fill=-3e38, base=0, pattern=[[-1, P]],
                             channel_multiplier=1).then_inc(hidden_ok, 1)

            def mask(b, s, first):
                Sq = S[:, s % 2]
                pool.wait_ge(e_done, (b * NQ + s) * 3 + (2 if first else 3))
                pool.sem_inc(waited, 1)
                if first:
                    x = Sq[:, 0:QH, 0:P]
                    gp.affine_select(out=x, in_=x, compare_op=ALU.is_ge, fill=0.0, base=0, pattern=[[0, QH], [1, P]],
                                     channel_multiplier=-1)
                    x = Sq[:, 0:QH, T:T + 2 * P].rearrange("p c (k n) -> p c k n", k=2)
                    gp.affine_select(out=x, in_=x, compare_op=ALU.is_ge, fill=0.0, base=0, pattern=[[0, QH], [0, 2], [1, P]],
                                     channel_multiplier=-1).then_inc(m_done, 1)
                else:
                    x = Sq[:, QH].rearrange("p (j n) -> p j n", j=QH)[:, :, 0:P]
                    gp.affine_select(out=x, in_=x, compare_op=ALU.is_ge, fill=0.0, base=0, pattern=[[0, QH], [1, P]],
                                     channel_multiplier=-1).then_inc(m_done, 1)

            def split(n, bn, k):
                src, r, pt = {"q": sQ, "k": sK, "a": sA}[n][:], rest[:], {"q": partsQ, "k": partsK, "a": partsA}[n]
                link = Link(pool, split_chain, (bn * 3 + "qka".index(n)) * 3)
                pool.wait_ge(misc_used, k + 1)
                if n == "a":
                    pool.wait_ge(stored["q"], bn * 16 + 16)
                elif not (isinstance(bn, int) and bn == 0):
                    if n == "k":
                        pool.wait_ge(stored["k"], bn * 16)
                    else:
                        pool.wait_ge(stored["a"], bn * 16)
                        pool.wait_ge(h_stored, bn * 32)
                link(gp.tensor_tensor(pt[:, 0, :], src, ones_t, ALU.mult))
                link(gp.tensor_tensor(r, src, pt[:, 0, :], ALU.subtract))
                link(gp.tensor_tensor(pt[:, 1, :], r, ones_t, ALU.mult))
                gp.tensor_tensor(pt[:, 2, :], r, pt[:, 1, :], ALU.subtract).then_inc(split_ok[n], 1)
                pool.wait_ge(split_ok[n], bn + 1)

            def scatter(tile):
                pool.wait_ge(xs_ok, tile + 1)
                gp.indirect_dma_start(out=xs_d, out_offset=bass.IndirectOffsetOnAxis(ap=posu[:, tile:tile + 1], axis=0),
                                      in_=xs[tile % NXS], in_offset=None).then_inc(xs_sent[tile % NXS], 16)

            def gather(tile):
                if tile >= NXS:
                    pool.wait_ge(sum_ok, tile - NXS + 1)
                gp.indirect_dma_start(out=xs[tile % NXS], out_offset=None, in_=ys_d,
                                      in_offset=bass.IndirectOffsetOnAxis(ap=posu[:, tile:tile + 1], axis=0)).then_inc(yg_in[tile % NXS], 16)

            def relu(k, i, n):
                pool.wait_ge(misc_used, n + 1)
                pool.sem_inc(waited, 1)
                gp.tensor_scalar(hid[i][:], hid[i][:], 0.0, None, ALU.max).then_inc(relu_ok, 1)

            for n, name in (("q", "q"), ("k", "k"), ("a", "mixed")):
                split(n, 0, PROLOGUE.index(name))

            def body(b, pb, kind):
                for s in range(NQ):
                    mask(b, s, True)
                    mask(b, s, False)
                    for at_s, n, name in ((0, "q", "q"), (0, "k", "k"), (1, "a", "mixed")):
                        if s == at_s and kind != "last":
                            split(n, b + 1, turn(b, kind, name))
                    if kind in ("first", "second"):
                        for i in range(SCATTERS[s]):
                            scatter(b * (NTOK // 2) + first_tile(SCATTERS, s) + i)
                    if kind == "ffn":
                        for at_s, i, group in RELUS:
                            if s == at_s:
                                relu((b - F_FROM) * 2 + "AB".index(group), i, turn(b, kind, f"h{i}{group}"))
                    if kind in ("plain", "last"):
                        if kind == "plain" and s == 1:
                            pool.wait_ge(y_all, 1)
                        n = (b - B + 2) * NQ + s
                        for i in range(GATHERS[b - B + 2][s]):
                            gather(first_tile(GATHERS[0] + GATHERS[1], n) + i)
                if kind == "second":
                    for i in range(NXS):
                        pool.wait_ge(xs_sent[i], (NTOK - i + NXS - 1) // NXS * 16)
                    pool.sem_inc(xs_done, 1)

            each_batch(pool, body)
            for tile in range(sum(GATHERS[0] + GATHERS[1]), NTOK):
                gather(tile)

        @block.sync
        def _(sp):
            sp.sem_inc(y_out, 1)

            def load_x(b, pb):
                src = xt_d[b] if isinstance(b, int) else xt_d[bass.ds(b, 1)].rearrange("b p n -> p (b n)")
                sp.dma_start(xTr[pb][:], src).then_inc(xt_in[pb], 16)

            def stack_q(bn, pn):
                sp.wait_ge(split_ok["q"], bn + 1)
                sp.dma_start(qp_d[pn].rearrange("t r n -> r t n"), partsQ[:]).then_inc(stored["q"], 16)
                sp.wait_ge(stored["q"], bn * 16 + 16)
                if not (isinstance(bn, int) and bn == 0):
                    sp.wait_ge(raw_full, (bn - 1) * (NQ * NC) + 1)
                    sp.wait_ge(lin_full, (bn - 1) * (NQ * NC * 2) + 1)
                for t in range(NTERM):
                    sp.dma_start(QS[pn][t * HD:(t + 1) * HD].rearrange("d h n -> d (h n)"),
                                 qp_d[pn, QPART[t]].rearrange("(d h) n -> d (h n)", h=H)).then_inc(raw_in[pn], 16)

            def stack_k(bn, pn):
                sp.wait_ge(split_ok["k"], bn + 1)
                sp.dma_start(kp_d[pn].rearrange("t r n -> r t n"), partsK[:]).then_inc(stored["k"], 16)
                sp.wait_ge(stored["k"], bn * 16 + 16)
                for r0, k in ((0, 3), (3, 2), (5, 1)):
                    sp.dma_start(RK[pn][r0 * HD:(r0 + k) * HD].rearrange("d h n -> d (h n)"),
                                 kp_d[pn, 0:k].rearrange("t (d h) n -> (t d) (h n)", h=H)).then_inc(raw_in[pn], 16)

            def stack_a(bn, pn):
                sp.wait_ge(split_ok["a"], bn + 1)
                for kind in range(2):
                    r0 = HAM0 + (1 + kind) * NE6
                    sp.dma_start(hp_d[pn, kind].rearrange("t e n -> e t n"), partsA[r0:r0 + NE6]).then_inc(h_stored, 16)
                sp.dma_start(ap_d[pn, :, 0:HAM0 + NE6].rearrange("t r n -> r t n"), partsA[0:HAM0 + NE6]).then_inc(stored["a"], 16)
                sp.wait_ge(h_stored, bn * 32 + 32)
                for kind in range(2):
                    for r0, k in ((0, 3), (3, 2), (5, 1)):
                        row = RK_ROWS + (kind * NTERM + r0) * NE6
                        sp.dma_start(LK[pn][row:row + k * NE6, :],
                                     hp_d[pn, kind, 0:k].rearrange("t e n -> (t e) n")).then_inc(lin_in[pn], 16)
                sp.wait_ge(stored["a"], bn * 16 + 16)
                for t in range(NTERM):
                    row = RK_ROWS + t * NE6
                    sp.dma_start(QS[pn][row:row + NE6].rearrange("e h n -> e (h n)"),
                                 ap_d[pn, QPART[t], 0:HAM0].rearrange("(e h) n -> e (h n)", h=H)).then_inc(lin_in[pn], 16)
                    row = RK_ROWS + (NTERM + t) * NE6
                    sp.dma_start(QS[pn][row:row + NE6],
                                 ap_d[pn, QPART[t], HAM0:HAM0 + NE6].rearrange("e (a n) -> e a n", a=1).to_broadcast([NE6, H, T])).then_inc(lin_in[pn], 16)

            def load_experts(e):
                if e >= 2:
                    n = e - 2
                    kind, b = ("first", 0) if n < E // 2 else ("second", 1)
                    sp.wait_ge(misc_full, turn(b, kind, f"w{n % (E // 2) * 2 + 1}") + 1)
                sp.dma_start(w1[e % 2][:, 0:F].rearrange("p (c d) -> p c d", c=FC),
                             a["L0_ffn_W1"][e].rearrange("(c p) d -> p c d", p=P)).then_inc(ew_in[e % 2], 16)
                sp.dma_start(w2[e % 2][:, 0:F], a["L0_ffn_W2"][e]).then_inc(ew_in[e % 2], 16)

            def store_expert(b, kind, i):
                e = b * (E // 2) + i // 2
                sp.wait_ge(misc_used, turn(b, kind, f"w{i}") + 1)
                if i % 2 == 0:
                    sp.dma_start(w1_d[e, :, 0:F], hid[0][:].rearrange("p c n -> p (c n)")).then_inc(ew_out[0], 16)
                else:
                    sp.dma_start(w2_d[e, :, 0:F], hid[1][:].rearrange("p c n -> p (c n)")).then_inc(ew_out[1], 16)

            def expert(s):
                sp.sem_inc(waited_sp, 1)
                return sp.value_load(etile[0:1, bass.ds(s, 1)], min_val=0, max_val=E - 1)

            def load_rows(k, before):
                sp.wait_ge(misc_full, before("fx") + 1)
                sp.dma_start(xin[:], xs_d[bass.ds(k * (FG * P), FG * P), :].rearrange("(i p) d -> p i d", p=P)).then_inc(fx_in, 16)

            def load_w1(k, i, before):
                sp.wait_ge(misc_used, before(f"h{i}") + 1)
                e = expert(k * FG + i)
                sp.dma_start(w1[i][:], w1_d[bass.ds(e, 1)].rearrange("e p f -> p (e f)")).then_inc(w1_in[i], 16)

            def load_w2(k, i, before):
                sp.wait_ge(misc_used, before(f"y{i}") + 1)
                e = expert(k * FG + i)
                sp.dma_start(w2[i][:], w2_d[bass.ds(e, 1)].rearrange("e p f -> p (e f)")).then_inc(w2_in, 16)

            def store_rows(k, n):
                sp.wait_ge(misc_used, n + 1)
                sp.dma_start(ys_d[bass.ds(k * (FG * P), FG * P), :].rearrange("(i p) d -> p i d", p=P), ysb[:]).then_inc(y_out, 16)

            def shift(bn, pn):
                sp.wait_ge(px_split, bn * 4 + 4)
                sp.dma_start(mx_d[pn].rearrange("t (r n) -> r t n", n=P), mparts[:]).then_inc(px_out, 16)
                sp.wait_ge(px_out, bn * 16 + 16)
                sp.dma_start(QS[pn][SHIFT0:ROWS].rearrange("r h n -> r (h n)"), mx_d[pn]).then_inc(px_in, 16)

            load_x(0, 0)
            load_x(1, 1)
            load_experts(0)
            load_experts(1)
            sp.wait_ge(rk_clear, 3)
            stack_q(0, 0)
            stack_k(0, 0)
            stack_a(0, 0)
            with general(sp):
                shift(0, 0)

            def body(b, pb, kind):
                bn, pn = b + 1, 1 - pb
                k = (b - F_FROM) * 2 if kind == "ffn" else None
                if kind in ("first", "second"):
                    stack_q(bn, pn)
                    stack_k(bn, pn)
                    for i in range(E):
                        store_expert(b, kind, i)
                        if i % 2 == 1:
                            e = b * (E // 2) + i // 2 + 2
                            if e < E:
                                load_experts(e)
                        if i == 2:
                            stack_a(bn, pn)
                            with general(sp):
                                shift(bn, pn)
                    if kind == "second":
                        sp.wait_ge(xs_done, 1)
                        for i in range(2):
                            sp.wait_ge(ew_out[i], E * 16)
                if kind == "ffn":
                    prior = lambda j: turn(b - 1, kind, j + "B")
                    load_rows(k, prior)
                    for i in range(FG):
                        load_w1(k, i, prior)
                    for i in range(FG):
                        load_w2(k, i, prior)
                    stack_q(bn, pn)
                    stack_k(bn, pn)
                    own = lambda j: turn(b, kind, j + "A")
                    load_rows(k + 1, own)
                    for i in range(FG):
                        load_w1(k + 1, i, own)
                    stack_a(bn, pn)
                    with general(sp):
                        shift(bn, pn)
                    for i in range(FG):
                        load_w2(k + 1, i, own)
                    store_rows(k, turn(b, kind, "y2A"))
                    store_rows(k + 1, turn(b, kind, "y2B"))
                if kind == "plain":
                    sp.wait_ge(y_out, NSLOT // FG * 16 + 1)
                    sp.sem_inc(y_all, 1)
                    stack_q(bn, pn)
                    stack_k(bn, pn)
                    stack_a(bn, pn)
                    with general(sp):
                        shift(bn, pn)
                if kind in ("first", "second", "ffn"):
                    sp.wait_ge(misc_full, turn(b, kind, "o3"))
                    load_x(b + 2, pb)

            each_batch(sp, body)

            def store_out(b):
                sp.wait_ge(sum_ok, (b + 1) * TT)
                if b == B - 1:
                    sp.wait_ge(misc_used, TAIL_TURN + 2)
                sp.dma_start(out[b].rearrange("(t p) d -> p t d", p=P), z[:, b * TT:(b + 1) * TT, :]).then_inc(final_out, 16)

            for b in range(B):
                store_out(b)
            sp.wait_ge(final_out, 16 * B)


_OUTS = [((16, 512, 128), 'float32')]
def kernel(**inputs):
    import numpy as _np
    import concourse.bacc as _bacc
    from concourse import mybir as _mybir
    from concourse.bass_utils import run_bass_kernel_spmd as _run
    nc = _bacc.Bacc("TRN2", target_bir_lowering=False, num_devices=1)
    arrays, args = {}, {}
    for name in inputs:
        a = _np.ascontiguousarray(inputs[name])
        arrays[f"in_{name}_dram"] = a
        args[name] = nc.dram_tensor(f"in_{name}_dram", a.shape, _mybir.dt.from_np(a.dtype), kind="ExternalInput").ap()
    out = nc.dram_tensor("out_0_dram", (16, 512, 128), _mybir.dt.float32, kind="ExternalOutput").ap()
    build(nc, args, out)
    r = _run(nc, [arrays], core_ids=[0])
    return r.results[0]["out_0_dram"]
```

```python
from contextlib import ExitStack

import concourse.bass as bass
from concourse import mybir

F32 = mybir.dt.float32
BF16 = mybir.dt.bfloat16
I32 = mybir.dt.int32
U32 = mybir.dt.uint32
ALU = mybir.AluOpType
ACT = mybir.ActivationFunctionType
AX = mybir.AxisListType.X

P = 128
B, T, D = 16, 512, 128
H, HD = 16, 8
NT, NE6 = 7, 6
E, F = 8, 512
TT = T // P
NTOK = B * TT
FC = F // P
NSLOT = 72
FG = 3
HP = 32
QH = 4
NQ = H // QH
CH = 2 * T
NC = 5
NTERM = 6
QPART = (0, 0, 0, 1, 1, 2)
RK_ROWS = NTERM * HD
LK_ROWS = 2 * NTERM * NE6
NSHIFT = 3
SHIFT0 = RK_ROWS + LK_ROWS
ROWS = SHIFT0 + NSHIFT
HEX0 = 32
HAM0 = H * NE6
NA = HAM0 + 3 * NE6
SAFE_RANGE = 40.0


def chunk_parts():
    parts = []
    for j in range(QH):
        parts.append((j, 0, j, 0, 0))
        parts.append((j, T, j, 3, 3 * P))
        parts.append((j, T + P, j, 1, P))
        parts.append((QH, j * 2 * P, j, 2, 2 * P))
    return parts


PARTS = chunk_parts()


def build(nc, a, out):
    x_d = a["L0_attn_x"]
    with ExitStack() as ctx:
        def sb(name, shape, dt=F32):
            return ctx.enter_context(nc.sbuf_tensor(name, shape, dt))

        def sem(name):
            return ctx.enter_context(nc.semaphore(name))

        w1_d = nc.dram_tensor("w1_transposed_b1", [E, P, F + FC], F32, kind="Internal").ap()
        w2_d = nc.dram_tensor("w2_transposed_b2", [E, P, F + D], F32, kind="Internal").ap()
        mx_d = nc.dram_tensor("shift_parts", [2, NSHIFT, H * T], BF16, kind="Internal").ap()
        xt_d = nc.dram_tensor("xn_transposed", [B, P, T], F32, kind="Internal").ap()
        xs_d = nc.dram_tensor("x_sorted", [NSLOT * P, D], F32, kind="Internal").ap()
        ys_d = nc.dram_tensor("y_sorted", [NSLOT * P, D], F32, kind="Internal").ap()
        m_d = nc.dram_tensor("mix", [H, NE6 * NE6], F32, kind="Internal").ap()
        qp_d = nc.dram_tensor("q_parts", [2, 3, P, T], BF16, kind="Internal").ap()
        kp_d = nc.dram_tensor("k_parts", [2, 3, P, T], BF16, kind="Internal").ap()
        ap_d = nc.dram_tensor("a_parts", [2, 3, P, T], BF16, kind="Internal").ap()
        hp_d = nc.dram_tensor("h_parts", [2, 2, 3, NE6, T], BF16, kind="Internal").ap()

        ident = sb("ident", [P, P])
        z = sb("z", [P, NTOK, D])
        wqkvT = sb("wqkvT", [P, 3 * D])
        woT = sb("woT", [P, D])
        hexT = sb("hexT", [P, 64])
        mixS = sb("mixS", [64, P])
        par = sb("par", [P, 8])
        posu = sb("posu", [P, NTOK], U32)
        etile = sb("etile", [P, NSLOT], I32)
        flag = sb("flag", [1, 1], I32)
        mean = sb("mean", [P, NTOK])
        rstd = sb("rstd", [P, NTOK])
        S = sb("S", [P, 2, NC, CH])
        QS = [sb(f"QS{i}", [ROWS, H, T], BF16) for i in range(2)]
        LK = [sb(f"LK{i}", [ROWS, T], BF16) for i in range(2)]
        V1 = [sb(f"V1_{i}", [P, TT, H, HP]) for i in range(2)]

        raw = [ctx.enter_context(nc.psum_tensor(f"raw{i}", [P, CH], F32)) for i in range(2)]
        lin = [ctx.enter_context(nc.psum_tensor(f"lin{i}", [P, T], F32)) for i in range(2)]
        pv = ctx.enter_context(nc.psum_tensor("pv", [P, T], F32))
        misc = ctx.enter_context(nc.psum_tensor("misc", [P, T], F32))

        setup(nc, a, out, locals())
        layer(nc, a, out, locals())


def router_scratch(S):
    room, used, views = S[:, 1].rearrange("p c n -> p (c n)"), 0, {}
    for name, shape, dt in (("lg", (NTOK, E), F32), ("eq", (NTOK, E), F32), ("ohf", (NTOK, E), F32), ("scan0", (NTOK, E), F32),
                            ("scan1", (NTOK, E), F32), ("rank", (NTOK, E), F32), ("tot", (NTOK, E), F32),
                            ("cmp", (NSLOT, E), F32), ("sm", (8, E), F32), ("tA", (NTOK,), F32), ("desc", (E,), F32),
                            ("j128", (NTOK,), F32), ("slotid", (NSLOT,), F32), ("ohb", (NTOK, E), BF16),
                            ("tri", (P,), BF16), ("onesb", (P,), BF16)):
        words = (shape[0] * shape[1] if len(shape) == 2 else shape[0]) // (2 if dt == BF16 else 1)
        x = room[:, used:used + words]
        if dt == BF16:
            x = x.bitcast(BF16)
        views[name] = x.rearrange("p (t e) -> p t e", e=shape[1]) if len(shape) == 2 else x
        used += words
    assert used <= NC * CH
    return views


class Link:

    def __init__(self, eng, sem, base=0):
        self.eng, self.sem, self.n = eng, sem, base

    def __call__(self, ins):
        self.n = self.n + 1
        ins.then_inc(self.sem, 1)
        self.eng.wait_ge(self.sem, self.n)


def setup(nc, a, out, g):
    ident, z, wqkvT, woT, hexT, mixS, par = (g[k] for k in ("ident", "z", "wqkvT", "woT", "hexT", "mixS", "par"))
    posu, etile, flag, mean, rstd, S, V1 = (g[k] for k in ("posu", "etile", "flag", "mean", "rstd", "S", "V1"))
    QS, LK, raw, lin, pv, misc = (g[k] for k in ("QS", "LK", "raw", "lin", "pv", "misc"))
    w1_d, w2_d, xt_d, xs_d, m_d, x_d = (g[k] for k in ("w1_d", "w2_d", "xt_d", "xs_d", "m_d", "x_d"))
    NCLEAR = 4
    SX = NSLOT * D // NCLEAR
    with ExitStack() as ctx:
        def sb(name, shape, dt=F32):
            return ctx.enter_context(nc.sbuf_tensor(name, shape, dt))

        def sem(name):
            return ctx.enter_context(nc.semaphore(name))

        small_in, x_in, w_in = sem("small_in"), [sem(f"x_in{i}") for i in range(4)], sem("w_in")
        const_ok, cleared, zeros_ok = sem("const_ok"), sem("cleared"), sem("zeros_ok")
        pe_small, small_out, dve_chain, pool_chain = sem("pe_small"), sem("small_out"), sem("dve_chain"), sem("pool_chain")
        b1_ok, b1_out, b2_out = sem("b1_ok"), sem("b1_out"), sem("b2_out")
        var_ok, root_ok, xn_ok, xnT_full, xnT_ok, lg_full, lg_out, xt_out = (sem(n) for n in (
            "var_ok", "root_ok", "xn_ok", "xnT_full", "xnT_ok", "lg_full", "lg_out", "xt_out"))
        stats_ok = sem("stats_ok")
        mix_exp_in, mix_exp, sig_exp, mix_sb, mix_out, mix_in, ones_in = (sem(n) for n in (
            "mix_exp_in", "mix_exp", "sig_exp", "mix_sb", "mix_out", "mix_in", "ones_in"))

        wqkv = sb("wqkv", [P, 3, D])
        wo = sb("wo", [P, D])
        hx = sb("hx", [64, D])
        wr = sb("wr", [E, D])
        wrT = sb("wrT", [P, E])
        brr = sb("brr", [P, E])
        b1 = sb("b1", [E * FC, P])
        b1T = sb("b1T", [P, E * FC])
        b2r = sb("b2r", [P, E, D])
        tw = sb("tw", [H, NT])
        twT = sb("twT", [NT, H])
        tr = sb("tr", [NT, NE6 * NE6])
        st16 = sb("st16", [H, 8])
        mix = sb("mix_sb_t", [H, NE6 * NE6])
        plog = sb("plog", [P, 8])
        stats = sb("stats", [P, NTOK, 6])
        tA, tB, tC, tD = (sb(f"norm_{n}", [P, NTOK]) for n in ("mean_sq", "var", "root", "newton"))
        xn = [sb(f"xn{i}", [P, TT, D]) for i in range(2)]
        xT = [sb(f"xT{i}", [P, T]) for i in range(2)]
        scratch = router_scratch(S)
        lg, desc, j128, slotid, tri, onesb = (scratch[n] for n in ("lg", "desc", "j128", "slotid", "tri", "onesb"))
        onesrow = sb("onesrow", [NSHIFT, T], BF16)
        zeros = S[:, 0].rearrange("p c n -> p (c n)")[:, 0:SX]

        block = ctx.enter_context(nc.Block())

        @block.sync
        def _(sp):
            sp.sem_inc(xt_out, 1)
            def load_tokens(i):
                q = NTOK // 4
                sp.dma_start(z[:, i * q:(i + 1) * q, :],
                             x_d[4 * i:4 * i + 4].rearrange("b (t p) d -> p (b t) d", p=P)).then_inc(x_in[i], 16)

            load_tokens(0)
            sp.dma_start(wqkv[:], a["L0_attn_qkv_w"].rearrange("(c p) d -> p c d", p=P)).then_inc(w_in, 16)
            sp.dma_start(wo[:], a["L0_attn_out_w"]).then_inc(w_in, 16)
            load_tokens(1)
            sp.wait_ge(zeros_ok, 1)
            sp.dma_start(hx[0:NE6], a["L0_attn_hex_w"]).then_inc(w_in, 16)
            sp.dma_start(hx[HEX0:HEX0 + NE6], a["L0_attn_q6_w"]).then_inc(w_in, 16)
            sp.dma_start(wr[:], a["L0_ffn_Wr"]).then_inc(w_in, 16)
            sp.dma_start(b1[:], a["L0_ffn_b1"].rearrange("e (c p) -> (e c) p", p=P)).then_inc(w_in, 16)
            load_tokens(2)
            load_tokens(3)
            sp.wait_ge(b1_ok, 1)
            sp.dma_start(w1_d[:, :, F:F + FC].rearrange("e p c -> p e c"), b1T[:].rearrange("p (e c) -> p e c", c=FC)).then_inc(b1_out, 16)
            with sp.Fori(0, B // 2) as bp:
                for i in range(2):
                    sp.wait_ge(xnT_ok, bp * 2 + i + 2)
                    sp.dma_start(xt_d[bass.ds(bp * 2 + i, 1)].rearrange("b p n -> p (b n)"), xT[i][:]).then_inc(xt_out, 16)
            sp.wait_ge(mix_in, 16)
            sp.wait_ge(xt_out, 16 * B + 1)
            sp.wait_ge(b1_out, 16)
            sp.wait_ge(b2_out, 16)

        @block.scalar
        def _(act):
            act.sem_inc(xnT_ok, 1)
            for k, (dst, src) in enumerate((
                (par[:, 0:1], a["L0_attn_sips_alpha"].rearrange("(a n) -> a n", a=1).to_broadcast([P, 1])),
                (plog[:, 0:1], a["L0_attn_sips_beta"].rearrange("(a n) -> a n", a=1).to_broadcast([P, 1])),
                (plog[:, 1:2], bass.AP(a["L0_attn_hamming_lambda_logit"].tensor, 0, [[0, P], [1, 1]])),
                (plog[:, 2:3], bass.AP(a["L0_attn_scale_logit"].tensor, 0, [[0, P], [1, 1]])),
                (brr[:], a["L0_ffn_br"].rearrange("(a n) -> a n", a=1).to_broadcast([P, E])),
                (b2r[:], bass.AP(a["L0_ffn_b2"].tensor, 0, [[0, P], [D, E], [1, D]])),
                (tw[:], a["L0_attn_transform_weights"]),
                (tr[:], a["L0_attn_transforms"].rearrange("t d e -> t (d e)")),
            )):
                act.dma_start(dst, src).then_inc(small_in, 16)
            act.wait_ge(zeros_ok, 1)
            for i in range(2):
                act.dma_start(LK[i][SHIFT0:ROWS, :], onesrow[:]).then_inc(ones_in, 16)
            act.wait_ge(mix_exp_in, 1)
            nc.scalar.activation(st16[:, 0:NT], tw[:], ACT.Exp, bias=st16[:, 7:8], scale=2.0).then_inc(mix_exp, 1)
            nc.scalar.activation(plog[:, 4:6], plog[:, 1:3], ACT.Exp, scale=-1.0).then_inc(sig_exp, 1)
            act.wait_ge(mix_sb, 1)
            act.dma_start(g["m_d"], mix[:]).then_inc(mix_out, 16)
            act.wait_ge(mix_out, 16)
            act.dma_start(mixS[HEX0:HEX0 + NE6, 0:H * NE6].rearrange("d (e h) -> d e h", h=H),
                          g["m_d"].rearrange("h (d e) -> d e h", e=NE6), allow_slow_non_contiguous=True).then_inc(mix_in, 16)
            act.wait_ge(small_in, 16 * 8)
            act.dma_start(w2_d[:, :, F:F + D].rearrange("e p d -> p e d"), b2r[:]).then_inc(b2_out, 16)

            def root(half):
                act.wait_ge(var_ok, half + 1)
                cols = slice(half * NTOK // 2, (half + 1) * NTOK // 2)
                nc.scalar.activation(rstd[:, cols], tB[:, cols], ACT.Sqrt).then_inc(root_ok, 1)

            def turned(bp):
                for i in range(2):
                    act.wait_ge(xnT_full, bp * 2 + i + 2)
                    act.wait_ge(xt_out, bp * 32 + 1)
                    act.wait_ge(lg_full, bp * 2 + 1)
                    nc.scalar.copy(xT[i][:], lin[i][:]).then_inc(xnT_ok, 1)

            root(0)
            for i in range(NCLEAR):
                act.dma_start(xs_d.rearrange("(p r) d -> p (r d)", p=P)[:, i * SX:(i + 1) * SX], zeros).then_inc(cleared, 16)
            with act.Fori(0, B // 4) as bp:
                turned(bp)
            root(1)
            with act.Fori(0, B // 4) as bp:
                turned(bp + B // 4)
            act.wait_ge(ones_in, 32)
            act.wait_ge(cleared, 16 * NCLEAR)

        @block.gpsimd
        def _(pool):
            link = Link(pool, pool_chain)
            link(nc.gpsimd.memset(hx[:], 0.0))
            link(nc.gpsimd.memset(zeros, 0.0))
            for i in range(2):
                link(nc.gpsimd.memset(LK[i][:], 0.0))
            nc.gpsimd.memset(onesrow[:], 1.0).then_inc(zeros_ok, 1)
            link(nc.gpsimd.memset(ident[:], 0.0))
            link(nc.gpsimd.affine_select(out=ident[:], in_=ident[:], compare_op=ALU.not_equal, fill=1.0, base=0,
                                         pattern=[[-1, P]], channel_multiplier=1))
            link(nc.gpsimd.memset(onesb[:], 1.0))
            link(nc.gpsimd.affine_select(out=tri[:], in_=onesb[:], compare_op=ALU.is_gt, fill=0.0, base=0,
                                         pattern=[[1, P]], channel_multiplier=-1))
            link(nc.gpsimd.iota(j128[:], pattern=[[P, NTOK]], base=0, channel_multiplier=0, allow_small_or_imprecise_dtypes=True))
            link(nc.gpsimd.iota(slotid[:], pattern=[[1, NSLOT]], base=0, channel_multiplier=0, allow_small_or_imprecise_dtypes=True))
            nc.gpsimd.iota(desc[:], pattern=[[-1, E]], base=E, channel_multiplier=0,
                           allow_small_or_imprecise_dtypes=True).then_inc(const_ok, 1)
            for i in range(2):
                link(nc.gpsimd.memset(V1[i][:], 0.0))
                link(nc.gpsimd.memset(V1[i][:, :, :, HD:HD + 1], 1.0))
                link(nc.gpsimd.memset(QS[i][96:ROWS].rearrange("p h n -> p (h n)"), 0.0))

        @block.tensor
        def _(pe):
            pe.sem_inc(xnT_full, 1)
            pe.sem_inc(lg_full, 1)
            pe.wait_ge(const_ok, 1)
            pe.wait_ge(w_in, 96)
            for c in range(3):
                m = nc.tensor.transpose(misc[:, c * D:(c + 1) * D], wqkv[:, c, :], ident[:])
            m.then_inc(pe_small, 1)
            m = nc.tensor.transpose(pv[:, 0:D], wo[:], ident[:])
            m = nc.tensor.transpose(pv[:, D:D + 64], hx[:], ident[0:64, 0:64])
            m = nc.tensor.transpose(pv[:, 192:192 + E], wr[:], ident[0:E, 0:E])
            nc.tensor.transpose(pv[:, 256:256 + E * FC], b1[:], ident[0:E * FC, 0:E * FC]).then_inc(pe_small, 1)
            pe.wait_ge(mix_exp, 2)
            pe.wait_ge(small_out, 3)
            nc.tensor.transpose(misc[0:NT, 0:H], st16[:, 0:NT], ident[0:H, 0:H]).then_inc(pe_small, 1)
            pe.wait_ge(small_out, 4)
            nc.tensor.matmul(misc[0:H, 64:64 + NE6 * NE6], twT[:], tr[:], start=True, stop=True).then_inc(pe_small, 1)
            pe.wait_ge(small_out, 5)
            nc.tensor.matmul(misc[0:1, 128:128 + H], st16[:, 0:1], ident[0:H, 0:H], start=True, stop=True).then_inc(pe_small, 1)
            with pe.Fori(0, B // 2) as bp:
                for i in range(2):
                    pe.wait_ge(xn_ok, bp * 2 + i + 1)
                    pe.wait_ge(xnT_ok, bp * 2 + 1)
                    for t in range(TT):
                        m = nc.tensor.transpose(lin[i][:, t * P:(t + 1) * P], xn[i][:, t, :], ident[:])
                    m.then_inc(xnT_full, 1)
                for i in range(2):
                    pe.wait_ge(xnT_ok, bp * 2 + i + 2)
                    pe.wait_ge(lg_out, bp * 2 + i + 1)
                    for t in range(TT):
                        m = nc.tensor.matmul(raw[i][:, t * E:(t + 1) * E], xT[i][:, t * P:(t + 1) * P], wrT[:],
                                             start=True, stop=True)
                    m.then_inc(lg_full, 1)

        @block.vector
        def _(dve):
            link = Link(dve, dve_chain)
            v = nc.vector
            dve.sem_inc(lg_out, 2)

            def token_stats(bp):
                for t in range(2 * TT):
                    tile = bp * (2 * TT) + t
                    m = v.bn_stats(stats[:, bass.ds(tile, 1), :], z[:, bass.ds(tile, 1), :])
                m.then_inc(stats_ok, 1)

            def half_stats(half):
                dve.wait_ge(stats_ok, (half + 1) * B // 4)
                cols = slice(half * NTOK // 2, (half + 1) * NTOK // 2)
                me, mo, qe, qo = (stats[:, cols, k] for k in (1, 4, 2, 5))
                mn, rs, a1, b1_, c1, d1 = (x[:, cols] for x in (mean, rstd, tA, tB, tC, tD))
                link(v.tensor_tensor(a1, me, mo, ALU.add))
                link(v.tensor_scalar(mn, a1, 0.5, None, ALU.mult))
                link(v.tensor_tensor(a1, me, mo, ALU.subtract))
                link(v.tensor_tensor(a1, a1, a1, ALU.mult))
                link(v.tensor_scalar(a1, a1, 0.25, None, ALU.mult))
                link(v.tensor_tensor(b1_, qe, qo, ALU.add))
                link(v.scalar_tensor_tensor(out=b1_, in0=b1_, scalar=1.0 / D, in1=a1, op0=ALU.mult, op1=ALU.add))
                v.tensor_scalar(b1_, b1_, 1e-5, None, ALU.add).then_inc(var_ok, 1)
                dve.wait_ge(root_ok, half + 1)
                link(v.reciprocal(c1, rs))
                link(v.tensor_tensor(d1, c1, c1, ALU.mult))
                link(v.tensor_tensor(d1, d1, b1_, ALU.mult))
                link(v.tensor_scalar(d1, d1, -0.5, 1.5, ALU.mult, ALU.add))
                link(v.tensor_tensor(rs, c1, d1, ALU.mult))

            def normalise_pair(bp):
                for i in range(2):
                    if not (isinstance(bp, int) and bp == 0):
                        dve.wait_ge(xnT_full, bp * 2 + i)
                    for t in range(TT):
                        tile = (bp * 2 + i) * TT + t
                        m = v.tensor_scalar(xn[i][:, t, :], z[:, bass.ds(tile, 1), :], mean[:, bass.ds(tile, 1)],
                                            rstd[:, bass.ds(tile, 1)], ALU.subtract, ALU.mult)
                    m.then_inc(xn_ok, 1)

            def logits_out(bp):
                for i in range(2):
                    dve.wait_ge(lg_full, bp * 2 + i + 2)
                    v.tensor_tensor(lg[:, bass.ds((bp * 2 + i) * TT, TT), :],
                                    raw[i][:, 0:TT * E].rearrange("p (t e) -> p t e", e=E),
                                    brr[:].rearrange("p (a e) -> p a e", a=1).to_broadcast([P, TT, E]), ALU.add).then_inc(lg_out, 1)

            for i in range(2):
                dve.wait_ge(x_in[i], 16)
                with dve.Fori(0, B // 8) as bp:
                    token_stats(bp + i * (B // 8))
            link(v.memset(mixS[:], 0.0))
            dve.wait_ge(pe_small, 1)
            v.tensor_copy(wqkvT[:, 0:2 * D].rearrange("p (c d h) -> p c d h", c=2, h=H)[:, 0],
                          misc[:, 0:D].rearrange("p (h d) -> p d h", h=H))
            v.tensor_copy(wqkvT[:, 0:2 * D].rearrange("p (c d h) -> p c d h", c=2, h=H)[:, 1],
                          misc[:, D:2 * D].rearrange("p (h d) -> p d h", h=H))
            v.tensor_copy(wqkvT[:, 2 * D:3 * D], misc[:, 2 * D:3 * D]).then_inc(small_out, 1)
            dve.wait_ge(pe_small, 2)
            dve.wait_ge(w_in, 96)
            v.tensor_copy(woT[:], pv[:, 0:D]).then_inc(small_out, 1)
            v.tensor_copy(hexT[:], pv[:, D:D + 64])
            v.tensor_copy(wrT[:], pv[:, 192:192 + E]).then_inc(small_out, 1)
            v.tensor_copy(b1T[:], pv[:, 256:256 + E * FC]).then_inc(b1_ok, 1)
            dve.wait_ge(small_in, 16 * 8)
            link(v.reduce_max(st16[:, 7:8], tw[:], AX))
            v.tensor_scalar(st16[:, 7:8], st16[:, 7:8], -2.0, None, ALU.mult).then_inc(mix_exp_in, 1)
            dve.wait_ge(mix_exp, 1)
            link(v.reduce_sum(st16[:, 7:8], st16[:, 0:NT], AX))
            link(v.reciprocal(st16[:, 7:8], st16[:, 7:8]))
            v.tensor_scalar(st16[:, 0:NT], st16[:, 0:NT], st16[:, 7:8], None, ALU.mult).then_inc(mix_exp, 1)
            dve.wait_ge(sig_exp, 1)
            link(v.tensor_scalar(plog[:, 4:6], plog[:, 4:6], 1.0, None, ALU.add))
            link(v.reciprocal(par[:, 2:4], plog[:, 4:6]))
            link(v.reciprocal(par[:, 1:2], plog[:, 0:1]))
            link(v.tensor_scalar(par[:, 4:5], par[:, 2:3], 0.5, None, ALU.mult))
            link(v.tensor_scalar(par[:, 5:6], par[:, 3:4], 2.0 / 6.0, None, ALU.mult))
            link(v.tensor_scalar(mixS[0:NE6, HAM0:HAM0 + NE6], ident[0:NE6, 0:NE6], par[0:NE6, 4:5], None, ALU.mult))
            link(v.tensor_copy(mixS[HEX0:HEX0 + NE6, HAM0 + NE6:HAM0 + 2 * NE6], ident[HEX0:HEX0 + NE6, HEX0:HEX0 + NE6]))
            link(v.tensor_copy(mixS[0:NE6, HAM0 + 2 * NE6:NA], ident[0:NE6, 0:NE6]))
            dve.wait_ge(pe_small, 3)
            v.tensor_copy(twT[:], misc[0:NT, 0:H]).then_inc(small_out, 1)
            dve.wait_ge(pe_small, 4)
            v.tensor_scalar(mix[:], misc[0:H, 64:64 + NE6 * NE6], par[0:H, 5:6], None, ALU.mult).then_inc(mix_sb, 1)
            dve.wait_ge(mix_sb, 1)
            v.tensor_reduce(st16[:, 0:1], mix[:], AX, ALU.add, apply_absolute_value=True).then_inc(small_out, 1)
            dve.wait_ge(pe_small, 5)
            link(v.reduce_max(plog[0:1, 6:7], misc[0:1, 128:128 + H], AX))
            link(v.scalar_tensor_tensor(out=plog[0:1, 6:7], in0=par[0:1, 2:3], scalar=3.0, in1=plog[0:1, 6:7],
                                        op0=ALU.mult, op1=ALU.add))
            link(v.tensor_scalar(plog[0:1, 7:8], par[0:1, 0:1], -1.0, None, ALU.mult))
            link(v.tensor_tensor(plog[0:1, 7:8], plog[0:1, 7:8], par[0:1, 0:1], ALU.max))
            link(v.tensor_tensor(plog[0:1, 6:7], plog[0:1, 6:7], plog[0:1, 7:8], ALU.add))
            link(v.tensor_scalar(flag[:], plog[0:1, 6:7], SAFE_RANGE, None, ALU.is_le))

            for i in (2, 3):
                dve.wait_ge(x_in[i], 16)
            half_stats(0)
            normalise_pair(0)
            with dve.Fori(0, B // 4 - 1) as bp:
                token_stats(bp + B // 4)
                normalise_pair(bp + 1)
                logits_out(bp)
            token_stats(B // 2 - 1)
            half_stats(1)
            normalise_pair(B // 4)
            logits_out(B // 4 - 1)
            with dve.Fori(0, B // 4 - 1) as bp:
                normalise_pair(bp + B // 4 + 1)
                logits_out(bp + B // 4)
            logits_out(B // 2 - 1)

            dve.wait_ge(lg_out, B + 2)

PROLOGUE = ["codes", "mixed", "q", "k", "v"]
MERGE_JOBS = [(0, 2, "merge"), (0, 9, "proj")]
ATTN_JOBS = [(0, 1, "q"), (0, 3, "k"), (0, 5, "codes"), (0, 7, "mixed"), (3, 9, "v")]
W_JOBS = [(1, 1, "w0"), (1, 4, "w1"), (1, 7, "w2"), (2, 1, "w3"), (2, 4, "w4"), (2, 7, "w5"), (3, 1, "w6"), (3, 4, "w7")]
F_JOBS = [(1, 1, "fxA"), (1, 3, "h0A"), (1, 5, "h1A"), (1, 7, "h2A"), (2, 1, "y0A"), (2, 2, "y1A"), (2, 3, "fxB"),
          (2, 4, "y2A"), (2, 5, "h0B"), (2, 7, "h1B"), (3, 1, "h2B"), (3, 3, "y0B"), (3, 5, "y1B"), (3, 7, "y2B")]
assert all(j[:2] < (3, 9) for j in MERGE_JOBS + W_JOBS + F_JOBS)
KINDS = {
    "first": sorted(ATTN_JOBS + W_JOBS),
    "second": sorted(ATTN_JOBS + MERGE_JOBS + W_JOBS),
    "ffn": sorted(ATTN_JOBS + MERGE_JOBS + F_JOBS),
    "plain": sorted(ATTN_JOBS + MERGE_JOBS),
    "last": sorted(MERGE_JOBS),
}
NU = 2 * NC
MAXIMA_AT = (NQ - 2, 6)
PV_AT = {2: [0], 4: [1, 3], 6: [2]}
SCATTERS = [4, 8, 10, 10]
RELUS = [(1, 0, "A"), (1, 1, "A"), (1, 2, "A"), (2, 0, "B"), (2, 1, "B"), (3, 2, "B")]
GATHERS = [[0, 4, 9, 9], [9, 9, 8, 8]]
F_FROM, F_TO = 2, 14
assert (F_TO - F_FROM) * 2 * FG == NSLOT
N_RAW_IN, N_LIN_IN = 9, 18


def turn(b, kind, job):
    names = [j[2] for j in KINDS[kind]]
    n = len(PROLOGUE) + names.index(job)
    if kind == "first":
        return n
    n += len(KINDS["first"])
    if kind == "second":
        return n
    n += len(KINDS["second"])
    if kind == "ffn":
        return (b - F_FROM) * len(KINDS["ffn"]) + n
    n += len(KINDS["ffn"]) * (F_TO - F_FROM)
    if kind == "plain":
        return n
    return n + len(KINDS["plain"])


TAIL_TURN = turn(B - 1, "last", KINDS["last"][-1][2]) + 1


def each_batch(eng, body):
    body(0, 0, "first")
    body(1, 1, "second")
    with eng.Fori(0, (F_TO - F_FROM) // 2) as bp:
        body(bp * 2 + F_FROM, 0, "ffn")
        body(bp * 2 + F_FROM + 1, 1, "ffn")
    body(B - 2, 0, "plain")
    body(B - 1, 1, "last")


def following(b, pb, q):
    return (b, pb, q + 1) if q + 1 < NQ else (b + 1, 1 - pb, 0)


def layer(nc, a, out, g):
    z, wqkvT, woT, hexT, mixS, par, ident, S = (g[k] for k in ("z", "wqkvT", "woT", "hexT", "mixS", "par", "ident", "S"))
    QS, LK, V1, raw, lin, pv, misc = (g[k] for k in ("QS", "LK", "V1", "raw", "lin", "pv", "misc"))
    xt_d, qp_d, kp_d, ap_d, hp_d = (g[k] for k in ("xt_d", "qp_d", "kp_d", "ap_d", "hp_d"))
    w1_d, w2_d, xs_d, ys_d = (g[k] for k in ("w1_d", "w2_d", "xs_d", "ys_d"))
    etile, posu, mean, rstd = (g[k] for k in ("etile", "posu", "mean", "rstd"))

    with ExitStack() as ctx:
        def sb(name, shape, dt=F32):
            return ctx.enter_context(nc.sbuf_tensor(name, shape, dt))

        def sem(name):
            return ctx.enter_context(nc.semaphore(name))

        RK = [sb(f"RK{i}", [ROWS, H, T], BF16) for i in range(2)]
        xTr = [sb(f"xTr{i}", [P, T]) for i in range(2)]
        sQ, sK, rest, oT = (sb(n, [P, T]) for n in ("sQ", "sK", "rest", "oT"))
        sA = sQ
        ht = sb("ht", [64, T])
        partsQ, partsK = sb("partsQ", [P, 3, T], BF16), sb("partsK", [P, 3, T], BF16)
        partsA = partsQ
        at = sb("at", [P, TT, D])
        rec = sb("rec", [P, TT, QH])
        w1 = [sb(f"w1_{i}", [P, F + FC]) for i in range(FG)]
        w2 = [sb(f"w2_{i}", [P, F + D]) for i in range(FG)]
        one = sb("one", [P, 1])
        xin = sb("xin", [P, FG, D])
        xsT = sb("xsT", [P, FG, P])
        hid = [sb(f"hid{i}", [P, FC, P]) for i in range(FG)]
        ysb = sb("ysb", [P, FG, D])
        xs = [x[:, i, :] for x in (xin, xsT, ysb, hid[2]) for i in range(FG)]
        NXS = len(xs)

        raw_full, t_done, lin_full, s_done, e_done, m_done = (sem(n) for n in (
            "raw_full", "t_done", "lin_full", "s_done", "e_done", "m_done"))
        pv_done, oT_ok, o_full, rec_ok, o_used = (sem(n) for n in ("pv_done", "oT_ok", "o_full", "rec_ok", "o_used"))
        misc_full, misc_used = sem("misc_full"), sem("misc_used")
        waited, waited_sp, waited_pe, rk_clear = sem("waited"), sem("waited_sp"), sem("waited_pe"), sem("rk_clear")
        split_ok, split_chain = {n: sem(f"split_{n}") for n in "qka"}, sem("split_chain")
        stored, h_stored = {n: sem(f"stored_{n}") for n in "qka"}, sem("h_stored")
        xt_in = [sem(f"xt_in{i}") for i in range(2)]
        raw_in = [sem(f"raw_in{i}") for i in range(2)]
        lin_in = [sem(f"lin_in{i}") for i in range(2)]
        ew_in, ew_out = ([sem(f"{n}{i}") for i in range(2)] for n in ("ew_in", "ew_out"))
        mx_d = g["mx_d"]
        xs_ok, xs_sent, xs_done = sem("xs_ok"), [sem(f"xs_sent{i}") for i in range(NXS)], sem("xs_done")
        relu_ok, hidden_ok = sem("relu_ok"), sem("hidden_ok")
        fx_in, w1_in, w2_in, y_out = sem("fx_in"), [sem(f"w1_in{i}") for i in range(FG)], sem("w2_in"), sem("y_out")
        y_all, yg_in, sum_ok, final_out = sem("y_all"), [sem(f"yg_in{i}") for i in range(NXS)], sem("sum_ok"), sem("final_out")

        def turns_before_maxima(b, kind):
            return turn(b, kind, KINDS[kind][0][2]) + len([j for j in KINDS[kind] if j[:2] < MAXIMA_AT])

        def jobs_at(kind, s, u):
            return [j[2] for j in KINDS[kind] if j[:2] == (s, u)]

        def first_tile(counts, s):
            return sum(counts[:s])

        tmax = sb("tmax", [P, T])
        aT = tmax
        mx = sb("mx", [P, H * TT])
        mrest = tmax[0:H * TT, 0:P]
        mparts = sb("mparts", [H * TT, NSHIFT, P], BF16)
        hidden = sb("hidden", [P, P], BF16)
        px_full, px_used, px_sum, px_max, px_split, px_out, px_in = (sem(n) for n in (
            "px_full", "px_used", "px_sum", "px_max", "px_split", "px_out", "px_in"))
        NPX = 2 * H * TT + 1
        HT = H * TT

        def general(eng):
            return eng.If(eng.value_load(g["flag"][0:1, 0:1], min_val=0, max_val=1) == 0)

        oh_ok, rank_full, rank_read, routed, route_chain = (sem(n) for n in (
            "oh_ok", "rank_full", "rank_read", "routed", "route_chain"))
        scratch = router_scratch(S)
        lg, eq, ohf, ohb, cmp, sm, tA, desc, j128, slotid, rank, tot = (scratch[n] for n in (
            "lg", "eq", "ohf", "ohb", "cmp", "sm", "tA", "desc", "j128", "slotid", "rank", "tot"))
        scan = [scratch["scan0"], scratch["scan1"]]

        block = ctx.enter_context(nc.Block())

        @block.tensor
        def _(pe):
            mm = nc.tensor.matmul
            pe.sem_inc(raw_full, 1)
            pe.sem_inc(lin_full, 1)
            pe.sem_inc(pv_done, 1)

            def fill_raw(bf, pf, q, c):
                n = (bf * NQ + q) * NC + c
                if not (isinstance(n, int) and n < 2):
                    pe.wait_ge(t_done, n - 1)
                if q == 0 and c == 0:
                    pe.wait_ge(lin_in[pf], (bf - pf) * (8 * N_LIN_IN) + 16 * N_LIN_IN)
                    pe.wait_ge(raw_in[pf], (bf - pf) * (8 * N_RAW_IN) + 16 * N_RAW_IN)
                for cc, col, j, kt, qs in PARTS:
                    if cc == c:
                        h = q * QH + j
                        m = mm(raw[(q + c) % 2][:, col:col + T - qs], RK[pf][:, h, kt * P:(kt + 1) * P],
                               QS[pf][:, h, qs:T], start=True, stop=True)
                m.then_inc(raw_full, 1)

            def fill_lin(bf, pf, q, u):
                c, half = u // 2, u % 2
                n = (bf * NQ + q) * NU + u
                if not (isinstance(n, int) and n < 2):
                    pe.wait_ge(s_done, n - 1)
                for cc, col, j, kt, qs in PARTS:
                    if cc == c and col // T == half:
                        h = q * QH + j
                        m = mm(lin[half][:, col - half * T:col - half * T + T - qs], LK[pf][:, kt * P:(kt + 1) * P],
                               QS[pf][:, h, qs:T], start=True, stop=True)
                m.then_inc(lin_full, 1)

            def weigh(pb, q, kts):
                for kt in kts:
                    for cc, col, j, k, qs in PARTS:
                        if k == kt:
                            m = mm(pv[j * HP:(j + 1) * HP, qs:T], V1[pb][:, kt, q * QH + j, :],
                                   S[:, q % 2, cc, col:col + T - qs], start=(kt == 0), stop=(kt == 2))
                return m

            def turn_tiles(src, n=TT):
                for t in range(n):
                    m = nc.tensor.transpose(misc[:, t * P:(t + 1) * P], src(t), ident[:])
                return m

            def job(name, n, b, pb):
                if not (isinstance(n, int) and n == 0):
                    pe.wait_ge(misc_used, n)
                bn, pn = b + 1, 1 - pb
                k = (b - F_FROM) * 2 + (1 if name[-1] == "B" else 0)
                if name == ("codes" if isinstance(b, int) and b < 0 else "q"):
                    pe.wait_ge(xt_in[pn], (bn - pn) * 8 + 16)
                if name == "q":
                    m = mm(misc[:], wqkvT[:, 0:D], xTr[pn][:], start=True, stop=True)
                elif name == "k":
                    m = mm(misc[:], wqkvT[:, D:2 * D], xTr[pn][:], start=True, stop=True)
                elif name == "codes":
                    m = mm(misc[0:64], hexT[:], xTr[pn][:], start=True, stop=True)
                elif name == "mixed":
                    m = mm(misc[:], mixS[:], ht[:], start=True, stop=True)
                elif name == "v":
                    for t in range(TT):
                        m = mm(misc[:, t * P:(t + 1) * P], xTr[pn][:, t * P:(t + 1) * P], wqkvT[:, 2 * D:3 * D],
                               start=True, stop=True)
                elif name == "merge":
                    pe.wait_ge(o_used, b * NQ + 1)
                    m = turn_tiles(lambda t: at[:, t, :])
                elif name == "proj":
                    for t in range(TT):
                        m = mm(misc[:, t * P:(t + 1) * P], aT[:, t * P:(t + 1) * P], woT[:], start=True, stop=True)
                elif name[0] == "w":
                    i, e = int(name[1]), b * (E // 2) + int(name[1]) // 2
                    if i % 2 == 0:
                        pe.wait_ge(ew_in[e % 2], (e // 2 + 1) * 32)
                    m = turn_tiles(lambda t: (w1, w2)[i % 2][e % 2][:, t * P:(t + 1) * P])
                elif name[:2] == "fx":
                    pe.wait_ge(fx_in, k * 16 + 16)
                    m = turn_tiles(lambda t: xin[:, t, :], FG)
                elif name[0] == "h":
                    i = int(name[1])
                    pe.wait_ge(w1_in[i], k * 16 + 16)
                    for c in range(FC):
                        m = mm(misc[:, c * P:(c + 1) * P], w1[i][:, c * P:(c + 1) * P], xsT[:, i, :], start=True, stop=True)
                elif name[0] == "y":
                    i = int(name[1])
                    pe.wait_ge(w2_in, k * 48 + 48)
                    pe.wait_ge(relu_ok, k * FG + i + 1)
                    for c in range(FC):
                        m = mm(misc[:, 0:P], hid[i][:, c, :], w2[i][:, c * P:(c + 1) * P], start=(c == 0), stop=(c == FC - 1))
                m.then_inc(misc_full, 1)

            def turn_outputs(b, s):
                pe.wait_ge(oT_ok, b * NQ + s + 1)
                for t in range(TT):
                    m = nc.tensor.transpose(pv[:, t * P:(t + 1) * P], oT[:, t * P:(t + 1) * P], ident[:])
                m.then_inc(o_full, 1)

            def maxima(bn, pn, n):
                pe.wait_ge(lin_in[pn], (bn - pn) * (8 * N_LIN_IN) + 16 * N_LIN_IN)
                pe.wait_ge(raw_in[pn], (bn - pn) * (8 * N_RAW_IN) + 16 * N_RAW_IN)
                pe.wait_ge(misc_used, n)
                pe.sem_inc(waited_pe, 1)
                with pe.Fori(0, H) as h:
                    for qt in range(TT):
                        w, t = (qt + 1) * P, bn * NPX + (h * TT + qt) * 2
                        query = QS[pn][0:SHIFT0, bass.ds(h, 1), qt * P:w].rearrange("r h n -> r (h n)")
                        pe.wait_ge(px_used, t + 1)
                        mm(misc[:, 0:w], query, RK[pn][0:SHIFT0, bass.ds(h, 1), 0:w].rearrange("r h n -> r (h n)"),
                           start=True, stop=True).then_inc(px_full, 1)
                        pe.wait_ge(px_used, t + 2)
                        mm(misc[:, 0:w], query, LK[pn][0:SHIFT0, 0:w], start=True, stop=True).then_inc(px_full, 1)
                pe.wait_ge(px_used, bn * NPX + NPX)
                pe.wait_ge(px_max, (bn + 1) * HT + 1)
                pe.sem_inc(waited_pe, 1)
                nc.tensor.transpose(misc[0:HT, 0:P], mx[:], ident[:]).then_inc(px_full, 1)
                pe.wait_ge(px_used, (bn + 1) * NPX + 1)
                pe.wait_ge(px_in, bn * 16 + 16)

            for n, name in enumerate(PROLOGUE):
                job(name, n, -1, 1)
            pe.wait_ge(oh_ok, 1)
            oh = scratch["ohb"].rearrange("p t e -> p (t e)")
            mm(pv[:, 0:T], scratch["tri"], oh, start=True, stop=True).then_inc(rank_full, 1)
            mm(raw[1][:, 0:T], scratch["onesb"], oh, start=True, stop=True).then_inc(rank_full, 1)
            with general(pe):
                maxima(0, 0, len(PROLOGUE))
            fill_raw(0, 0, 0, 0)
            pe.wait_ge(rank_read, 1)
            fill_raw(0, 0, 0, 1)
            for u in range(NU):
                fill_lin(0, 0, 0, u)
                if u % 2 == 0:
                    fill_raw(0, 0, (u // 2 + 2) // NC, (u // 2 + 2) % NC)
            fill_lin(0, 0, 1, 0)

            def body(b, pb, kind):
                for s in range(NQ):
                    bf, pf, qf = following(b, pb, s)
                    last_front = kind == "last" and s == NQ - 2
                    front = not (kind == "last" and s == NQ - 1)
                    for u in range(NU):
                        c = u // 2
                        if front:
                            if u + 1 < NU:
                                fill_lin(bf, pf, qf, u + 1)
                            elif not last_front:
                                fill_lin(*following(bf, pf, qf), 0)
                            if u % 2 == 0:
                                if c + 2 < NC:
                                    fill_raw(bf, pf, qf, c + 2)
                                elif not last_front:
                                    if (s, u) == MAXIMA_AT:
                                        with general(pe):
                                            maxima(b + 1, 1 - pb, turns_before_maxima(b, kind))
                                    fill_raw(*following(bf, pf, qf), c + 2 - NC)
                        if u in PV_AT:
                            if u == 2:
                                pe.wait_ge(m_done, (b * NQ + s) * 2 + 1)
                                pe.wait_ge(o_used, b * NQ + s + 1)
                            if u == 6:
                                pe.wait_ge(m_done, (b * NQ + s) * 2 + 2)
                            m = weigh(pb, s, PV_AT[u])
                            if u == 6:
                                m.then_inc(pv_done, 1)
                        for name in jobs_at(kind, s, u):
                            job(name, turn(b, kind, name), b, pb)
                        if u == NU - 1:
                            turn_outputs(b, s)

            each_batch(pe, body)
            job("merge", TAIL_TURN, B, 0)
            job("proj", TAIL_TURN + 1, B, 0)

        @block.scalar
        def _(act):
            def tanh(bf, q, c):
                n = (bf * NQ + q) * NC + c
                act.wait_ge(raw_full, n + 2)
                if c == 0 and not (isinstance(n, int) and n == 0):
                    act.wait_ge(pv_done, bf * NQ + q)
                nc.scalar.activation(S[:, q % 2, c, :], raw[(q + c) % 2][:], ACT.Tanh).then_inc(t_done, 1)

            def exp(bf, q, c0, c1):
                act.wait_ge(s_done, (bf * NQ + q) * (2 * NC) + 2 * c1)
                x = S[:, q % 2, c0:c1, :]
                nc.scalar.activation(x, x, ACT.Exp).then_inc(e_done, 1)

            def codes(n):
                act.wait_ge(misc_full, n + 1)
                nc.scalar.activation(ht[:], misc[0:64], ACT.Tanh).then_inc(misc_used, 1)

            def maxima(bn):
                with act.Fori(0, H) as h:
                    for qt in range(TT):
                        w, i = (qt + 1) * P, h * TT + qt
                        act.wait_ge(px_full, bn * NPX + i * 2 + 1)
                        act.wait_ge(px_max, bn * HT + i + 1)
                        nc.scalar.activation(tmax[:, 0:w], misc[:, 0:w], ACT.Tanh).then_inc(px_used, 1)

            codes(PROLOGUE.index("codes"))
            with general(act):
                maxima(0)
            for c in range(4):
                tanh(0, 0, c)
            exp(0, 0, 0, 2)
            tanh(0, 0, 4)
            act.wait_ge(routed, 1)
            tanh(0, 1, 0)
            exp(0, 0, 2, 4)

            def body(b, pb, kind):
                for s in range(NQ):
                    bf, pf, qf = following(b, pb, s)
                    if kind == "last" and s == NQ - 1:
                        exp(b, s, 4, 5)
                        continue
                    tanh(bf, qf, 1)
                    exp(b, s, 4, 5)
                    tanh(bf, qf, 2)
                    tanh(bf, qf, 3)
                    exp(bf, qf, 0, 2)
                    if s == 0 and kind != "last":
                        codes(turn(b, kind, "codes"))
                    tanh(bf, qf, 4)
                    if s == MAXIMA_AT[0] and kind != "last":
                        with general(act):
                            maxima(b + 1)
                    if not (kind == "last" and s == NQ - 2):
                        b2, _, q2 = following(bf, pf, qf)
                        tanh(b2, q2, 0)
                    exp(bf, qf, 2, 4)

            each_batch(act, body)

        @block.vector
        def _(dve):
            v = nc.vector
            dve.sem_inc(o_used, 1)
            v.memset(one[:], 1.0).then_inc(hidden_ok, 1)
            v.memset(hidden[:], 0.0).then_inc(hidden_ok, 1)

            def add(bf, q, c, half):
                n = (bf * NQ + q) * NC + c
                if half == 0:
                    dve.wait_ge(t_done, n + 1)
                dve.wait_ge(lin_full, n * 2 + half + 2)
                x = S[:, q % 2, c, half * T:(half + 1) * T]
                v.scalar_tensor_tensor(out=x, in0=x, scalar=par[:, 0:1], in1=lin[half][:], op0=ALU.mult,
                                       op1=ALU.add).then_inc(s_done, 1)

            def take(name, n, b, pb):
                bn, pn = b + 1, 1 - pb
                first = isinstance(b, int) and b < 0
                dve.wait_ge(misc_full, n + 1)
                if name == "q":
                    dve.wait_ge(split_ok["a"], 1 if first else b + 1)
                    v.tensor_scalar(sQ[:], misc[:], par[:, 1:2], None, ALU.mult).then_inc(misc_used, 1)
                elif name == "k":
                    if not first:
                        dve.wait_ge(split_ok["k"], b + 1)
                    v.tensor_copy(sK[:], misc[:]).then_inc(misc_used, 1)
                elif name == "mixed":
                    if not first:
                        dve.wait_ge(split_ok["q"], b + 2)
                    v.tensor_copy(sA[:], misc[:]).then_inc(misc_used, 1)
                elif name == "v":
                    if not first:
                        dve.wait_ge(pv_done, b * NQ + 1)
                    v.tensor_copy(V1[pn][:, :, :, 0:HD], misc[:].rearrange("p (t h d) -> p t h d", t=TT, h=H)).then_inc(misc_used, 1)
                elif name == "merge":
                    v.tensor_copy(aT[:], misc[:]).then_inc(misc_used, 1)
                elif name == "proj":
                    bp = b - 1
                    zb = z[:, bass.ds(bp * TT, TT), :]
                    v.tensor_tensor(zb, misc[:].rearrange("p (t d) -> p t d", t=TT), zb, ALU.add).then_inc(misc_used, 1)
                elif name[0] == "w":
                    i = int(name[1])
                    dst = (hid[0], hid[1])[i % 2]
                    j = b * (E // 2) * 2 + i
                    if j >= 2:
                        dve.wait_ge(ew_out[i % 2], j // 2 * 16)
                    v.tensor_copy(dst[:].rearrange("p c n -> p (c n)"), misc[:]).then_inc(misc_used, 1)
                elif name[:2] == "fx":
                    v.tensor_copy(xsT[:], misc[:, 0:FG * P].rearrange("p (i n) -> p i n", i=FG)).then_inc(misc_used, 1)
                elif name[0] == "h":
                    i = int(name[1])
                    v.tensor_tensor(hid[i][:], misc[:].rearrange("p (c n) -> p c n", c=FC),
                                    w1[i][:, F:F + FC].rearrange("p (c a) -> p c a", a=1).to_broadcast([P, FC, P]),
                                    ALU.add).then_inc(misc_used, 1)
                elif name[0] == "y":
                    i, k = int(name[1]), (b - F_FROM) * 2 + (1 if name[-1] == "B" else 0)
                    if i == 0:
                        dve.wait_ge(y_out, k * 16 + 1)
                    v.tensor_tensor(ysb[:, i, :], misc[:, 0:P], w2[i][:, F:F + D], ALU.add).then_inc(misc_used, 1)

            def take_outputs(b, s):
                dve.wait_ge(o_full, b * NQ + s + 1)
                o = pv[:].rearrange("p (t j r) -> p t j r", t=TT, j=QH)
                v.reciprocal(rec[:], o[:, :, :, HD]).then_inc(rec_ok, 1)
                dve.wait_ge(rec_ok, b * NQ + s + 1)
                v.tensor_tensor(at[:, :, s * QH * HD:(s + 1) * QH * HD].rearrange("p t (j d) -> p t j d", j=QH),
                                o[:, :, :, 0:HD],
                                rec[:].rearrange("p t (j a) -> p t j a", a=1).to_broadcast([P, TT, QH, HD]),
                                ALU.mult).then_inc(o_used, 1)

            def normalise(tile):
                i = tile % NXS
                if tile >= NXS:
                    dve.wait_ge(xs_sent[i], tile // NXS * 16)
                v.tensor_scalar(xs[i], z[:, tile, :], mean[:, tile:tile + 1], rstd[:, tile:tile + 1],
                                ALU.subtract, ALU.mult).then_inc(xs_ok, 1)

            def add_back(tile):
                i = tile % NXS
                dve.wait_ge(yg_in[i], tile // NXS * 16 + 16)
                v.tensor_tensor(z[:, tile, :], z[:, tile, :], xs[i], ALU.add).then_inc(sum_ok, 1)

            def maxima(bn):
                with dve.Fori(0, H) as h:
                    for qt in range(TT):
                        w, i = (qt + 1) * P, h * TT + qt
                        dve.wait_ge(px_full, bn * NPX + i * 2 + 2)
                        v.scalar_tensor_tensor(out=tmax[:, 0:w], in0=tmax[:, 0:w], scalar=par[:, 0:1], in1=misc[:, 0:w],
                                               op0=ALU.mult, op1=ALU.add).then_inc(px_sum, 1)
                        dve.wait_ge(px_sum, (bn * HT + i) * 2 + 1)
                        v.tensor_tensor(tmax[:, w - P:w], tmax[:, w - P:w], hidden[:], ALU.add).then_inc(px_sum, 1)
                        dve.wait_ge(px_sum, (bn * HT + i) * 2 + 2)
                        v.tensor_reduce(mx[:, bass.ds(i, 1)], tmax[:, 0:w], AX, ALU.max, negate=True).then_inc(px_max, 1)
                        dve.sem_inc(px_used, 1)
                dve.wait_ge(px_full, (bn + 1) * NPX)
                m, link = misc[0:HT, 0:P], Link(dve, px_split, bn * 4)
                link(v.tensor_copy(mparts[:, 0, :], m))
                link(v.tensor_tensor(mrest, m, mparts[:, 0, :], ALU.subtract))
                link(v.tensor_copy(mparts[:, 1, :], mrest))
                link(v.tensor_tensor(mparts[:, 2, :], mrest, mparts[:, 1, :], ALU.subtract))
                dve.sem_inc(px_used, 1)

            def route():
                link = Link(dve, route_chain)

                def over_t(ap):
                    return ap.rearrange("p (t a) -> p t a", a=1).to_broadcast([P, NTOK, E])

                def over_e(ap):
                    return ap.rearrange("p (a e) -> p a e", a=1).to_broadcast([P, NTOK, E])

                link(v.tensor_reduce(tA[:], lg[:], AX, ALU.max))
                link(v.tensor_tensor(eq[:], lg[:], over_t(tA[:]), ALU.is_ge))
                link(v.tensor_tensor(eq[:], eq[:], over_e(desc[:]), ALU.mult))
                link(v.tensor_reduce(tA[:], eq[:], AX, ALU.max))
                link(v.tensor_tensor(ohf[:], eq[:], over_t(tA[:]), ALU.is_equal))
                v.tensor_copy(ohb[:], ohf[:]).then_inc(oh_ok, 1)
                dve.wait_ge(rank_full, 2)
                link(v.tensor_copy(tot, raw[1][:, 0:T].rearrange("p (t e) -> p t e", e=E)))
                v.tensor_copy(rank, pv[:, 0:T].rearrange("p (t e) -> p t e", e=E)).then_inc(rank_read, 1)
                dve.wait_ge(rank_read, 1)
                link(v.tensor_copy(scan[0][:], tot))
                cur, k = 0, 1
                while k < NTOK:
                    link(v.tensor_copy(scan[1 - cur][:, 0:k, :], scan[cur][:, 0:k, :]))
                    link(v.tensor_tensor(scan[1 - cur][:, k:, :], scan[cur][:, k:, :], scan[cur][:, 0:NTOK - k, :], ALU.add))
                    cur, k = 1 - cur, 2 * k
                incl, other = scan[cur], scan[1 - cur]
                link(v.tensor_copy(sm[:, 0, :], incl[:, NTOK - 1, :]))
                link(v.tensor_tensor(eq[:], over_e(sm[:, 0, :]), over_t(j128[:]), ALU.is_gt))
                link(v.tensor_reduce(sm[:, 1, :], eq[:].rearrange("p t e -> p e t"), AX, ALU.add))
                src, k = 1, 1
                while k < E:
                    link(v.tensor_copy(sm[:, src + 1, 0:k], sm[:, src, 0:k]))
                    link(v.tensor_tensor(sm[:, src + 1, k:], sm[:, src, k:], sm[:, src, 0:E - k], ALU.add))
                    src, k = src + 1, 2 * k
                link(v.tensor_tensor(sm[:, 5, :], sm[:, src, :], sm[:, 1, :], ALU.subtract))
                link(v.tensor_scalar(sm[:, 6, :], sm[:, 5, :], float(P), None, ALU.mult))
                link(v.tensor_tensor(incl[:], incl[:], tot, ALU.subtract))
                link(v.tensor_tensor(other[:], rank, incl[:], ALU.add))
                link(v.tensor_tensor(other[:], other[:], over_e(sm[:, 6, :]), ALU.add))
                link(v.tensor_tensor(other[:], other[:], ohf[:], ALU.mult))
                link(v.tensor_reduce(tA[:], other[:], AX, ALU.add))
                link(v.tensor_copy(posu[:], tA[:]))
                link(v.tensor_tensor(cmp[:], slotid[:].rearrange("p (t a) -> p t a", a=1).to_broadcast([P, NSLOT, E]),
                                     sm[:, src, :].rearrange("p (a e) -> p a e", a=1).to_broadcast([P, NSLOT, E]), ALU.is_ge))
                link(v.tensor_reduce(slotid[:], cmp[:], AX, ALU.add))
                v.tensor_scalar(etile[:], slotid[:], float(E - 1), None, ALU.min).then_inc(routed, 1)

            dve.sem_inc(px_used, 1)
            dve.sem_inc(px_max, 1)
            for n, name in enumerate(PROLOGUE):
                if name != "codes":
                    take(name, n, -1, 1)
            route()
            dve.wait_ge(hidden_ok, 3)
            with general(dve):
                maxima(0)
            for u in range(NU):
                add(0, 0, u // 2, u % 2)

            def body(b, pb, kind):
                pending = []
                if kind != "first":
                    pending = [("v", turn(b, kind, KINDS[kind][0][2]) - 1, b - 1, 1 - pb)]
                for s in range(NQ):
                    bf, _, qf = following(b, pb, s)
                    front = not (kind == "last" and s == NQ - 1)
                    tiles = []
                    if kind in ("first", "second"):
                        t0 = b * (NTOK // 2) + first_tile(SCATTERS, s)
                        tiles = range(t0, t0 + SCATTERS[s])
                    if kind in ("plain", "last"):
                        counts, n = GATHERS[0] + GATHERS[1], (b - B + 2) * NQ + s
                        tiles = range(first_tile(counts, max(n - 1, 0)), first_tile(counts, n))
                    for u in range(NU):
                        if u == 8:
                            dve.wait_ge(pv_done, b * NQ + s + 2)
                            v.tensor_copy(oT[:], pv[:]).then_inc(oT_ok, 1)
                        if front:
                            add(bf, qf, u // 2, u % 2)
                        if u == 0 and s > 0:
                            take_outputs(b, s - 1)
                        elif u == 0 and kind != "first":
                            take_outputs(b - 1, NQ - 1)
                        for p in pending:
                            take(*p)
                        if (s, u) == (MAXIMA_AT[0], MAXIMA_AT[1] + 1) and kind != "last":
                            with general(dve):
                                maxima(b + 1)
                        pending = [(name, turn(b, kind, name), b, pb) for name in jobs_at(kind, s, u) if name != "codes"]
                        for tile in tiles[u * len(tiles) // NU:(u + 1) * len(tiles) // NU]:
                            (normalise if kind in ("first", "second") else add_back)(tile)

            each_batch(dve, body)
            take_outputs(B - 1, NQ - 1)
            take("merge", TAIL_TURN, B, 0)
            take("proj", TAIL_TURN + 1, B, 0)
            for tile in range(sum(GATHERS[0] + GATHERS[1][:-1]), NTOK):
                add_back(tile)

        @block.gpsimd
        def _(pool):
            gp = nc.gpsimd
            ones_t = one[:].to_broadcast([P, T])
            gp.memset(RK[0][:].bitcast(U32), 0).then_inc(rk_clear, 1)
            pool.wait_ge(hidden_ok, 2)
            gp.affine_select(out=hidden[:], in_=hidden[:], compare_op=ALU.is_ge, fill=-3e38, base=0, pattern=[[-1, P]],
                             channel_multiplier=1).then_inc(hidden_ok, 1)

            def mask(b, s, first):
                Sq = S[:, s % 2]
                pool.wait_ge(e_done, (b * NQ + s) * 3 + (2 if first else 3))
                pool.sem_inc(waited, 1)
                if first:
                    x = Sq[:, 0:QH, 0:P]
                    gp.affine_select(out=x, in_=x, compare_op=ALU.is_ge, fill=0.0, base=0, pattern=[[0, QH], [1, P]],
                                     channel_multiplier=-1)
                    x = Sq[:, 0:QH, T:T + 2 * P].rearrange("p c (k n) -> p c k n", k=2)
                    gp.affine_select(out=x, in_=x, compare_op=ALU.is_ge, fill=0.0, base=0, pattern=[[0, QH], [0, 2], [1, P]],
                                     channel_multiplier=-1).then_inc(m_done, 1)
                else:
                    x = Sq[:, QH].rearrange("p (j n) -> p j n", j=QH)[:, :, 0:P]
                    gp.affine_select(out=x, in_=x, compare_op=ALU.is_ge, fill=0.0, base=0, pattern=[[0, QH], [1, P]],
                                     channel_multiplier=-1).then_inc(m_done, 1)

            def split(n, bn, k):
                src, r, pt = {"q": sQ, "k": sK, "a": sA}[n][:], rest[:], {"q": partsQ, "k": partsK, "a": partsA}[n]
                start = isinstance(bn, int) and bn == 0
                link = Link(pool, split_chain, (bn * 3 + ("aqk" if start else "qka").index(n)) * 3)
                pool.wait_ge(misc_used, k + 1)
                if n == "q":
                    pool.wait_ge(stored["a"], 16 if start else bn * 16)
                    pool.wait_ge(h_stored, 32 if start else bn * 32)
                elif not start:
                    if n == "k":
                        pool.wait_ge(stored["k"], bn * 16)
                    else:
                        pool.wait_ge(stored["q"], bn * 16 + 16)
                link(gp.tensor_tensor(pt[:, 0, :], src, ones_t, ALU.mult))
                link(gp.tensor_tensor(r, src, pt[:, 0, :], ALU.subtract))
                link(gp.tensor_tensor(pt[:, 1, :], r, ones_t, ALU.mult))
                gp.tensor_tensor(pt[:, 2, :], r, pt[:, 1, :], ALU.subtract).then_inc(split_ok[n], 1)
                pool.wait_ge(split_ok[n], bn + 1)

            def scatter(tile):
                pool.wait_ge(xs_ok, tile + 1)
                gp.indirect_dma_start(out=xs_d, out_offset=bass.IndirectOffsetOnAxis(ap=posu[:, tile:tile + 1], axis=0),
                                      in_=xs[tile % NXS], in_offset=None).then_inc(xs_sent[tile % NXS], 16)

            def gather(tile):
                if tile >= NXS:
                    pool.wait_ge(sum_ok, tile - NXS + 1)
                gp.indirect_dma_start(out=xs[tile % NXS], out_offset=None, in_=ys_d,
                                      in_offset=bass.IndirectOffsetOnAxis(ap=posu[:, tile:tile + 1], axis=0)).then_inc(yg_in[tile % NXS], 16)

            def relu(k, i, n):
                pool.wait_ge(misc_used, n + 1)
                pool.sem_inc(waited, 1)
                gp.tensor_scalar(hid[i][:], hid[i][:], 0.0, None, ALU.max).then_inc(relu_ok, 1)

            for n, name in (("a", "mixed"), ("q", "q"), ("k", "k")):
                split(n, 0, PROLOGUE.index(name))
            gp.memset(RK[1][:].bitcast(U32), 0).then_inc(rk_clear, 1)

            def body(b, pb, kind):
                for s in range(NQ):
                    mask(b, s, True)
                    mask(b, s, False)
                    for at_s, n, name in ((0, "q", "q"), (0, "k", "k"), (1, "a", "mixed")):
                        if s == at_s and kind != "last":
                            split(n, b + 1, turn(b, kind, name))
                    if kind in ("first", "second"):
                        for i in range(SCATTERS[s]):
                            scatter(b * (NTOK // 2) + first_tile(SCATTERS, s) + i)
                    if kind == "ffn":
                        for at_s, i, group in RELUS:
                            if s == at_s:
                                relu((b - F_FROM) * 2 + "AB".index(group), i, turn(b, kind, f"h{i}{group}"))
                    if kind in ("plain", "last"):
                        if kind == "plain" and s == 1:
                            pool.wait_ge(y_all, 1)
                        n = (b - B + 2) * NQ + s
                        for i in range(GATHERS[b - B + 2][s]):
                            gather(first_tile(GATHERS[0] + GATHERS[1], n) + i)
                if kind == "second":
                    for i in range(NXS):
                        pool.wait_ge(xs_sent[i], (NTOK - i + NXS - 1) // NXS * 16)
                    pool.sem_inc(xs_done, 1)

            each_batch(pool, body)
            for tile in range(sum(GATHERS[0] + GATHERS[1]), NTOK):
                gather(tile)

        @block.sync
        def _(sp):
            sp.sem_inc(y_out, 1)

            def load_x(b, pb):
                src = xt_d[b] if isinstance(b, int) else xt_d[bass.ds(b, 1)].rearrange("b p n -> p (b n)")
                sp.dma_start(xTr[pb][:], src).then_inc(xt_in[pb], 16)

            def stack_q(bn, pn):
                sp.wait_ge(split_ok["q"], bn + 1)
                sp.dma_start(qp_d[pn].rearrange("t r n -> r t n"), partsQ[:]).then_inc(stored["q"], 16)
                sp.wait_ge(stored["q"], bn * 16 + 16)
                if not (isinstance(bn, int) and bn == 0):
                    sp.wait_ge(raw_full, (bn - 1) * (NQ * NC) + 1)
                    sp.wait_ge(lin_full, (bn - 1) * (NQ * NC * 2) + 1)
                for t in range(NTERM):
                    sp.dma_start(QS[pn][t * HD:(t + 1) * HD].rearrange("d h n -> d (h n)"),
                                 qp_d[pn, QPART[t]].rearrange("(d h) n -> d (h n)", h=H)).then_inc(raw_in[pn], 16)

            def stack_k(bn, pn):
                sp.wait_ge(split_ok["k"], bn + 1)
                sp.dma_start(kp_d[pn].rearrange("t r n -> r t n"), partsK[:]).then_inc(stored["k"], 16)
                sp.wait_ge(stored["k"], bn * 16 + 16)
                for r0, k in ((0, 3), (3, 2), (5, 1)):
                    sp.dma_start(RK[pn][r0 * HD:(r0 + k) * HD].rearrange("d h n -> d (h n)"),
                                 kp_d[pn, 0:k].rearrange("t (d h) n -> (t d) (h n)", h=H)).then_inc(raw_in[pn], 16)

            def stack_a(bn, pn):
                sp.wait_ge(split_ok["a"], bn + 1)
                for kind in range(2):
                    r0 = HAM0 + (1 + kind) * NE6
                    sp.dma_start(hp_d[pn, kind].rearrange("t e n -> e t n"), partsA[r0:r0 + NE6]).then_inc(h_stored, 16)
                sp.dma_start(ap_d[pn, :, 0:HAM0 + NE6].rearrange("t r n -> r t n"), partsA[0:HAM0 + NE6]).then_inc(stored["a"], 16)
                sp.wait_ge(h_stored, bn * 32 + 32)
                for kind in range(2):
                    for r0, k in ((0, 3), (3, 2), (5, 1)):
                        row = RK_ROWS + (kind * NTERM + r0) * NE6
                        sp.dma_start(LK[pn][row:row + k * NE6, :],
                                     hp_d[pn, kind, 0:k].rearrange("t e n -> (t e) n")).then_inc(lin_in[pn], 16)
                sp.wait_ge(stored["a"], bn * 16 + 16)
                for t in range(NTERM):
                    row = RK_ROWS + t * NE6
                    sp.dma_start(QS[pn][row:row + NE6].rearrange("e h n -> e (h n)"),
                                 ap_d[pn, QPART[t], 0:HAM0].rearrange("(e h) n -> e (h n)", h=H)).then_inc(lin_in[pn], 16)
                    row = RK_ROWS + (NTERM + t) * NE6
                    sp.dma_start(QS[pn][row:row + NE6],
                                 ap_d[pn, QPART[t], HAM0:HAM0 + NE6].rearrange("e (a n) -> e a n", a=1).to_broadcast([NE6, H, T])).then_inc(lin_in[pn], 16)

            def load_experts(e):
                if e >= 2:
                    n = e - 2
                    kind, b = ("first", 0) if n < E // 2 else ("second", 1)
                    sp.wait_ge(misc_full, turn(b, kind, f"w{n % (E // 2) * 2 + 1}") + 1)
                sp.dma_start(w1[e % 2][:, 0:F].rearrange("p (c d) -> p c d", c=FC),
                             a["L0_ffn_W1"][e].rearrange("(c p) d -> p c d", p=P)).then_inc(ew_in[e % 2], 16)
                sp.dma_start(w2[e % 2][:, 0:F], a["L0_ffn_W2"][e]).then_inc(ew_in[e % 2], 16)

            def store_expert(b, kind, i):
                e = b * (E // 2) + i // 2
                sp.wait_ge(misc_used, turn(b, kind, f"w{i}") + 1)
                if i % 2 == 0:
                    sp.dma_start(w1_d[e, :, 0:F], hid[0][:].rearrange("p c n -> p (c n)")).then_inc(ew_out[0], 16)
                else:
                    sp.dma_start(w2_d[e, :, 0:F], hid[1][:].rearrange("p c n -> p (c n)")).then_inc(ew_out[1], 16)

            def expert(s):
                sp.sem_inc(waited_sp, 1)
                return sp.value_load(etile[0:1, bass.ds(s, 1)], min_val=0, max_val=E - 1)

            def load_rows(k, before):
                sp.wait_ge(misc_full, before("fx") + 1)
                sp.dma_start(xin[:], xs_d[bass.ds(k * (FG * P), FG * P), :].rearrange("(i p) d -> p i d", p=P)).then_inc(fx_in, 16)

            def load_w1(k, i, before):
                sp.wait_ge(misc_used, before(f"h{i}") + 1)
                e = expert(k * FG + i)
                sp.dma_start(w1[i][:], w1_d[bass.ds(e, 1)].rearrange("e p f -> p (e f)")).then_inc(w1_in[i], 16)

            def load_w2(k, i, before):
                sp.wait_ge(misc_used, before(f"y{i}") + 1)
                e = expert(k * FG + i)
                sp.dma_start(w2[i][:], w2_d[bass.ds(e, 1)].rearrange("e p f -> p (e f)")).then_inc(w2_in, 16)

            def store_rows(k, n):
                sp.wait_ge(misc_used, n + 1)
                sp.dma_start(ys_d[bass.ds(k * (FG * P), FG * P), :].rearrange("(i p) d -> p i d", p=P), ysb[:]).then_inc(y_out, 16)

            def shift(bn, pn):
                sp.wait_ge(px_split, bn * 4 + 4)
                sp.dma_start(mx_d[pn].rearrange("t (r n) -> r t n", n=P), mparts[:]).then_inc(px_out, 16)
                sp.wait_ge(px_out, bn * 16 + 16)
                sp.dma_start(QS[pn][SHIFT0:ROWS].rearrange("r h n -> r (h n)"), mx_d[pn]).then_inc(px_in, 16)

            load_x(0, 0)
            load_x(1, 1)
            load_experts(0)
            load_experts(1)
            stack_a(0, 0)
            stack_q(0, 0)
            sp.wait_ge(rk_clear, 1)
            stack_k(0, 0)
            sp.wait_ge(rk_clear, 2)
            with general(sp):
                shift(0, 0)

            def body(b, pb, kind):
                bn, pn = b + 1, 1 - pb
                k = (b - F_FROM) * 2 if kind == "ffn" else None
                if kind in ("first", "second"):
                    stack_q(bn, pn)
                    stack_k(bn, pn)
                    for i in range(E):
                        store_expert(b, kind, i)
                        if i % 2 == 1:
                            e = b * (E // 2) + i // 2 + 2
                            if e < E:
                                load_experts(e)
                        if i == 1:
                            stack_a(bn, pn)
                        if i == 4:
                            with general(sp):
                                shift(bn, pn)
                    if kind == "second":
                        sp.wait_ge(xs_done, 1)
                        for i in range(2):
                            sp.wait_ge(ew_out[i], E * 16)
                if kind == "ffn":
                    prior = lambda j: turn(b - 1, kind, j + "B")
                    load_rows(k, prior)
                    for i in range(FG):
                        load_w1(k, i, prior)
                    for i in range(FG):
                        load_w2(k, i, prior)
                    stack_q(bn, pn)
                    stack_k(bn, pn)
                    own = lambda j: turn(b, kind, j + "A")
                    load_rows(k + 1, own)
                    stack_a(bn, pn)
                    for i in range(FG):
                        load_w1(k + 1, i, own)
                    with general(sp):
                        shift(bn, pn)
                    for i in range(FG):
                        load_w2(k + 1, i, own)
                    store_rows(k, turn(b, kind, "y2A"))
                    store_rows(k + 1, turn(b, kind, "y2B"))
                if kind == "plain":
                    sp.wait_ge(y_out, NSLOT // FG * 16 + 1)
                    sp.sem_inc(y_all, 1)
                    stack_q(bn, pn)
                    stack_k(bn, pn)
                    stack_a(bn, pn)
                    with general(sp):
                        shift(bn, pn)
                if kind in ("first", "second", "ffn"):
                    sp.wait_ge(misc_full, turn(b, kind, "q") + 1)
                    load_x(b + 2, pb)

            each_batch(sp, body)

            def store_out(b):
                sp.wait_ge(sum_ok, (b + 1) * TT)
                if b == B - 1:
                    sp.wait_ge(misc_used, TAIL_TURN + 2)
                sp.dma_start(out[b].rearrange("(t p) d -> p t d", p=P), z[:, b * TT:(b + 1) * TT, :]).then_inc(final_out, 16)

            for b in range(B):
                store_out(b)
            sp.wait_ge(final_out, 16 * B)


_OUTS = [((16, 512, 128), 'float32')]
def kernel(**inputs):
    import numpy as _np
    import concourse.bacc as _bacc
    from concourse import mybir as _mybir
    from concourse.bass_utils import run_bass_kernel_spmd as _run
    nc = _bacc.Bacc("TRN2", target_bir_lowering=False, num_devices=1)
    arrays, args = {}, {}
    for name in inputs:
        a = _np.ascontiguousarray(inputs[name])
        arrays[f"in_{name}_dram"] = a
        args[name] = nc.dram_tensor(f"in_{name}_dram", a.shape, _mybir.dt.from_np(a.dtype), kind="ExternalInput").ap()
    out = nc.dram_tensor("out_0_dram", (16, 512, 128), _mybir.dt.float32, kind="ExternalOutput").ap()
    build(nc, args, out)
    r = _run(nc, [arrays], core_ids=[0])
    return r.results[0]["out_0_dram"]
```
